# Optimizing a Trainium2 kernel written in Bass

```python
import numpy as np
import jax
import jax.numpy as jnp

def _softmax(x, axis=-1):
    return jax.nn.softmax(x, axis=axis)

def _gelu(x):
    return jax.nn.gelu(x, approximate=True)

def _silu(x):
    return jax.nn.silu(x)

def _sigmoid(x):
    return jax.nn.sigmoid(x)

def _layernorm(x, axis=-1, eps=1e-05):
    m = jnp.mean(x, axis=axis, keepdims=True)
    v = jnp.var(x, axis=axis, keepdims=True)
    return (x - m) / jnp.sqrt(v + eps)

def _scatter_add(tgt, idx, src, axis=0):
    return tgt.at[idx].add(src)

def _segment_sum(src, seg, n):
    return jax.ops.segment_sum(src, seg, n)
kernel_name = 'mk_cond_seq_d4_seqx_r4_fde7a9'

def setup_inputs(seed: int=0):
    np.random.seed(seed)
    _w = jnp.asarray

    def _rec_inputs():
        import jax
        import jax.numpy as jnp
        _rk = jax.random.key(seed)
        x = -7.109e-05 + 0.9999 * jax.random.normal(jax.random.fold_in(_rk, 1), (64, 64, 256), jnp.float32)
        _lenS = 64 - jax.random.randint(jax.random.fold_in(_rk, 7), (64,), 0, max(1, 64 // 4) + 1, jnp.int32)
        _lenS2 = 64 - jax.random.randint(jax.random.fold_in(_rk, 8), (64,), 0, max(1, 64 // 4) + 1, jnp.int32)
        itok_B_0_2 = jax.random.randint(jax.random.fold_in(_rk, 11), (64,), 0, 3, jnp.int32)
        itok_B_0_15 = jax.random.randint(jax.random.fold_in(_rk, 12), (64,), 0, 16, jnp.int32)
        itok_B_34_63 = jax.random.randint(jax.random.fold_in(_rk, 14), (64,), 34, 64, jnp.int32)
        fside_Bx16xSxS_0 = -1.47943e-05 + 1.00017 * jax.random.normal(jax.random.fold_in(_rk, 15), (64, 16, 64, 64), jnp.float32)
        itok_B_6_14 = jax.random.randint(jax.random.fold_in(_rk, 16), (64,), 6, 15, jnp.int32)
        _validS = jnp.arange(64)[None, :] < _lenS[:, None]
        _validS2 = jnp.arange(64)[None, :] < _lenS2[:, None]
        _causal = jnp.tril(jnp.ones((64, 64), dtype=bool))
        mask_Bx1xSxS_bk0 = jnp.logical_not(jnp.broadcast_to(_validS[:, None, None, :], (64, 1, 64, 64)))
        return (x, itok_B_0_2, itok_B_0_15, itok_B_34_63, fside_Bx16xSxS_0, itok_B_6_14, mask_Bx1xSxS_bk0)
    x, itok_B_0_2, itok_B_0_15, itok_B_34_63, fside_Bx16xSxS_0, itok_B_6_14, mask_Bx1xSxS_bk0 = _rec_inputs()

    def _L0_cond_setup():
        import jax, jax.numpy as jnp
        import numpy as np
        H = 256
        EPS = 1e-05

        def _gelu(x):
            return jax.nn.gelu(x, approximate=False)
        key = jax.random.key(seed)
        ks = jax.random.split(key, 16)
        s = 1.0 / np.sqrt(H)
        inp = {'x': jax.random.normal(ks[0], (64, 256, H), dtype=jnp.float32), 'condition': jax.random.randint(ks[1], (64,), 0, 3), 'w1_nr': jax.random.normal(ks[2], (H, H), dtype=jnp.float32) * s, 'b1_nr': jnp.zeros((H,), dtype=jnp.float32), 'w2_nr': jax.random.normal(ks[3], (H, H), dtype=jnp.float32) * s, 'b2_nr': jnp.zeros((H,), dtype=jnp.float32), 'w1_tsr': jax.random.normal(ks[4], (H, H), dtype=jnp.float32) * s, 'b1_tsr': jnp.zeros((H,), dtype=jnp.float32), 'w2_tsr': jax.random.normal(ks[5], (H, H), dtype=jnp.float32) * s, 'b2_tsr': jnp.zeros((H,), dtype=jnp.float32), 'w1_sr': jax.random.normal(ks[6], (H, 2 * H), dtype=jnp.float32) * s, 'b1_sr': jnp.zeros((2 * H,), dtype=jnp.float32), 'w2_sr': jax.random.normal(ks[7], (2 * H, H), dtype=jnp.float32) * (1.0 / np.sqrt(2 * H)), 'b2_sr': jnp.zeros((H,), dtype=jnp.float32), 'w3_sr': jax.random.normal(ks[8], (H, H), dtype=jnp.float32) * s, 'b3_sr': jnp.zeros((H,), dtype=jnp.float32), 'gamma': jnp.ones((H,), dtype=jnp.float32), 'beta': jnp.zeros((H,), dtype=jnp.float32)}
        return inp
    _L0_cond_all = _L0_cond_setup()
    _L0_cond_in = {k: v for k, v in _L0_cond_all.items() if k in ('w1_nr', 'b1_nr', 'w2_nr', 'b2_nr', 'w1_tsr', 'b1_tsr', 'w2_tsr', 'b2_tsr', 'w1_sr', 'b1_sr', 'w2_sr', 'b2_sr', 'w3_sr', 'b3_sr', 'gamma', 'beta')}
    del _L0_cond_all

    def _L1_cond_setup():
        import jax, jax.numpy as jnp
        import numpy as np
        B, S, D = (32, 256, 256)
        A = 64
        E = 16
        LN_EPS = 1e-05
        key = jax.random.key(seed)
        ks = jax.random.split(key, 10)
        s = lambda fan_in: 1.0 / np.sqrt(fan_in)
        return {'hidden_states': jax.random.normal(ks[0], (B, S, D), dtype=jnp.float32), 'domain_id': jax.random.randint(ks[1], (B,), 0, E, dtype=jnp.int64), 'down_W': jax.random.uniform(ks[2], (A, D), jnp.float32, -s(D), s(D)), 'down_b': jax.random.uniform(ks[3], (A,), jnp.float32, -s(D), s(D)), 'up_W': jax.random.uniform(ks[4], (D, A), jnp.float32, -s(A), s(A)), 'up_b': jax.random.uniform(ks[5], (D,), jnp.float32, -s(A), s(A)), 'expert_W': jax.random.uniform(ks[6], (E, A, A), jnp.float32, -s(A), s(A)), 'expert_b': jax.random.uniform(ks[7], (E, A), jnp.float32, -s(A), s(A)), 'domain_emb': jax.random.normal(ks[8], (E, A), dtype=jnp.float32), 'ln_gamma': jnp.ones((D,), jnp.float32), 'ln_beta': jnp.zeros((D,), jnp.float32)}
    _L1_cond_all = _L1_cond_setup()
    _L1_cond_in = {k: v for k, v in _L1_cond_all.items() if k in ('down_W', 'down_b', 'up_W', 'up_b', 'expert_W', 'expert_b', 'domain_emb', 'ln_gamma', 'ln_beta')}
    del _L1_cond_all

    def _L2_cond_setup():
        import jax, jax.numpy as jnp
        import numpy as np
        import math
        D_MODEL = 256
        N_HEAD = 16
        HEAD_DIM = D_MODEL // N_HEAD
        D_FF = 1024
        NUM_STEPS = 100.0
        RESCALE = 4000.0
        EPS = 1e-05

        def _sin_emb(t):
            half = D_MODEL // 2
            x = t.astype(jnp.float32) / NUM_STEPS * RESCALE
            freqs = jnp.exp(jnp.arange(half, dtype=jnp.float32) * (-math.log(10000.0) / (half - 1)))
            e = x[:, None] * freqs[None, :]
            return jnp.concatenate([jnp.sin(e), jnp.cos(e)], axis=-1)

        def _ln(x):
            m = jnp.mean(x, axis=-1, keepdims=True)
            v = jnp.var(x, axis=-1, keepdims=True)
            return (x - m) / jnp.sqrt(v + EPS)

        def _gelu2(x):
            return x * jax.nn.sigmoid(1.702 * x)
        key = jax.random.key(seed)
        ks = jax.random.split(key, 24)
        B, S, D, F = (4, 128, D_MODEL, D_FF)
        std = 0.02
        inp = {'src': jax.random.normal(ks[0], (B, S, D), dtype=jnp.float32), 'src_mask': jax.random.randint(ks[1], (B, 1, S, S), 0, 2).astype(bool), 'timestep': jax.random.randint(ks[2], (B,), 0, 100, dtype=jnp.int32), 'attention_bias': jax.random.normal(ks[3], (B, N_HEAD, S, S), dtype=jnp.float32), 'W_ada': jax.random.normal(ks[4], (D, 2 * D), dtype=jnp.float32) * std, 'b_ada': jnp.zeros((2 * D,), dtype=jnp.float32), 'Wq': jax.random.normal(ks[5], (D, D), dtype=jnp.float32) * std, 'bq': jnp.zeros((D,), dtype=jnp.float32), 'Wk': jax.random.normal(ks[6], (D, D), dtype=jnp.float32) * std, 'bk': jnp.zeros((D,), dtype=jnp.float32), 'Wv': jax.random.normal(ks[7], (D, D), dtype=jnp.float32) * std, 'bv': jnp.zeros((D,), dtype=jnp.float32), 'Wo': jax.random.normal(ks[8], (D, D), dtype=jnp.float32) * std, 'bo': jnp.zeros((D,), dtype=jnp.float32), 'W1': jax.random.normal(ks[9], (D, F), dtype=jnp.float32) * std, 'b1': jnp.zeros((F,), dtype=jnp.float32), 'W2': jax.random.normal(ks[10], (F, D), dtype=jnp.float32) * std, 'b2': jnp.zeros((D,), dtype=jnp.float32), 'g2': jnp.ones((D,), dtype=jnp.float32), 'beta2': jnp.zeros((D,), dtype=jnp.float32)}
        return inp
    _L2_cond_all = _L2_cond_setup()
    _L2_cond_in = {k: v for k, v in _L2_cond_all.items() if k in ('W_ada', 'b_ada', 'Wq', 'bq', 'Wk', 'bk', 'Wv', 'bv', 'Wo', 'bo', 'W1', 'b1', 'W2', 'b2', 'g2', 'beta2')}
    del _L2_cond_all

    def _L3_cond_setup():
        import jax, jax.numpy as jnp
        import numpy as np
        D = 256
        E = 8
        FF = 1024
        TOPK = 2
        S = 32
        SE = 64
        SH = 128
        B, T = (2, 512)

        def _forward(x, subject_ids, ln_g, ln_b, subj_emb, hyp_w1, hyp_b1, hyp_w2, hyp_b2, sty_w1, sty_b1, sty_w2, sty_b2, router_w, exp_w1, exp_b1, exp_w2, exp_b2):
            mu = x.mean(-1, keepdims=True)
            var = x.var(-1, keepdims=True)
            h = (x - mu) * jax.lax.rsqrt(var + 1e-05) * ln_g + ln_b
            m_t = h.mean(1, keepdims=True)
            v_t = h.var(1, keepdims=True)
            h_norm = (h - m_t) * jax.lax.rsqrt(v_t + 1e-08)
            se = subj_emb[subject_ids]
            hyp = jax.nn.relu(se @ hyp_w1 + hyp_b1) @ hyp_w2 + hyp_b2
            sty = jax.nn.relu(hyp @ sty_w1 + sty_b1) @ sty_w2 + sty_b2
            gamma, beta = jnp.split(sty, 2, axis=-1)
            gamma = jax.nn.softplus(gamma) + 1e-08
            h = h_norm * gamma[:, None, :] + beta[:, None, :]
            h_flat = h.reshape(-1, D)
            probs = jax.nn.softmax(h_flat @ router_w, axis=-1)
            gates, idx = jax.lax.top_k(probs, TOPK)
            gates = gates / gates.sum(-1, keepdims=True)
            N = h_flat.shape[0]
            combine = jnp.zeros((N, E), h_flat.dtype).at[jnp.arange(N)[:, None], idx].add(gates)
            hid = jax.nn.relu(jnp.einsum('nd,edf->nef', h_flat, exp_w1) + exp_b1)
            eout = jnp.einsum('nef,efd->ned', hid, exp_w2) + exp_b2
            y = jnp.einsum('ned,ne->nd', eout, combine)
            return x + y.reshape(x.shape)
        key = jax.random.key(seed)
        ks = jax.random.split(key, 16)
        n = lambda k, sh, s=0.02: jax.random.normal(k, sh, dtype=jnp.float32) * s
        return {'x': jax.random.normal(ks[0], (B, T, D), dtype=jnp.float32), 'subject_ids': jax.random.randint(ks[1], (B,), 0, S), 'ln_g': jnp.ones((D,), jnp.float32), 'ln_b': jnp.zeros((D,), jnp.float32), 'subj_emb': n(ks[2], (S, SE)), 'hyp_w1': n(ks[3], (SE, SH), 1.0 / np.sqrt(SE)), 'hyp_b1': jnp.zeros((SH,), jnp.float32), 'hyp_w2': n(ks[4], (SH, SH), 1.0 / np.sqrt(SH)), 'hyp_b2': jnp.zeros((SH,), jnp.float32), 'sty_w1': n(ks[5], (SH, SH // 2), 1.0 / np.sqrt(SH)), 'sty_b1': jnp.zeros((SH // 2,), jnp.float32), 'sty_w2': n(ks[6], (SH // 2, 2 * D), 1.0 / np.sqrt(SH // 2)), 'sty_b2': jnp.zeros((2 * D,), jnp.float32), 'router_w': n(ks[7], (D, E), 1.0 / np.sqrt(D)), 'exp_w1': n(ks[8], (E, D, FF), 1.0 / np.sqrt(D)), 'exp_b1': jnp.zeros((E, FF), jnp.float32), 'exp_w2': n(ks[9], (E, FF, D), 1.0 / np.sqrt(FF)), 'exp_b2': jnp.zeros((E, D), jnp.float32)}
    _L3_cond_all = _L3_cond_setup()
    _L3_cond_in = {k: v for k, v in _L3_cond_all.items() if k in ('ln_g', 'ln_b', 'subj_emb', 'hyp_w1', 'hyp_b1', 'hyp_w2', 'hyp_b2', 'sty_w1', 'sty_b1', 'sty_w2', 'sty_b2', 'router_w', 'exp_w1', 'exp_b1', 'exp_w2', 'exp_b2')}
    del _L3_cond_all
    return {'x': x, 'itok_B_0_2': itok_B_0_2, 'itok_B_0_15': itok_B_0_15, 'itok_B_34_63': itok_B_34_63, 'fside_Bx16xSxS_0': fside_Bx16xSxS_0, 'itok_B_6_14': itok_B_6_14, 'mask_Bx1xSxS_bk0': mask_Bx1xSxS_bk0, 'L0_cond_w1_nr': _L0_cond_in['w1_nr'], 'L0_cond_b1_nr': _L0_cond_in['b1_nr'], 'L0_cond_w2_nr': _L0_cond_in['w2_nr'], 'L0_cond_b2_nr': _L0_cond_in['b2_nr'], 'L0_cond_w1_tsr': _L0_cond_in['w1_tsr'], 'L0_cond_b1_tsr': _L0_cond_in['b1_tsr'], 'L0_cond_w2_tsr': _L0_cond_in['w2_tsr'], 'L0_cond_b2_tsr': _L0_cond_in['b2_tsr'], 'L0_cond_w1_sr': _L0_cond_in['w1_sr'], 'L0_cond_b1_sr': _L0_cond_in['b1_sr'], 'L0_cond_w2_sr': _L0_cond_in['w2_sr'], 'L0_cond_b2_sr': _L0_cond_in['b2_sr'], 'L0_cond_w3_sr': _L0_cond_in['w3_sr'], 'L0_cond_b3_sr': _L0_cond_in['b3_sr'], 'L0_cond_gamma': _L0_cond_in['gamma'], 'L0_cond_beta': _L0_cond_in['beta'], 'L1_cond_down_W': _L1_cond_in['down_W'], 'L1_cond_down_b': _L1_cond_in['down_b'], 'L1_cond_up_W': _L1_cond_in['up_W'], 'L1_cond_up_b': _L1_cond_in['up_b'], 'L1_cond_expert_W': _L1_cond_in['expert_W'], 'L1_cond_expert_b': _L1_cond_in['expert_b'], 'L1_cond_domain_emb': _L1_cond_in['domain_emb'], 'L1_cond_ln_gamma': _L1_cond_in['ln_gamma'], 'L1_cond_ln_beta': _L1_cond_in['ln_beta'], 'L2_cond_W_ada': _L2_cond_in['W_ada'], 'L2_cond_b_ada': _L2_cond_in['b_ada'], 'L2_cond_Wq': _L2_cond_in['Wq'], 'L2_cond_bq': _L2_cond_in['bq'], 'L2_cond_Wk': _L2_cond_in['Wk'], 'L2_cond_bk': _L2_cond_in['bk'], 'L2_cond_Wv': _L2_cond_in['Wv'], 'L2_cond_bv': _L2_cond_in['bv'], 'L2_cond_Wo': _L2_cond_in['Wo'], 'L2_cond_bo': _L2_cond_in['bo'], 'L2_cond_W1': _L2_cond_in['W1'], 'L2_cond_b1': _L2_cond_in['b1'], 'L2_cond_W2': _L2_cond_in['W2'], 'L2_cond_b2': _L2_cond_in['b2'], 'L2_cond_g2': _L2_cond_in['g2'], 'L2_cond_beta2': _L2_cond_in['beta2'], 'L3_cond_ln_g': _L3_cond_in['ln_g'], 'L3_cond_ln_b': _L3_cond_in['ln_b'], 'L3_cond_subj_emb': _L3_cond_in['subj_emb'], 'L3_cond_hyp_w1': _L3_cond_in['hyp_w1'], 'L3_cond_hyp_b1': _L3_cond_in['hyp_b1'], 'L3_cond_hyp_w2': _L3_cond_in['hyp_w2'], 'L3_cond_hyp_b2': _L3_cond_in['hyp_b2'], 'L3_cond_sty_w1': _L3_cond_in['sty_w1'], 'L3_cond_sty_b1': _L3_cond_in['sty_b1'], 'L3_cond_sty_w2': _L3_cond_in['sty_w2'], 'L3_cond_sty_b2': _L3_cond_in['sty_b2'], 'L3_cond_router_w': _L3_cond_in['router_w'], 'L3_cond_exp_w1': _L3_cond_in['exp_w1'], 'L3_cond_exp_b1': _L3_cond_in['exp_b1'], 'L3_cond_exp_w2': _L3_cond_in['exp_w2'], 'L3_cond_exp_b2': _L3_cond_in['exp_b2']}

def reference(x, itok_B_0_2, itok_B_0_15, itok_B_34_63, fside_Bx16xSxS_0, itok_B_6_14, mask_Bx1xSxS_bk0, L0_cond_w1_nr, L0_cond_b1_nr, L0_cond_w2_nr, L0_cond_b2_nr, L0_cond_w1_tsr, L0_cond_b1_tsr, L0_cond_w2_tsr, L0_cond_b2_tsr, L0_cond_w1_sr, L0_cond_b1_sr, L0_cond_w2_sr, L0_cond_b2_sr, L0_cond_w3_sr, L0_cond_b3_sr, L0_cond_gamma, L0_cond_beta, L1_cond_down_W, L1_cond_down_b, L1_cond_up_W, L1_cond_up_b, L1_cond_expert_W, L1_cond_expert_b, L1_cond_domain_emb, L1_cond_ln_gamma, L1_cond_ln_beta, L2_cond_W_ada, L2_cond_b_ada, L2_cond_Wq, L2_cond_bq, L2_cond_Wk, L2_cond_bk, L2_cond_Wv, L2_cond_bv, L2_cond_Wo, L2_cond_bo, L2_cond_W1, L2_cond_b1, L2_cond_W2, L2_cond_b2, L2_cond_g2, L2_cond_beta2, L3_cond_ln_g, L3_cond_ln_b, L3_cond_subj_emb, L3_cond_hyp_w1, L3_cond_hyp_b1, L3_cond_hyp_w2, L3_cond_hyp_b2, L3_cond_sty_w1, L3_cond_sty_b1, L3_cond_sty_w2, L3_cond_sty_b2, L3_cond_router_w, L3_cond_exp_w1, L3_cond_exp_b1, L3_cond_exp_w2, L3_cond_exp_b2):
    import jax
    import jax.numpy as jnp

    def _L0_cond_ref(x, condition, w1_nr, b1_nr, w2_nr, b2_nr, w1_tsr, b1_tsr, w2_tsr, b2_tsr, w1_sr, b1_sr, w2_sr, b2_sr, w3_sr, b3_sr, gamma, beta):
        import jax, jax.numpy as jnp
        import numpy as np
        H = 256
        EPS = 1e-05

        def _gelu(x):
            return jax.nn.gelu(x, approximate=False)
        out_nr = _gelu(jnp.einsum('bth,hk->btk', x, w1_nr) + b1_nr)
        out_nr = jnp.einsum('bth,hk->btk', out_nr, w2_nr) + b2_nr
        out_tsr = _gelu(jnp.einsum('bth,hk->btk', x, w1_tsr) + b1_tsr)
        out_tsr = jnp.einsum('bth,hk->btk', out_tsr, w2_tsr) + b2_tsr
        h = _gelu(jnp.einsum('bth,hk->btk', x, w1_sr) + b1_sr)
        h = _gelu(jnp.einsum('bth,hk->btk', h, w2_sr) + b2_sr)
        out_sr = jnp.einsum('bth,hk->btk', h, w3_sr) + b3_sr
        c = condition[:, None, None]
        out = jnp.where(c == 0, out_nr, jnp.where(c == 1, out_tsr, jnp.where(c == 2, out_sr, jnp.zeros_like(x))))
        y = x + out
        mu = jnp.mean(y, axis=-1, keepdims=True)
        var = jnp.mean((y - mu) ** 2, axis=-1, keepdims=True)
        return (y - mu) * jax.lax.rsqrt(var + EPS) * gamma + beta

    def _L1_cond_ref(hidden_states, domain_id, down_W, down_b, up_W, up_b, expert_W, expert_b, domain_emb, ln_gamma, ln_beta):
        import jax, jax.numpy as jnp
        import numpy as np
        B, S, D = (32, 256, 256)
        A = 64
        E = 16
        LN_EPS = 1e-05
        residual = hidden_states
        hidden = jnp.einsum('bsd,ad->bsa', hidden_states, down_W) + down_b
        hidden = jax.nn.gelu(hidden, approximate=False)
        valid = (domain_id >= 0) & (domain_id < E)
        idx = jnp.clip(domain_id, 0, E - 1)
        Wsel = expert_W[idx]
        bsel = expert_b[idx]
        expert_out = jnp.einsum('bsa,boa->bso', hidden, Wsel) + bsel[:, None, :]
        domain_output = jnp.where(valid[:, None, None], expert_out, hidden)
        hidden = domain_output + domain_emb[idx][:, None, :]
        hidden = jnp.einsum('bsa,da->bsd', hidden, up_W) + up_b
        x = hidden + residual
        mu = jnp.mean(x, axis=-1, keepdims=True)
        var = jnp.mean(jnp.square(x - mu), axis=-1, keepdims=True)
        return (x - mu) * jax.lax.rsqrt(var + LN_EPS) * ln_gamma + ln_beta

    def _L2_cond_ref(src, src_mask, timestep, attention_bias, W_ada, b_ada, Wq, bq, Wk, bk, Wv, bv, Wo, bo, W1, b1, W2, b2, g2, beta2):
        import jax, jax.numpy as jnp
        import numpy as np
        import math
        D_MODEL = 256
        N_HEAD = 16
        HEAD_DIM = D_MODEL // N_HEAD
        D_FF = 1024
        NUM_STEPS = 100.0
        RESCALE = 4000.0
        EPS = 1e-05

        def _sin_emb(t):
            half = D_MODEL // 2
            x = t.astype(jnp.float32) / NUM_STEPS * RESCALE
            freqs = jnp.exp(jnp.arange(half, dtype=jnp.float32) * (-math.log(10000.0) / (half - 1)))
            e = x[:, None] * freqs[None, :]
            return jnp.concatenate([jnp.sin(e), jnp.cos(e)], axis=-1)

        def _ln(x):
            m = jnp.mean(x, axis=-1, keepdims=True)
            v = jnp.var(x, axis=-1, keepdims=True)
            return (x - m) / jnp.sqrt(v + EPS)

        def _gelu2(x):
            return x * jax.nn.sigmoid(1.702 * x)
        B, S, D = src.shape
        emb = jax.nn.silu(_sin_emb(timestep)) @ W_ada + b_ada
        scale, shift = jnp.split(emb[:, None, :], 2, axis=-1)
        x = _ln(src) * (1.0 + scale) + shift
        q = (x @ Wq + bq).reshape(B, S, N_HEAD, HEAD_DIM).transpose(0, 2, 1, 3)
        k = (x @ Wk + bk).reshape(B, S, N_HEAD, HEAD_DIM).transpose(0, 2, 1, 3)
        v = (x @ Wv + bv).reshape(B, S, N_HEAD, HEAD_DIM).transpose(0, 2, 1, 3)
        scores = jnp.einsum('bhqd,bhkd->bhqk', q / math.sqrt(HEAD_DIM), k)
        scores = scores + attention_bias
        scores = jnp.where(src_mask, -jnp.inf, scores.astype(jnp.float32))
        probs = jax.nn.softmax(scores, axis=-1).astype(v.dtype)
        ctx = jnp.einsum('bhqk,bhkd->bhqd', probs, v)
        ctx = ctx.transpose(0, 2, 1, 3).reshape(B, S, D)
        x = x + (ctx @ Wo + bo)
        h = _ln(x) * g2 + beta2
        ff = _gelu2(h @ W1 + b1) @ W2 + b2
        return x + ff

    def _L3_cond_ref(x, subject_ids, ln_g, ln_b, subj_emb, hyp_w1, hyp_b1, hyp_w2, hyp_b2, sty_w1, sty_b1, sty_w2, sty_b2, router_w, exp_w1, exp_b1, exp_w2, exp_b2):
        import jax, jax.numpy as jnp
        import numpy as np
        D = 256
        E = 8
        FF = 1024
        TOPK = 2
        S = 32
        SE = 64
        SH = 128
        B, T = (2, 512)

        def _forward(x, subject_ids, ln_g, ln_b, subj_emb, hyp_w1, hyp_b1, hyp_w2, hyp_b2, sty_w1, sty_b1, sty_w2, sty_b2, router_w, exp_w1, exp_b1, exp_w2, exp_b2):
            mu = x.mean(-1, keepdims=True)
            var = x.var(-1, keepdims=True)
            h = (x - mu) * jax.lax.rsqrt(var + 1e-05) * ln_g + ln_b
            m_t = h.mean(1, keepdims=True)
            v_t = h.var(1, keepdims=True)
            h_norm = (h - m_t) * jax.lax.rsqrt(v_t + 1e-08)
            se = subj_emb[subject_ids]
            hyp = jax.nn.relu(se @ hyp_w1 + hyp_b1) @ hyp_w2 + hyp_b2
            sty = jax.nn.relu(hyp @ sty_w1 + sty_b1) @ sty_w2 + sty_b2
            gamma, beta = jnp.split(sty, 2, axis=-1)
            gamma = jax.nn.softplus(gamma) + 1e-08
            h = h_norm * gamma[:, None, :] + beta[:, None, :]
            h_flat = h.reshape(-1, D)
            probs = jax.nn.softmax(h_flat @ router_w, axis=-1)
            gates, idx = jax.lax.top_k(probs, TOPK)
            gates = gates / gates.sum(-1, keepdims=True)
            N = h_flat.shape[0]
            combine = jnp.zeros((N, E), h_flat.dtype).at[jnp.arange(N)[:, None], idx].add(gates)
            hid = jax.nn.relu(jnp.einsum('nd,edf->nef', h_flat, exp_w1) + exp_b1)
            eout = jnp.einsum('nef,efd->ned', hid, exp_w2) + exp_b2
            y = jnp.einsum('ned,ne->nd', eout, combine)
            return x + y.reshape(x.shape)
        return _forward(x, subject_ids, ln_g, ln_b, subj_emb, hyp_w1, hyp_b1, hyp_w2, hyp_b2, sty_w1, sty_b1, sty_w2, sty_b2, router_w, exp_w1, exp_b1, exp_w2, exp_b2)
    x = _L0_cond_ref(x, itok_B_0_2, L0_cond_w1_nr, L0_cond_b1_nr, L0_cond_w2_nr, L0_cond_b2_nr, L0_cond_w1_tsr, L0_cond_b1_tsr, L0_cond_w2_tsr, L0_cond_b2_tsr, L0_cond_w1_sr, L0_cond_b1_sr, L0_cond_w2_sr, L0_cond_b2_sr, L0_cond_w3_sr, L0_cond_b3_sr, L0_cond_gamma, L0_cond_beta)
    x = _L1_cond_ref(x, itok_B_0_15, L1_cond_down_W, L1_cond_down_b, L1_cond_up_W, L1_cond_up_b, L1_cond_expert_W, L1_cond_expert_b, L1_cond_domain_emb, L1_cond_ln_gamma, L1_cond_ln_beta)
    x = _L2_cond_ref(x, mask_Bx1xSxS_bk0, itok_B_34_63, fside_Bx16xSxS_0, L2_cond_W_ada, L2_cond_b_ada, L2_cond_Wq, L2_cond_bq, L2_cond_Wk, L2_cond_bk, L2_cond_Wv, L2_cond_bv, L2_cond_Wo, L2_cond_bo, L2_cond_W1, L2_cond_b1, L2_cond_W2, L2_cond_b2, L2_cond_g2, L2_cond_beta2)
    x = _L3_cond_ref(x, itok_B_6_14, L3_cond_ln_g, L3_cond_ln_b, L3_cond_subj_emb, L3_cond_hyp_w1, L3_cond_hyp_b1, L3_cond_hyp_w2, L3_cond_hyp_b2, L3_cond_sty_w1, L3_cond_sty_b1, L3_cond_sty_w2, L3_cond_sty_b2, L3_cond_router_w, L3_cond_exp_w1, L3_cond_exp_b1, L3_cond_exp_w2, L3_cond_exp_b2)
    return x

_drawn_inputs = setup_inputs


def setup_inputs(seed=0):
    import zlib

    import numpy as np

    out = dict(_drawn_inputs(seed))
    spreads = {'L0_cond_b1_nr': (0.0, 0.1),
     'L0_cond_b2_nr': (0.0, 0.1),
     'L0_cond_b1_tsr': (0.0, 0.1),
     'L0_cond_b2_tsr': (0.0, 0.1),
     'L0_cond_b1_sr': (0.0, 0.282),
     'L0_cond_b2_sr': (0.0, 0.1),
     'L0_cond_b3_sr': (0.0, 0.1),
     'L0_cond_gamma': (1.0, 0.2),
     'L0_cond_beta': (0.0, 0.1),
     'L1_cond_ln_gamma': (1.0, 0.2),
     'L1_cond_ln_beta': (0.0, 0.1),
     'L2_cond_b_ada': (0.0, 0.1),
     'L2_cond_bq': (0.0, 0.8),
     'L2_cond_bk': (0.0, 2.0),
     'L2_cond_bv': (0.0, 0.1),
     'L2_cond_bo': (0.0, 0.1),
     'L2_cond_b1': (0.0, 0.1),
     'L2_cond_b2': (0.0, 0.1),
     'L2_cond_g2': (1.0, 0.2),
     'L2_cond_beta2': (0.0, 0.329),
     'L3_cond_ln_g': (1.0, 0.6),
     'L3_cond_ln_b': (0.0, 2.0),
     'L3_cond_hyp_b1': (0.0, 0.1),
     'L3_cond_hyp_b2': (0.0, 0.1),
     'L3_cond_sty_b1': (0.0, 0.1),
     'L3_cond_sty_b2': (0.0, 0.1),
     'L3_cond_exp_b1': (0.0, 0.1),
     'L3_cond_exp_b2': (0.0, 0.1)}
    factors = {'L1_cond_down_b': 2.819, 'L2_cond_Wq': 4.331, 'L2_cond_Wk': 3.941}
    for name, (base, spread) in spreads.items():
        noise = np.random.default_rng([zlib.crc32(name.encode()), seed]).standard_normal(out[name].shape)
        drawn = base * np.exp(spread * noise) if base else spread * noise
        out[name] = jnp.asarray(drawn.astype(out[name].dtype))
    for name, factor in factors.items():
        out[name] = (out[name] * factor).astype(out[name].dtype)
    return out
```

```python
import concourse.bass as bass
from concourse import mybir
from contextlib import ExitStack

F32 = mybir.dt.float32
BF16 = mybir.dt.bfloat16
I32 = mybir.dt.int32
U32 = mybir.dt.uint32
U8 = mybir.dt.uint8
ALU = mybir.AluOpType
ACT = mybir.ActivationFunctionType
AX = mybir.AxisListType

B, S, D = 64, 64, 256
P = 128
DC = D // P
GB = 8
GT = GB * S
NG = B // GB
TT = GT // P
NT = B * S // P
H, HD = 16, 16
FF = 1024
FC = FF // P
A1 = 64
ND = 16
NE, TOPK = 8, 2
NSUB, SE, SH = 32, 64, 128
CAP = B * S + P
MT = TOPK * B * S // P + NE - 1
MTP = MT + 1
EPS, EPS_T = 1e-5, 1e-8
NEG = -1e30
MAGIC = 12582912.0
INV2PI, PI = 0.15915494309189535, 3.141592653589793
C1, C2, C3 = 6.28125, 0.0019350051879882812, 3.0199159819e-07

A_UNITS = ([(f"xT{c}", "dve", (c,)) for c in range(2)]
           + [(n, "act", ((2 + k) % 4,)) for k, n in enumerate(["nr0", "nr1", "ts0", "ts1", "sr0", "sr1", "sr2", "sr3"])]
           + [("su0", "act", (2,)), ("su1", "act", (3,)), ("y0", "dve", (0,)), ("y1", "dve", (1,)),
              ("r00", "dve", (2,)), ("r01", "dve", (3,)), ("x10", "act", (0,)), ("x11", "act", (1,)),
              ("dn", "act", (2,)), ("ex", "dve", (3,)), ("u0", "dve", (0,)), ("u1", "dve", (1,)),
              ("r10", "dve", (2,)), ("r11", "dve", (3,)), ("x20", "dve", (0,)), ("x21", "dve", (1,)),
              ("q0", "act", (2,)), ("q1", "act", (3,)), ("k0", "dve", (0,)), ("k1", "dve", (1,)),
              ("v0", "dve", (2,)), ("v1", "dve", (3,)), ("v2", "dve", (0,)), ("v3", "dve", (1,))])
B_TAIL = ([("lg", "dve", (2,)), ("hr0", "act", (3,)), ("hr1", "act", (0,)), ("rk", "dve", (1,)),
           ("ct", "dve", (2,)), ("b20", "dve", (3,)), ("b21", "dve", (0,))])
B_UNITS = ([("sc0", "dve", (0, 1, 2, 3))] + B_TAIL[:4]
           + [(f"pt0{k}", "act" if k % 2 else "dve", (k,)) for k in range(4)] + [("cx0", "act", (0,))]
           + [("sc1", "dve", (0, 1, 2, 3))] + B_TAIL[4:]
           + [(f"pt1{k}", "act" if k % 2 else "dve", (k,)) for k in range(4)] + [("cx1", "act", (0,))]
           + [("o0", "dve", (1,)), ("o1", "dve", (2,)), ("r20", "dve", (3,)), ("r21", "dve", (0,)),
              ("h30", "act", (1,)), ("h31", "act", (2,))]
           + [(f"f{c}", "act", (c % 4,)) for c in range(FC)]
           + [("g0", "dve", (0,)), ("g1", "dve", (1,)), ("r30", "dve", (2,)), ("r31", "dve", (3,)),
              ("h40", "act", (0,)), ("h41", "act", (1,))])

ORDER = ["B.s0", "A.xT", "C.lg", "A.hid0", "B.m0", "A.hid1", "C.rk", "B.p0", "B.s1", "C.ct", "A.sr2", "B.m1", "A.out",
         "A.r0", "B.p1", "B.o", "A.x1", "B.r2", "A.dn", "A.ex", "B.h3", "B.f1a", "A.up", "B.f1b", "A.r1", "B.f1c",
         "B.f1d", "B.f2a", "A.x2", "B.f2b", "B.r3", "A.q", "A.k", "B.h4", "A.v0", "A.v1"]


class Units:

    def __init__(self, units, banks, filled, read_by, late=(), end=NG):
        self.units, self.banks, self.filled_sem, self.read_by = units, banks, filled, read_by
        self.late, self.end = {n for n, _, _ in late}, end
        self.at = {n: k for k, (n, _, _) in enumerate(units)}

    def present(self, i, name):
        if isinstance(i, int) and i in (0, self.end):
            return (name in self.late) == (i == self.end)
        return True

    def count(self, i, names, name):
        here = len([n for n in names[:names.index(name) + 1] if self.present(i, n)])
        if isinstance(i, int) and i == 0:
            return here
        return i * len(names) + (here - len([n for n in names if n in self.late]))

    def filled(self, i, name):
        return self.filled_sem, self.count(i, [n for n, _, _ in self.units], name)

    def read(self, i, name):
        who = self.units[self.at[name]][1]
        return self.read_by[who], self.count(i, [n for n, w, _ in self.units if w == who], name)

    def wait_free(self, pe, i, name):
        k, last = self.at[name], {}
        for bank in self.units[k][2]:
            here = [j for j, u in enumerate(self.units[:k]) if bank in u[2] and self.present(i, u[0])]
            if here:
                before = (1, here[-1])
            elif isinstance(i, int) and i == 0:
                continue
            else:
                before = (0, max(j for j, u in enumerate(self.units) if bank in u[2] and self.present(i - 1, u[0])))
            who = self.units[before[1]][1]
            last[who] = max(last.get(who, before), before)
        for same, j in last.values():
            pe.wait_ge(*self.read(i if same else i - 1, self.units[j][0]))

    def bank(self, name):
        return self.banks[:, self.units[self.at[name]][2][0], :]

    def fill(self, ins):
        ins.then_inc(self.filled_sem, 1)

    def done(self, ins, name):
        ins.then_inc(self.read_by[self.units[self.at[name]][1]], 1)


VECS = [("L0_cond_b1_nr", 2), ("L0_cond_b2_nr", 2), ("L0_cond_b1_tsr", 2), ("L0_cond_b2_tsr", 2),
        ("L0_cond_b1_sr", 4), ("L0_cond_b2_sr", 2), ("L0_cond_b3_sr", 2), ("L0_cond_gamma", 2),
        ("L0_cond_beta", 2), ("L1_cond_up_b", 2), ("L2_cond_b_ada", 4), ("L2_cond_bq", 2), ("L2_cond_bk", 2),
        ("L2_cond_bo", 2), ("L2_cond_b1", 8), ("L2_cond_b2", 2), ("L2_cond_g2", 2), ("L2_cond_beta2", 2),
        ("L3_cond_ln_g", 2), ("L3_cond_ln_b", 2), ("L3_cond_hyp_b1", 1), ("L3_cond_hyp_b2", 1),
        ("L3_cond_sty_b2", 4), ("freqs", 1)]
HALVES = ["L1_cond_down_b", "L3_cond_sty_b1"]
ROW, NROWS = {}, 0
for _name, _n in VECS:
    ROW[_name] = NROWS
    NROWS += _n
for _name in HALVES:
    ROW[_name] = NROWS
    NROWS += 1


def part(i, n, at=0, size=None):
    size = n if size is None else size
    if isinstance(i, int):
        return slice(i * n + at, i * n + at + size)
    return bass.ds(i * n + at, size)


def wait_apart(engine, semaphore, value):
    if not isinstance(value, int):
        value = engine.to_reg(value)
        engine.wait_ge(semaphore, 1)
    engine.wait_ge(semaphore, value)


def build(nc, t):
    ctx = ExitStack()
    with ctx:
        def sb(name, shape, dt=F32):
            return ctx.enter_context(nc.sbuf_tensor(name, shape, dt))

        sems = {}

        def sem(name):
            if name not in sems:
                sems[name] = ctx.enter_context(nc.semaphore(name))
            return sems[name]

        def dram(name):
            return nc.dram_tensor(name, DRAMS[name], F32, kind="Internal").ap()

        DRAMS = {"rows_in": [NE * CAP, D], "rows_out": [MT * P, D]}
        rows_in = dram("rows_in")
        rows_out = dram("rows_out")

        ident = sb("ident", [P, P])
        upper = sb("upper", [P, P], BF16)
        ones = sb("ones", [P, P], BF16)
        head_half = sb("head_half", [P, 2])
        pidx = sb("pidx", [P, 1])
        pidx_i = sb("pidx_i", [P, 2], I32)
        iot = sb("iot", [P, 2, MTP])
        eoff = sb("eoff", [P, NE])
        mhalf = sb("mhalf", [P, DC * GB])
        colv = sb("colv", [P, NROWS])
        bq4 = sb("bq4", [P, DC])
        eb1 = sb("eb1", [P, NE * FC])
        wl0 = sb("wl0", [P, 18 * D])
        w0 = lambda a, k, n: wl0[:, a * D:a * D + k * n].rearrange("p (k n) -> p k n", k=k)
        w1nr, w2nr, w1ts, w2ts = w0(0, 2, D), w0(2, 2, D), w0(4, 2, D), w0(6, 2, D)
        w1sr, w2sr, w3sr = w0(8, 2, 2 * D), w0(12, 4, D), w0(16, 2, D)
        w1slot = [wl0[:, k * 2048:(k + 1) * 2048].rearrange("p (k n) -> p k n", k=2) for k in range(2)]
        downT = sb("downT", [P, DC, A1])
        upT = sb("upT", [A1, D])
        expT = sb("expT", [A1, ND + 1, A1])
        wsel = sb("wsel", [A1, GB, A1])
        wat = sb("wat", [P, 4 * DC * D])
        wq, wk, wv, wo = (wat[:, k * 512:(k + 1) * 512].rearrange("p (k n) -> p k n", k=2) for k in range(4))
        hid = wat[:, :].rearrange("p (a c n) -> p a c n", a=2, c=FC)
        wff = sb("wff", [P, 16 * D])
        wf1 = wff[:, 0:8 * D].rearrange("p (k n) -> p k n", k=2)
        wf2 = wff[:, 8 * D:16 * D].rearrange("p (k n) -> p k n", k=FC)
        xs = wff[:, 0:2 * D].rearrange("p (a n) -> p a n", a=2)
        xsT = wff[:, 2 * D:4 * D].rearrange("p (a n) -> p a n", a=2)
        ys = wff[:, 4 * D:6 * D].rearrange("p (a n) -> p a n", a=2)
        got = wff[:, 8 * D:16 * D].rearrange("p (t k n) -> p t k n", t=4, k=2)
        fin = wat[:, 0:4 * D].rearrange("p (t n) -> p t n", t=4)
        part1 = wat[:, 4 * D:8 * D].rearrange("p (t n) -> p t n", t=4)
        wrt = sb("wrt", [P, DC, NE])
        b2e = sb("b2e", [NE, D])
        g1row, be1row, bvrow = (sb(n, [P, D]) for n in ("g1row", "be1row", "bvrow"))
        mneg = sb("mneg", [P, B // 2, S], BF16)
        ints = sb("ints", [P, 4, B], I32)
        idf = sb("idf", [P, 4, B])
        mcond = sb("mcond", [P, 3, B])
        bsel0 = sb("bsel0", [P, DC, B])
        bsel1 = sb("bsel1", [A1, B])
        widx = sb("widx", [1, B], I32)
        ada = sb("ada", [P, 4, B])
        sty = sb("sty", [P, 4, B])
        xres = sb("xres", [P, NT, D])
        slot = sb("slot", [P, NT, TOPK])
        slot2 = sb("slot2", [P, NT * TOPK])
        slot_u = sb("slot_u", [P, NT, TOPK], U32)
        gate = sb("gate", [P, NT, TOPK])
        base = sb("base", [P, NE])

        early = sb("early", [P, NE * FC * D])
        w2all = early[:, :].rearrange("p (e n) -> p e n", n=D)

        def cut(k, n, shape, whole=early, parts=P):
            v = whole[0:parts, k * 512:k * 512 + n]
            names = "abcd"[:len(shape)]
            if len(shape) == 1:
                return v
            return v.rearrange(f"p ({' '.join(names)}) -> p {' '.join(names)}", **dict(zip(names, shape)))

        xin = cut(0, 1024, [TT, D])
        xb = cut(0, 1024, [DC, GT])
        xT = cut(2, 1024, [DC, GT])
        hn, ht = cut(4, 1024, [DC, GT]), cut(6, 1024, [DC, GT])
        hs, hs2 = cut(8, 2048, [4, GT]), cut(12, 1024, [DC, GT])
        nrow = cut(4, 1024, [TT, D])
        x1T, x2row = cut(8, 1024, [DC, GT]), cut(10, 1024, [TT, D])
        hd, he = cut(12, 512, [GT], parts=A1), cut(13, 512, [GT], parts=A1)
        qT = cut(14, 1024, [DC, GT])
        kbd = cut(16, 2048, [DC, GB, 2, S])
        vbd = cut(20, 2048, [GB, H // 2, 2 * HD])
        bias = cut(24, 4096, [2, 2, H, S])
        xmT = sb("xmT", [P, DC, GT])
        sc = sb("sc", [P, 2, H, S])
        late = sb("late", [P, 8 * 512])
        pT = sb("pT", [P, 4, GT])
        x3T = pT[:, 2:4, :]
        h3T = pT[:, 0:2, :]
        fT = late[:, 0:4096].rearrange("p (a b) -> p a b", a=FC)
        ctxT = cut(0, 1024, [DC, GT], late)
        n3row = cut(2, 1024, [TT, D], late)
        n4row = cut(0, 1024, [TT, D], late)
        h4T = cut(2, 1024, [DC, GT], late)
        hfT = cut(4, 1024, [DC, GT], late)
        hrow = sb("hrow", [P, TT, D])
        smx, ssum, rsum = (sb(n, [P, 2, H]) for n in ("smx", "ssum", "rsum"))
        st = {k: sb(f"st_{k}", [P, TT, 6]) for k in "AB"}
        mv = {k: sb(f"mv_{k}", [P, TT, 2]) for k in "AB"}
        ve = {k: sb(f"ve_{k}", [P, TT]) for k in "AB"}
        rs = {k: sb(f"rs_{k}", [P, TT]) for k in "AB"}
        st4 = sb("st4", [P, DC, GB, 6])
        tst = {n: sb(f"t_{n}", [P, DC, GB]) for n in ("sum", "dif", "sq", "var", "rstd", "mul", "mm", "add")}
        lgs = sb("lgs", [P, TT, NE])
        mx8 = sb("mx8", [P, TT, NE])
        mi8 = sb("mi8", [P, TT, NE], U32)
        mif = sb("mif", [P, TT, TOPK])
        oh = sb("oh", [P, TOPK, TT, NE])
        picked = sb("picked", [P, TT, NE], BF16)
        gd, ge, gp = (sb(n, [P, TT]) for n in ("gd", "ge", "gp"))
        cm = sb("cm", [P, TOPK, TT, NE])
        cmix = sb("cmix", [P, TT, NE])
        pos = sb("pos", [P, TT, NE])
        posk = sb("posk", [P, TOPK, TT, NE])
        idx = sb("idx", [P, TT, TOPK], U32)
        ctT = cut(6, 512, [GT], late, NE)
        cnt = sb("cnt", [P, NE])
        plan_space = sc[:, :, :, :].rearrange("p a h k -> p (a h k)")
        plan = {n: plan_space[:, k * MTP:(k + 1) * MTP]
                for k, n in enumerate(("e", "start", "over", "src"))}
        pl8 = {n: sb(f"pl8_{n}", [P, NE]) for n in ("n", "incl", "one", "shift", "step")}
        pl1 = sb("pl1", [P, 2])
        pge = plan_space[:, 4 * MTP:(4 + NE) * MTP].rearrange("p (t e) -> p t e", e=NE)
        meta = sb("meta", [P, 2, MTP], I32)
        padp = sb("padp", [P, NE])
        padu = sb("padu", [P, NE], U32)
        b1c = sb("b1c", [P, 2, FC])
        idxc = sb("idxc", [P, 4, TOPK], U32)

        zrow = plan_space[:, 900:900 + D]
        later = plan_space[:, 1200:1200 + NT * TOPK * NE].rearrange("p (n e) -> p n e", e=NE)

        vec = sc[:, 0, 0:2, :].rearrange("p a b -> p (a b)")
        eb1r = sc[0:NE * FC, 0, 2:4, :].rearrange("p a b -> p (a b)")
        upW = sc[:, 0, 4:6, :]
        downW = sc[0:A1, 0, 6:10, :].rearrange("p a b -> p (a b)")
        expW = sc[0:A1, 1, :, :]
        mask8 = pT[:, 2, :].bitcast(U8).rearrange("p (n k) -> p n k", k=S)
        semb = sc[0:NSUB, 0, 10, :]
        expb = sc[0:ND, 0, 11, :]
        demb = sc[0:ND, 0, 12, :]
        hw1 = pT[0:SE, 0, 0:SH]
        hw2 = pT[:, 0, SH:2 * SH]
        sw1 = pT[:, 0, 2 * SH:2 * SH + SH // 2]
        sw2 = pT[0:SH // 2, 1, :]
        wada = late[:, 0:1024].rearrange("p (k n) -> p k n", k=2)
        scr = lambda k, n=B: late[:, 1024 + 64 * k:1024 + 64 * k + n]
        sce = late[:, 3072:3072 + 512].rearrange("p (a b) -> p a b", a=8)

        PA = ctx.enter_context(nc.psum_tensor("banks_a", [P, 4, 512], F32))
        PB = ctx.enter_context(nc.psum_tensor("banks_b", [P, 4, 512], F32))
        ua = Units(A_UNITS, PA, sem("a_filled"), {"act": sem("a_read_by_act"), "dve": sem("a_read_by_dve")})
        ub = Units(B_UNITS, PB, sem("b_filled"), {"act": sem("b_read_by_act"), "dve": sem("b_read_by_dve")},
                   B_TAIL)

        col = lambda name, c=0, parts=P: colv[0:parts, ROW[name] + c:ROW[name] + c + 1]
        v_seqs = lambda n: [4 * (n % 2) + 2 * h + n // 2 for h in range(2)]
        by_seq = lambda ap: ap.rearrange("p (b s) -> p b s", s=S)

        def over_tokens(ap, n=GB):
            return ap.unsqueeze(2).broadcast_to([ap.shape[0], n, S])

        def rounds(steps, i, streams="ABC"):
            for s in ORDER:
                if s in steps and s[0] in streams:
                    k = "ABC".index(s[0])
                    steps[s](i - k if k else i)

        block = ctx.enter_context(nc.Block())
        NVEC = len(VECS) + len(HALVES)
        W_A = [("w1nr", w1nr, "L0_cond_w1_nr"), ("w1ts", w1ts, "L0_cond_w1_tsr"), ("w1sr", w1sr, "L0_cond_w1_sr"),
               ("w2sr", w2sr, "L0_cond_w2_sr"), ("w2nr", w2nr, "L0_cond_w2_nr"), ("w2ts", w2ts, "L0_cond_w2_tsr"),
               ("w3sr", w3sr, "L0_cond_w3_sr")]
        W_L2 = [(wq, "L2_cond_Wq"), (wk, "L2_cond_Wk"), (wv, "L2_cond_Wv"), (wo, "L2_cond_Wo"),
                (wf1, "L2_cond_W1"), (wf2, "L2_cond_W2")]
        kview = lambda name: t[name].rearrange("(k p) n -> p k n", p=P)

        @block.sync
        def _(sp):
            x_v = t["x"].rearrange("b s d -> (b s) d").rearrange("(n p) d -> p n d", p=P)
            mask_v = t["mask_Bx1xSxS_bk0"].rearrange("(n two) o q k -> two q (n o) k", two=2)
            bias_v = t["fside_Bx16xSxS_0"].rearrange("(g b) h q k -> b q g h k", b=GB)
            sp.dma_start(xin, x_v[:, 0:TT, :]).then_inc(sem("x_loaded"), 16)
            sp.wait_ge(sem("vec_cleared"), 1)
            for name, n in VECS + [(h, 0) for h in HALVES]:
                r = ROW[name]
                if n:
                    sp.dma_start(vec[r:r + n, :], t[name].rearrange("(c p) -> c p", p=P)).then_inc(sem("vec_loaded"), 16)
                else:
                    sp.dma_start(vec[r:r + 1, 0:A1], t[name].rearrange("(c p) -> c p", p=A1)).then_inc(sem("vec_loaded"), 16)
            for k, name in enumerate(["itok_B_0_2", "itok_B_0_15", "itok_B_34_63", "itok_B_6_14"]):
                sp.dma_start(ints[:, k, :], t[name].partition_broadcast(P)).then_inc(sem("ints_loaded"), 16)
            sp.dma_start(downW, t["L1_cond_down_W"]).then_inc(sem("l1_loaded"), 16)
            sp.dma_start(upW, t["L1_cond_up_W"].rearrange("(k p) a -> p k a", p=P)).then_inc(sem("l1_loaded"), 16)
            sp.dma_start(expW, t["L1_cond_expert_W"].rearrange("e o a -> o e a")).then_inc(sem("l1_loaded"), 16)
            sp.dma_start(expb, t["L1_cond_expert_b"]).then_inc(sem("l1_loaded"), 16)
            sp.dma_start(demb, t["L1_cond_domain_emb"]).then_inc(sem("l1_loaded"), 16)
            sp.dma_start(eb1r, t["L3_cond_exp_b1"].rearrange("e (c p) -> (e c) p", p=P)).then_inc(sem("l1_loaded"), 16)
            for row, name in ((g1row, "L1_cond_ln_gamma"), (be1row, "L1_cond_ln_beta"), (bvrow, "L2_cond_bv")):
                sp.dma_start(row[:, :], t[name].partition_broadcast(P)).then_inc(sem("rows_loaded"), 16)
            for two in range(2):
                sp.dma_start(mask8[two * S:(two + 1) * S, :, :], mask_v[two]).then_inc(sem("mask_loaded"), 16)
            sp.dma_start(wada, kview("L2_cond_W_ada")).then_inc(sem("tab_loaded"), 16)
            for dst, name in ((semb, "L3_cond_subj_emb"), (hw1, "L3_cond_hyp_w1"), (hw2, "L3_cond_hyp_w2"),
                              (sw1, "L3_cond_sty_w1"), (sw2, "L3_cond_sty_w2")):
                sp.dma_start(dst, t[name]).then_inc(sem("tab_loaded"), 16)
            for dst, name in W_L2:
                sp.dma_start(dst, kview(name)).then_inc(sem("l2_loaded"), 16)
            sp.dma_start(wrt[:, :, :], kview("L3_cond_router_w")).then_inc(sem("l3_loaded"), 16)
            sp.dma_start(b2e[:, :], t["L3_cond_exp_b2"]).then_inc(sem("l3_loaded"), 16)

            def load_bias(i, duo):
                for b in range(4):
                    sp.dma_start(bias[(b % 2) * S:(b % 2 + 1) * S, duo, b // 2, :, :],
                                 bias_v[4 * duo + b, :, part(i, 1), :, :].rearrange("q g h k -> q (g h) k"))\
                        .then_inc(sem(f"bias_loaded{duo}"), 16)

            for duo in range(2):
                load_bias(0, duo)
            with sp.Fori(1, NG) as i:
                sp.wait_ge(*ua.read(i - 1, "y1"))
                sp.dma_start(xin, x_v[:, part(i, TT), :]).then_inc(sem("x_loaded"), 16)
                for duo in range(2):
                    sp.wait_ge(sem("scored"), 2 * i + (duo - 1))
                    load_bias(i, duo)
            sp.wait_ge(*ub.read(NG - 1, "cx1"))
            sp.wait_ge(*ub.filled(NG - 1, "cx1"))
            for e in range(NE):
                sp.dma_start(w2all[:, e * FC:(e + 1) * FC, :],
                             t["L3_cond_exp_w2"][e].rearrange("(c p) n -> p c n", p=P)).then_inc(sem("w2_loaded"), 16)
            sp.wait_ge(sem("plan_ready"), 1)
            sp.wait_ge(sem("scattered"), 16 * (NG * TT * TOPK + NE))

            def load_tile(t_, k):
                e = sp.value_load(meta[0:1, 0, part(t_, 1)], min_val=0, max_val=NE - 1)
                r = sp.value_load(meta[0:1, 1, part(t_, 1)], min_val=0, max_val=(NE * CAP) - P)
                sp.dma_start(w1slot[k], t["L3_cond_exp_w1"][bass.ds(e, 1), :, :].rearrange("e (k p) n -> p (e k) n", p=P))\
                    .then_inc(sem(f"w1_loaded{k}"), 16)
                sp.dma_start(xs[:, k, :], rows_in[bass.ds(r, P), :]).then_inc(sem(f"xs_loaded{k}"), 16)

            def store_tile(t_, k):
                sp.wait_ge(sem("y_copied"), t_ + 1)
                sp.dma_start(rows_out[part(t_, P), :], ys[:, k, :]).then_inc(sem(f"y_stored{k}"), 16)

            load_tile(0, 0)
            load_tile(1, 1)
            with sp.Fori(1, (MT - 1) // 2) as j:
                for k in range(2):
                    sp.wait_ge(sem("g1_filled"), 4 * j + 2 * (k - 1))
                    load_tile(2 * j + k, k)
                    store_tile(2 * j + (k - 2), k)
            sp.wait_ge(sem("g1_filled"), 2 * (MT - 2))
            load_tile(MT - 1, 0)
            for t_ in range(MT - 3, MT):
                store_tile(t_, t_ % 2)
            out_v = t["out"].rearrange("b s d -> (b s) d").rearrange("(n p) d -> p n d", p=P)

            def store_out(g, k):
                sp.wait_ge(sem("mixed"), 4 * g + (k + 1))
                sp.dma_start(out_v[:, part(g, 4, k, 1), :], fin[:, k:k + 1, :]).then_inc(sem(f"out_stored{k}"), 16)

            with sp.Fori(0, NT // 4) as g:
                for k in range(4):
                    store_out(g, k)
            for k in range(4):
                sp.wait_ge(sem(f"out_stored{k}"), 16 * (NT // 4))

        @block.tensor
        def _(pe):
            mm = nc.tensor.matmul

            def dense(u, i, name, pairs, rows=P, cols=slice(0, GT)):
                u.wait_free(pe, i, name)
                o = u.bank(name)[0:rows, cols]
                for k, (a, b) in enumerate(pairs):
                    last = mm(o, a, b, start=(k == 0), stop=(k == len(pairs) - 1))
                u.fill(last)

            def to_rows(u, i, names, src):
                for n, name in enumerate(names):
                    u.wait_free(pe, i, name)
                    for h in range(2):
                        for c in range(DC):
                            at = (2 * n + h) * P
                            last = nc.tensor.transpose(u.bank(name)[:, h * D + c * P:h * D + (c + 1) * P],
                                                       src[:, c, at:at + P], ident[:, :])
                    u.fill(last)

            def from_rows(u, i, names, src):
                for c, name in enumerate(names):
                    u.wait_free(pe, i, name)
                    for n in range(TT):
                        last = nc.tensor.transpose(u.bank(name)[:, n * P:(n + 1) * P],
                                                   src[:, n, c * P:(c + 1) * P], ident[:, :])
                    u.fill(last)

            ck = lambda c: slice(c * P, (c + 1) * P)
            ready0 = lambda i: isinstance(i, int) and i == 0

            def a_xT(i):
                if ready0(i):
                    pe.wait_ge(sem("ident_ready"), 1)
                pe.wait_ge(sem("x_loaded"), 16 * i + 16)
                from_rows(ua, i, ["xT0", "xT1"], xin)

            def a_hid0(i):
                pe.wait_ge(*ua.read(i, "xT1"))
                if ready0(i):
                    pe.wait_ge(sem("w1nr_loaded"), 16)
                for c in range(2):
                    dense(ua, i, f"nr{c}", [(w1nr[:, k, ck(c)], xT[:, k, :]) for k in range(2)])
                if ready0(i):
                    pe.wait_ge(sem("w1ts_loaded"), 16)
                for c in range(2):
                    dense(ua, i, f"ts{c}", [(w1ts[:, k, ck(c)], xT[:, k, :]) for k in range(2)])

            def a_hid1(i):
                if ready0(i):
                    pe.wait_ge(sem("w1sr_loaded"), 16)
                for c in range(4):
                    dense(ua, i, f"sr{c}", [(w1sr[:, k, ck(c)], xT[:, k, :]) for k in range(2)])

            def a_sr2(i):
                if ready0(i):
                    pe.wait_ge(sem("w2sr_loaded"), 16)
                pe.wait_ge(*ua.read(i, "sr3"))
                for c in range(2):
                    dense(ua, i, f"su{c}", [(w2sr[:, k, ck(c)], hs[:, k, :]) for k in range(4)])

            def a_out(i):
                if ready0(i):
                    for n in ("w2nr", "w2ts", "w3sr"):
                        pe.wait_ge(sem(f"{n}_loaded"), 16)
                pe.wait_ge(sem("hidden_masked"), 2 * i + 2)
                for c in range(2):
                    dense(ua, i, f"y{c}", [(w[:, k, ck(c)], h[:, k, :]) for w, h in ((w2nr, hn), (w2ts, ht), (w3sr, hs2))
                                           for k in range(2)])

            def a_r0(i):
                pe.wait_ge(*ua.read(i, "y1"))
                to_rows(ua, i, ["r00", "r01"], xT)

            def a_x1(i):
                pe.wait_ge(*ua.read(i, "r01"))
                from_rows(ua, i, ["x10", "x11"], nrow)

            def a_dn(i):
                if ready0(i):
                    pe.wait_ge(sem("setup_read"), 3)
                pe.wait_ge(*ua.read(i, "x11"))
                dense(ua, i, "dn", [(downT[:, k, :], x1T[:, k, :]) for k in range(2)], A1)

            def a_ex(i):
                pe.wait_ge(sem("wsel_ready"), i + 1)
                ua.wait_free(pe, i, "ex")
                wait_apart(pe, *ua.read(i, "dn"))
                for b in range(GB):
                    at = slice(b * S, (b + 1) * S)
                    last = mm(ua.bank("ex")[0:A1, at], wsel[:, b, :], hd[:, at], start=True, stop=True)
                ua.fill(last)

            def a_up(i):
                pe.wait_ge(*ua.read(i, "ex"))
                for c in range(2):
                    dense(ua, i, f"u{c}", [(upT[:, ck(c)], he[:, :])])

            def a_r1(i):
                pe.wait_ge(*ua.read(i, "u1"))
                to_rows(ua, i, ["r10", "r11"], x1T)

            def a_x2(i):
                pe.wait_ge(sem("n2_ready"), i + 1)
                from_rows(ua, i, ["x20", "x21"], nrow)

            def a_q(i):
                if ready0(i):
                    pe.wait_ge(sem("l2_loaded"), 16 * len(W_L2))
                pe.wait_ge(sem("xm_ready"), i + 1)
                for c in range(2):
                    dense(ua, i, f"q{c}", [(wq[:, k, ck(c)], xmT[:, k, :]) for k in range(2)])

            def a_k(i):
                for c in range(2):
                    dense(ua, i, f"k{c}", [(wk[:, k, ck(c)], xmT[:, k, :]) for k in range(2)])

            def a_v(i, units):
                for n in units:
                    ua.wait_free(pe, i, f"v{n}")
                    for h, b in enumerate(v_seqs(n)):
                        o = ua.bank(f"v{n}")[:, h * D:(h + 1) * D]
                        for k in range(2):
                            if b + 1 < GB:
                                last = mm(o, xmT[:, k, b * S:(b + 2) * S], wv[:, k, :], start=(k == 0), stop=(k == 1))
                        if b + 1 == GB:
                            for j, bj in enumerate((b, 0)):
                                for k in range(2):
                                    last = mm(o[j * S:(j + 1) * S, :], xmT[:, k, bj * S:(bj + 1) * S], wv[:, k, :],
                                              start=(k == 0), stop=(k == 1))
                    ua.fill(last)

            def b_s(i, duo):
                if duo == 0:
                    pe.wait_ge(*ua.read(i, "q1"))
                    pe.wait_ge(*ua.read(i, "k1"))
                ub.wait_free(pe, i, f"sc{duo}")
                for pr in range(2):
                    for b in range(2):
                        g = 4 * duo + 2 * pr + b
                        for c in range(DC):
                            for r in range(4):
                                rows = slice(32 * r, 32 * r + 32)
                                last = mm(PB[b * S:(b + 1) * S, r, pr * D + c * P:pr * D + (c + 1) * P],
                                          qT[rows, c, g * S:(g + 1) * S],
                                          kbd[rows, c, g, :, :].rearrange("p j s -> p (j s)"), start=True, stop=True)
                ub.fill(last)

            def b_p(i, duo):
                pe.wait_ge(sem("probs_ready"), 2 * i + (duo + 1))
                for k in range(4):
                    ub.wait_free(pe, i, f"pt{duo}{k}")
                    for m in range(4):
                        n = 4 * k + m
                        last = nc.tensor.transpose(ub.bank(f"pt{duo}{k}")[:, m * P:(m + 1) * P],
                                                   sc[:, n // 8, 2 * (n % 8):2 * (n % 8) + 2, :].rearrange("p a b -> p (a b)"),
                                                   ident[:, :])
                    ub.fill(last)
                pe.wait_ge(*ub.read(i, f"pt{duo}2"))
                pe.wait_ge(*ub.read(i, f"pt{duo}3"))
                if duo == 0:
                    pe.wait_ge(*ua.read(i, "v3"))
                ub.wait_free(pe, i, f"cx{duo}")
                for pr in range(2):
                    for b in range(2):
                        for c in range(DC):
                            for r in range(4):
                                n = 8 * pr + 4 * c + r
                                at = c * D + pr * P + b * S
                                last = mm(ub.bank(f"cx{duo}")[32 * r:32 * r + 32, at:at + S],
                                          vbd[:, 4 * duo + 2 * pr + b, 4 * c + r, :],
                                          pT[:, n // 4, (n % 4) * P + b * S:(n % 4) * P + (b + 1) * S], start=True, stop=True)
                ub.fill(last)

            def b_o(i):
                pe.wait_ge(*ub.read(i, "cx1"))
                for c in range(2):
                    dense(ub, i, f"o{c}", [(wo[:, k, ck(c)], ctxT[:, k, :]) for k in range(2)])

            def b_r2(i):
                pe.wait_ge(*ub.read(i, "o1"))
                to_rows(ub, i, ["r20", "r21"], x3T)

            def b_h3(i):
                pe.wait_ge(*ub.read(i, "r21"))
                from_rows(ub, i, ["h30", "h31"], n3row)

            def b_f1(i, chunks):
                pe.wait_ge(*ub.read(i, "h31"))
                for f in chunks:
                    dense(ub, i, f"f{f}", [(wf1[:, k, ck(f)], h3T[:, k, :]) for k in range(2)])

            def b_f2(i, c):
                pe.wait_ge(*ub.read(i, "f7"))
                dense(ub, i, f"g{c}", [(wf2[:, k, ck(c)], fT[:, k, :]) for k in range(FC)])

            def b_r3(i):
                pe.wait_ge(*ub.read(i, "g1"))
                to_rows(ub, i, ["r30", "r31"], x3T)

            def b_h4(i):
                pe.wait_ge(*ub.read(i, "r31"))
                from_rows(ub, i, ["h40", "h41"], n4row)

            def c_lg(i):
                pe.wait_ge(sem("hf_ready"), i + 1)
                ub.wait_free(pe, i + 1, "lg")
                for n in range(TT):
                    for k in range(2):
                        last = mm(ub.bank("lg")[:, n * NE:(n + 1) * NE], hfT[:, k, n * P:(n + 1) * P], wrt[:, k, :],
                                  start=(k == 0), stop=(k == 1))
                ub.fill(last)
                to_rows(ub, i + 1, ["hr0", "hr1"], hfT)

            def c_rk(i):
                pe.wait_ge(sem("picked_ready"), i + 1)
                ub.wait_free(pe, i + 1, "rk")
                for n in range(TT + 1):
                    o = ub.bank("rk")[:, n * NE:(n + 1) * NE]
                    for m in range(min(n, TT)):
                        last = mm(o, ones[:, :], picked[:, m, :], start=(m == 0), stop=(m == min(n, TT) - 1 and n == TT))
                    if n < TT:
                        last = mm(o, upper[:, :], picked[:, n, :], start=(n == 0), stop=True)
                ub.fill(last)

            def c_ct(i):
                pe.wait_ge(sem("cmix_ready"), i + 1)
                ub.wait_free(pe, i + 1, "ct")
                for n in range(TT):
                    last = nc.tensor.transpose(ub.bank("ct")[0:NE, n * P:(n + 1) * P], cmix[:, n, :], ident[:, :])
                ub.fill(last)
                pe.wait_ge(*ub.read(i + 1, "ct"))
                for k in range(2):
                    ub.wait_free(pe, i + 1, f"b2{k}")
                    for h in range(2):
                        n = 2 * k + h
                        last = mm(ub.bank(f"b2{k}")[:, h * D:(h + 1) * D], ctT[:, n * P:(n + 1) * P], b2e[:, :],
                                  start=True, stop=True)
                    ub.fill(last)

            steps = {"A.xT": a_xT, "A.hid0": a_hid0, "A.hid1": a_hid1, "A.sr2": a_sr2, "A.out": a_out, "A.r0": a_r0,
                     "A.x1": a_x1, "A.dn": a_dn, "A.ex": a_ex, "A.up": a_up, "A.r1": a_r1, "A.x2": a_x2, "A.q": a_q,
                     "A.k": a_k, "A.v0": lambda i: a_v(i, (0, 1)), "A.v1": lambda i: a_v(i, (2, 3)),
                     "B.s0": lambda i: b_s(i, 0), "B.s1": lambda i: b_s(i, 1), "B.p0": lambda i: b_p(i, 0),
                     "B.p1": lambda i: b_p(i, 1), "B.o": b_o, "B.r2": b_r2, "B.h3": b_h3,
                     **{f"B.f1{n}": (lambda i, k=k: b_f1(i, (2 * k, 2 * k + 1))) for k, n in enumerate("abcd")},
                     "B.f2a": lambda i: b_f2(i, 0), "B.f2b": lambda i: b_f2(i, 1), "B.r3": b_r3, "B.h4": b_h4, "C.lg": c_lg, "C.rk": c_rk, "C.ct": c_ct}

            def setup_cols():
                pe.wait_ge(sem("ident_ready"), 1)
                pe.wait_ge(sem("vec_loaded"), 16 * NVEC)
                nc.tensor.transpose(PB[:, 0, 0:P], vec, ident[:, :]).then_inc(sem("setup_filled"), 1)

            def setup_l1():
                pe.wait_ge(sem("l1_loaded"), 16 * 6)
                nc.tensor.transpose(PB[:, 1, 0:NE * FC], eb1r, ident[0:64, 0:64])
                for k in range(2):
                    nc.tensor.transpose(PB[:, 1, P + k * A1:P + (k + 1) * A1], downW[:, ck(k)], ident[0:64, 0:64])
                    nc.tensor.transpose(PB[0:A1, 1, (2 + k) * P:(3 + k) * P], upW[:, k, :], ident[:, :])\
                        .then_inc(sem("setup_filled"), 1)
                for e in range(ND):
                    last = nc.tensor.transpose(PB[0:A1, 2 + e // 8, (e % 8) * A1:(e % 8 + 1) * A1], expW[:, e, :],
                                               ident[0:64, 0:64])
                last.then_inc(sem("setup_filled"), 1)
                pe.wait_ge(sem("onehot_ready"), 1)
                pe.wait_ge(sem("setup_read"), 1)
                mm(PB[0:A1, 0, P:P + B], expb, sce[0:ND, 0, 0:B], start=True, stop=False)
                mm(PB[0:A1, 0, P:P + B], demb, sce[0:ND, 1, 0:B], start=False, stop=True).then_inc(sem("setup_filled"), 1)

            def setup_ada():
                pe.wait_ge(sem("tab_loaded"), 16 * 6)
                pe.wait_ge(sem("emb_ready"), 1)
                pe.wait_ge(sem("setup_read"), 4)
                for m in range(4):
                    for k in range(2):
                        last = mm(PB[:, 1, m * B:(m + 1) * B], wada[:, k, ck(m)], scr(2 + k), start=(k == 0), stop=(k == 1))
                last.then_inc(sem("setup_filled"), 1)

            def setup_sty(n):
                if n == 0:
                    mm(PB[0:SE, 2, 0:B], semb, sce[0:NSUB, 2, 0:B], start=True, stop=True).then_inc(sem("setup_filled"), 1)
                    return
                pe.wait_ge(sem("sty_step"), n)
                if n == 1:
                    last = mm(PB[:, 2, 0:B], hw1, scr(4)[0:SE, :], start=True, stop=True)
                if n == 2:
                    last = mm(PB[:, 2, 0:B], hw2, scr(5), start=True, stop=True)
                if n == 3:
                    last = mm(PB[0:SE, 2, 0:B], sw1, scr(6), start=True, stop=True)
                if n == 4:
                    for m in range(4):
                        last = mm(PB[:, 3, m * B:(m + 1) * B], sw2[:, ck(m)], scr(7)[0:SE, :], start=True, stop=True)
                last.then_inc(sem("setup_filled"), 1)

            setup = {"A.xT": setup_cols, "A.hid0": setup_l1, "A.sr2": setup_ada, "A.out": lambda: setup_sty(0),
                     "A.r0": lambda: setup_sty(1), "A.x1": lambda: setup_sty(2), "A.ex": lambda: setup_sty(3),
                     "A.up": lambda: setup_sty(4)}
            for s in ORDER:
                if s[0] == "A":
                    steps[s](0)
                    if s in setup:
                        setup[s]()
            pe.wait_ge(sem("setup_read"), 7)
            pe.wait_ge(sem("l3_loaded"), 32)
            rounds(steps, 1, "AB")
            rounds(steps, 2)
            with pe.Fori(3, NG) as i:
                rounds(steps, i)
            rounds(steps, NG, "BC")
            rounds(steps, NG + 1, "C")

            bank8 = lambda k: (PA if k < 4 else PB)[:, k % 4, :]

            def up(t_, k, first=False):
                pe.wait_ge(sem(f"xs_loaded{k}"), 8 * (t_ - k) + 16)
                if not first:
                    pe.wait_ge(sem("xsT_copied"), t_ - 1)
                for c in range(DC):
                    last = nc.tensor.transpose(bank8(k)[:, ck(c)], xs[:, k, ck(c)], ident[:, :])
                last.then_inc(sem("xsT_filled"), 1)
                pe.wait_ge(sem("xsT_copied"), t_ + 1)
                pe.wait_ge(sem(f"w1_loaded{k}"), 8 * (t_ - k) + 16)
                for h in range(2):
                    if not first:
                        pe.wait_ge(sem(f"hid_done{h}"), t_ - 1)
                    for f in range(4 * h, 4 * h + 4):
                        for c in range(DC):
                            last = mm(bank8(2 + 2 * k + h)[:, ck(f % 4)], w1slot[k][:, c, ck(f)], xsT[:, k, ck(c)],
                                      start=(c == 0), stop=(c == 1))
                    last.then_inc(sem("g1_filled"), 1)
                last = None

            def down(t_, k, first=False):
                e = pe.value_load(meta[0:1, 0, part(t_, 1)], min_val=0, max_val=NE - 1)
                if not first:
                    pe.wait_ge(sem("y_copied"), t_ - 1)
                for f in range(FC):
                    if f % 4 == 0:
                        pe.wait_ge(sem(f"hid_done{f // 4}"), t_ + 1)
                    last = mm(bank8(6 + k)[:, 0:D], hid[:, k, f, :],
                              w2all[:, bass.ds(e * FC + f, 1), :].rearrange("p a n -> p (a n)"),
                              start=(f == 0), stop=(f == FC - 1))
                last.then_inc(sem("y_filled"), 1)

            pe.wait_ge(*ub.read(NG, "b21"))
            pe.wait_ge(*ub.read(NG, "hr1"))
            pe.wait_ge(sem("plan_ready"), 1)
            pe.wait_ge(sem("w2_loaded"), 16 * NE)
            up(0, 0, True)
            up(1, 1, True)
            down(0, 0, True)
            up(2, 0)
            down(1, 1, True)
            with pe.Fori(1, (MT - 1) // 2) as j:
                for k in range(2):
                    up(2 * j + (k + 1), 1 - k)
                    down(2 * j + k, k)
            down(MT - 1, 0)

        @block.scalar
        def _(act):
            def acts(out, src, func, **kw):
                return nc.scalar.activation(out, src, func, **kw)

            for n, dst, name in W_A:
                act.dma_start(dst, kview(name)).then_inc(sem(f"{n}_loaded"), 16)

            def gelu(u, i, name, out, bias_col, func=ACT.Gelu, rows=P):
                act.wait_ge(*u.filled(i, name))
                u.done(acts(out, u.bank(name)[0:rows, :], func, bias=bias_col), name)

            def affine(u, i, name, out, g, b):
                act.wait_ge(*u.filled(i, name))
                u.done(acts(out, u.bank(name), ACT.Identity, bias=b, scale=g), name)

            def a_hid0(i):
                if isinstance(i, int):
                    act.wait_ge(sem("setup_read"), 1)
                for n, h, b in (("nr", hn, "L0_cond_b1_nr"), ("ts", ht, "L0_cond_b1_tsr")):
                    for c in range(2):
                        gelu(ua, i, f"{n}{c}", h[:, c, :], col(b, c))

            def a_hid1(i):
                for c in range(4):
                    gelu(ua, i, f"sr{c}", hs[:, c, :], col("L0_cond_b1_sr", c))

            def a_sr2(i):
                for c in range(2):
                    gelu(ua, i, f"su{c}", hs2[:, c, :], col("L0_cond_b2_sr", c))

            def a_x1(i):
                for c in range(2):
                    affine(ua, i, f"x1{c}", x1T[:, c, :], col("L0_cond_gamma", c), col("L0_cond_beta", c))

            def a_dn(i):
                gelu(ua, i, "dn", hd[:, :], col("L1_cond_down_b", parts=A1), rows=A1)

            def a_q(i):
                if isinstance(i, int):
                    act.wait_ge(sem("bq4_ready"), 1)
                for c in range(2):
                    act.wait_ge(*ua.filled(i, f"q{c}"))
                    ua.done(acts(qT[:, c, :], ua.bank(f"q{c}"), ACT.Identity, bias=bq4[:, c:c + 1], scale=HD ** -0.5), f"q{c}")

            def b_s(i, duo):
                act.wait_ge(sem("centered"), 2 * i + (duo + 1))
                acts(sc[:, :, :, :], sc[:, :, :, :], ACT.Exp).then_inc(sem("exped"), 1)

            def b_p(i, duo):
                for k in (1, 3):
                    act.wait_ge(*ub.filled(i, f"pt{duo}{k}"))
                    ub.done(acts(pT[:, k, :], ub.bank(f"pt{duo}{k}"), ACT.Copy), f"pt{duo}{k}")
                act.wait_ge(*ub.filled(i, f"cx{duo}"))
                ub.done(acts(ctxT[:, :, duo * D:(duo + 1) * D], ub.bank(f"cx{duo}").rearrange("p (c n) -> p c n", c=2),
                             ACT.Copy), f"cx{duo}")

            def b_h3(i):
                for c in range(2):
                    affine(ub, i, f"h3{c}", h3T[:, c, :], col("L2_cond_g2", c), col("L2_cond_beta2", c))

            def b_f1(i, chunks):
                for f in chunks:
                    gelu(ub, i, f"f{f}", fT[:, f, :], col("L2_cond_b1", f), ACT.Gelu_apprx_sigmoid)

            def b_h4(i):
                for c in range(2):
                    affine(ub, i, f"h4{c}", h4T[:, c, :], col("L3_cond_ln_g", c), col("L3_cond_ln_b", c))

            def c_lg(i):
                if not (isinstance(i, int) and i == 0):
                    act.wait_ge(sem("scattered"), 16 * TT * TOPK * i)
                for n in range(2):
                    act.wait_ge(*ub.filled(i + 1, f"hr{n}"))
                    ub.done(acts(hrow[:, 2 * n:2 * n + 2, :].rearrange("p a d -> p (a d)"), ub.bank(f"hr{n}"), ACT.Copy),
                            f"hr{n}")
                act.wait_ge(sem("gate_diff"), i + 1)
                acts(ge[:, :], gd[:, :], ACT.Exp).then_inc(sem("gate_exp"), 1)

            steps = {"A.hid0": a_hid0, "A.hid1": a_hid1, "A.sr2": a_sr2, "A.x1": a_x1, "A.dn": a_dn, "A.q": a_q,
                     "B.s0": lambda i: b_s(i, 0), "B.s1": lambda i: b_s(i, 1), "B.p0": lambda i: b_p(i, 0),
                     "B.p1": lambda i: b_p(i, 1), "B.h3": b_h3, 
                     **{f"B.f1{n}": (lambda i, k=k: b_f1(i, (2 * k, 2 * k + 1))) for k, n in enumerate("abcd")}, "B.h4": b_h4, "C.lg": c_lg}

            def setup_ada():
                act.wait_ge(sem("angle_ready"), 1)
                acts(scr(8, 2 * B), scr(0, 2 * B), ACT.Sin).then_inc(sem("sin_done"), 1)
                act.wait_ge(sem("sin_done"), 1)
                acts(scr(10, 2 * B), scr(8, 2 * B), ACT.Exp, scale=-1.0).then_inc(sem("silu_exp"), 1)

            def setup_sty():
                act.wait_ge(sem("abs_ready"), 1)
                acts(scr(12, 2 * B), scr(12, 2 * B), ACT.Exp, scale=-1.0).then_inc(sem("sp_exp"), 1)
                act.wait_ge(sem("sp_exp"), 1)
                acts(scr(14, 2 * B), scr(12, 2 * B), ACT.Ln, bias=1.0).then_inc(sem("sp_ln"), 1)

            setup = {"A.sr2": setup_ada, "A.v1": setup_sty}
            for s in ORDER:
                if s in steps and s[0] == "A":
                    steps[s](0)
                if s in setup:
                    setup[s]()
            rounds(steps, 1, "AB")
            rounds(steps, 2)
            with act.Fori(3, NG) as i:
                rounds(steps, i)
            rounds(steps, NG, "BC")
            rounds(steps, NG + 1, "C")

            bank8 = lambda k: (PA if k < 4 else PB)[:, k % 4, :]

            def relu(t_, k, first=False):
                act.wait_ge(sem("b1_ready"), t_ + 1)
                if not first:
                    act.wait_ge(sem("y_filled"), t_ - 1)
                for h in range(2):
                    act.wait_ge(sem("g1_filled"), 2 * t_ + (h + 1))
                    for f in range(4 * h, 4 * h + 4):
                        last = acts(hid[:, k, f, :], bank8(2 + 2 * k + h)[:, (f % 4) * P:(f % 4 + 1) * P], ACT.Relu,
                                    bias=b1c[:, k, f:f + 1])
                    last.then_inc(sem(f"hid_done{h}"), 1)

            relu(0, 0, True)
            relu(1, 1, True)
            with act.Fori(1, (MT - 1) // 2) as j:
                for k in range(2):
                    relu(2 * j + k, k)
            relu(MT - 1, 0)

        @block.vector
        def _(v):
            ts, tt, stt, cp = v.tensor_scalar, v.tensor_tensor, v.scalar_tensor_tensor, v.tensor_copy

            once = [0]

            def link(ins):
                once[0] += 1
                ins.then_inc(sem("dve_setup"), 1)
                v.wait_ge(sem("dve_setup"), once[0])

            def after(ins, name, value):
                ins.then_inc(sem(name), 1)
                wait_apart(v, sem(name), value)

            def stats(i, s, srcs, tag, eps, wait=None):
                for n in range(TT):
                    if wait:
                        wait(n)
                    last = v.bn_stats(st[s][:, n, :], srcs[n])
                after(last, f"{tag}_stats", i + 1)
                for n in range(TT):
                    last = v.bn_aggr(mv[s][:, n, :], st[s][:, n, :])
                after(last, f"{tag}_aggr", i + 1)
                ts(ve[s][:, :], mv[s][:, :, 1], eps, None, ALU.add).then_inc(sem(f"{tag}_var"), 1)

            def normalise(i, u, units, s, tag, out, eps, before=None):
                srcs = [u.bank(units[n // 2])[:, (n % 2) * D:(n % 2 + 1) * D] for n in range(TT)]

                def wait(n):
                    if n % 2 == 0:
                        v.wait_ge(*u.filled(i, units[n // 2]))
                stats(i, s, srcs, tag, eps, wait)
                if before:
                    before()
                v.wait_ge(sem(f"{tag}_rstd"), i + 1)
                for n in range(TT):
                    last = ts(out[:, n, :], srcs[n], mv[s][:, n, 0:1], rs[s][:, n:n + 1], ALU.subtract, ALU.mult)
                    if n % 2:
                        u.done(last, units[n // 2])

            def a_xT(i):
                for c in range(2):
                    v.wait_ge(*ua.filled(i, f"xT{c}"))
                    ua.done(cp(xT[:, c, :], ua.bank(f"xT{c}")), f"xT{c}")

            def a_out(i):
                v.wait_ge(sem("xb_ready"), i + 1)
                for c in range(2):
                    v.wait_ge(*ua.filled(i, f"y{c}"))
                    ua.done(tt(xT[:, c, :], ua.bank(f"y{c}"), xb[:, c, :], ALU.add), f"y{c}")

            def a_r0(i):
                normalise(i, ua, ["r00", "r01"], "A", "l0", nrow, EPS)

            def a_ex(i):
                v.wait_ge(*ua.filled(i, "ex"))
                ua.done(tt(by_seq(he[:, :]), by_seq(ua.bank("ex")[0:A1, :]), over_tokens(bsel1[:, part(i, GB)]), ALU.add), "ex")

            def a_up(i):
                for c in range(2):
                    v.wait_ge(*ua.filled(i, f"u{c}"))
                    ua.done(stt(x1T[:, c, :], ua.bank(f"u{c}"), col("L1_cond_up_b", c), x1T[:, c, :], ALU.add, ALU.add), f"u{c}")

            def a_r1(i):
                normalise(i, ua, ["r10", "r11"], "A", "l1", nrow, EPS)
                v.wait_ge(sem("x2_ready"), i + 1)
                stats(i, "A", [x2row[:, n, :] for n in range(TT)], "l2", EPS)
                v.wait_ge(sem("l2_rstd"), i + 1)
                for n in range(TT):
                    last = ts(nrow[:, n, :], x2row[:, n, :], mv["A"][:, n, 0:1], rs["A"][:, n:n + 1], ALU.subtract, ALU.mult)
                last.then_inc(sem("n2_ready"), 1)

            def a_x2(i):
                for c in range(2):
                    v.wait_ge(*ua.filled(i, f"x2{c}"))
                    ua.done(tt(by_seq(xmT[:, c, :]), by_seq(ua.bank(f"x2{c}")), over_tokens(ada[:, c, part(i, GB)]), ALU.mult), f"x2{c}")
                for c in range(2):
                    v.wait_ge(*ua.read(i, f"x2{c}"))
                    last = tt(by_seq(xmT[:, c, :]), by_seq(xmT[:, c, :]), over_tokens(ada[:, 2 + c, part(i, GB)]), ALU.add)
                last.then_inc(sem("xm_ready"), 1)

            def a_k(i):
                for c in range(2):
                    v.wait_ge(*ua.filled(i, f"k{c}"))
                    src = by_seq(ua.bank(f"k{c}"))
                    for j in range(2):
                        last = ts(kbd[:, c, :, j, :], src, col("L2_cond_bk", c), head_half[:, j:j + 1], ALU.add, ALU.mult)
                    ua.done(last, f"k{c}")

            def a_v(i, units):
                for n in units:
                    v.wait_ge(*ua.filled(i, f"v{n}"))
                    for j in range(2):
                        rows = slice(j * S, (j + 1) * S)
                        src = ua.bank(f"v{n}")[rows, :].rearrange("p (b a j d) -> p b a j d", b=2, j=2, d=HD)[:, :, :, j, :]
                        bv = bvrow[rows, :].rearrange("p (a j d) -> p a j d", j=2, d=HD)[:, :, j, :]
                        b0, b1 = (b + j for b in v_seqs(n))
                        if b1 < GB:
                            last = tt(vbd[rows, b0:b1 + 1:2, :, j * HD:(j + 1) * HD], src,
                                      bv.unsqueeze(1).broadcast_to([S, 2, H // 2, HD]), ALU.add)
                        else:
                            for h, b in enumerate((b0, 0)):
                                last = tt(vbd[rows, b, :, j * HD:(j + 1) * HD], src[:, h], bv, ALU.add)
                    ua.done(last, f"v{n}")

            def b_s(i, duo):
                v.wait_ge(sem("bias_masked"), 2 * i + (duo + 1))
                v.wait_ge(*ub.filled(i, f"sc{duo}"))
                nat = lambda a: a.rearrange("p (c r j) k -> p r c (j k)", c=2, r=4)
                for pr in range(2):
                    last = tt(nat(sc[:, pr, :, :]), PB[:, :, pr * D:(pr + 1) * D].rearrange("p r (c x) -> p r c x", c=2),
                              nat(bias[:, duo, pr, :, :]), ALU.add)
                ub.done(last, f"sc{duo}")
                v.wait_ge(*ub.read(i, f"sc{duo}"))
                v.reduce_max(smx[:, :, :], sc[:, :, :, :], axis=AX.X).then_inc(sem("scored"), 1)

            def b_m(i, duo):
                v.wait_ge(sem("exped"), 2 * i + (duo + 1))
                after(v.reduce_sum(ssum[:, :, :], sc[:, :, :, :], axis=AX.X), "summed", 2 * i + (duo + 1))
                v.reciprocal(rsum[:, :, :], ssum[:, :, :]).then_inc(sem("rsum_ready"), 1)

            def b_p(i, duo):
                for k in (0, 2):
                    v.wait_ge(*ub.filled(i, f"pt{duo}{k}"))
                    ub.done(cp(pT[:, k, :], ub.bank(f"pt{duo}{k}")), f"pt{duo}{k}")

            def b_o(i):
                for c in range(2):
                    v.wait_ge(*ub.filled(i, f"o{c}"))
                    ub.done(stt(x3T[:, c, :], ub.bank(f"o{c}"), col("L2_cond_bo", c), xmT[:, c, :], ALU.add, ALU.add), f"o{c}")

            def b_r2(i):
                normalise(i, ub, ["r20", "r21"], "B", "l3", n3row, EPS)

            def b_f2(i, c):
                v.wait_ge(*ub.filled(i, f"g{c}"))
                ub.done(stt(x3T[:, c, :], ub.bank(f"g{c}"), col("L2_cond_b2", c), x3T[:, c, :], ALU.add, ALU.add), f"g{c}")

            def b_r3(i):
                def keep():
                    for k in range(2):
                        last = cp(xres[:, part(i, TT, 2 * k, 2), :], ub.bank(f"r3{k}").rearrange("p (a d) -> p a d", a=2))
                    last.then_inc(sem("xres_ready"), 1)
                normalise(i, ub, ["r30", "r31"], "B", "l4", n4row, EPS, keep)

            def b_h4(i):
                for c in range(2):
                    v.wait_ge(*ub.read(i, f"h4{c}"))
                    for b in range(GB):
                        last = v.bn_stats(st4[:, c, b, :], h4T[:, c, b * S:(b + 1) * S])
                after(last, "t_stats", i + 1)
                f = lambda k: st4[:, :, :, k]
                tt(tst["sum"][:, :, :], f(1), f(4), ALU.add)
                tt(tst["dif"][:, :, :], f(1), f(4), ALU.subtract)
                after(tt(tst["var"][:, :, :], f(2), f(5), ALU.add), "t_halves", i + 1)
                tt(tst["sq"][:, :, :], tst["dif"][:, :, :], tst["dif"][:, :, :], ALU.mult)
                after(ts(tst["var"][:, :, :], tst["var"][:, :, :], 1.0 / S, EPS_T, ALU.mult, ALU.add), "t_within", i + 1)
                stt(tst["var"][:, :, :], tst["sq"][:, :, :], 0.25, tst["var"][:, :, :], ALU.mult, ALU.add)\
                    .then_inc(sem("t_var"), 1)
                v.wait_ge(sem("t_rstd"), i + 1)
                after(tt(tst["mul"][:, :, :], tst["rstd"][:, :, :], sty[:, 0:2, part(i, GB)], ALU.mult), "t_mul", i + 1)
                after(stt(tst["mm"][:, :, :], tst["sum"][:, :, :], 0.5, tst["mul"][:, :, :], ALU.mult, ALU.mult), "t_mm", i + 1)
                tt(tst["add"][:, :, :], sty[:, 2:4, part(i, GB)], tst["mm"][:, :, :], ALU.subtract)
                for c in range(2):
                    last = tt(by_seq(hfT[:, c, :]), by_seq(h4T[:, c, :]), over_tokens(tst["mul"][:, c, :]), ALU.mult)
                after(last, "t_scaled", i + 1)
                for c in range(2):
                    last = tt(by_seq(hfT[:, c, :]), by_seq(hfT[:, c, :]), over_tokens(tst["add"][:, c, :]), ALU.add)
                last.then_inc(sem("hf_ready"), 1)

            def c_lg(i):
                v.wait_ge(*ub.filled(i + 1, "lg"))
                ub.done(cp(lgs[:, :, :], ub.bank("lg")[:, 0:TT * NE].rearrange("p (n e) -> p n e", e=NE)), "lg")
                wait_apart(v, *ub.read(i + 1, "lg"))
                for n in range(TT):
                    last = v.max(mx8[:, n, :], lgs[:, n, :])
                after(last, "top_values", i + 1)
                for n in range(TT):
                    last = v.max_index(mi8[:, n, :], mx8[:, n, :], lgs[:, n, :])
                tt(gd[:, :], mx8[:, :, 1], mx8[:, :, 0], ALU.subtract).then_inc(sem("gate_diff"), 1)
                v.wait_ge(sem("gate_diff"), i + 1)
                after(cp(mif[:, :, :], mi8[:, :, 0:TOPK]), "top_index", i + 1)
                for k in range(TOPK):
                    last = tt(oh[:, k, :, :], iot[:, 0, 0:NE].unsqueeze(1).broadcast_to([P, TT, NE]),
                              mif[:, :, k:k + 1].broadcast_to([P, TT, NE]), ALU.is_equal)
                after(last, "onehots", i + 1)
                tt(picked[:, :, :], oh[:, 0, :, :], oh[:, 1, :, :], ALU.add).then_inc(sem("picked_ready"), 1)
                wait_apart(v, sem("gate_exp"), i + 1)
                after(ts(gp[:, :], ge[:, :], 1.0, None, ALU.add), "gate_sum", i + 1)
                g = lambda k: gate[:, part(i, TT), k]
                after(v.reciprocal(gp[:, :], gp[:, :]), "gate_recip", i + 1)
                cp(g(0), gp[:, :])
                after(tt(gd[:, :], gp[:, :], ge[:, :], ALU.mult), "gate_second", i + 1)
                cp(g(1), gd[:, :])
                for k, a in enumerate((gp, gd)):
                    last = tt(cm[:, k, :, :], oh[:, k, :, :], a[:, :].unsqueeze(2).broadcast_to([P, TT, NE]), ALU.mult)
                after(last, "gates_placed", i + 1)
                tt(cmix[:, :, :], cm[:, 0, :, :], cm[:, 1, :, :], ALU.add).then_inc(sem("cmix_ready"), 1)

            def c_rk(i):
                v.wait_ge(*ub.filled(i + 1, "rk"))
                bank = ub.bank("rk")
                last = tt(pos[:, :, :], bank[:, 0:TT * NE].rearrange("p (n e) -> p n e", e=NE),
                          base[:, :].unsqueeze(1).broadcast_to([P, TT, NE]), ALU.add)
                after(last, "ranked", i + 1)
                ub.done(tt(base[:, :], bank[:, TT * NE:(TT + 1) * NE], base[:, :], ALU.add), "rk")
                for k in range(TOPK):
                    last = tt(posk[:, k, :, :], oh[:, k, :, :], pos[:, :, :], ALU.mult)
                after(last, "rank_picked", i + 1)
                for k in range(TOPK):
                    last = v.reduce_sum(slot[:, part(i, TT), k], posk[:, k, :, :], axis=AX.X)
                after(last, "slots", i + 1)
                if not (isinstance(i, int) and i == 0):
                    wait_apart(v, sem("scattered"), 16 * TT * TOPK * i)
                cp(idx[:, :, :], slot[:, part(i, TT), :]).then_inc(sem("idx_ready"), 1)

            def c_ct(i):
                v.wait_ge(*ub.filled(i + 1, "ct"))
                ub.done(cp(ctT, ub.bank("ct")[0:NE, :]), "ct")
                v.wait_ge(sem("xres_ready"), i + 1)
                for k in range(2):
                    v.wait_ge(*ub.filled(i + 1, f"b2{k}"))
                    x = xres[:, part(i, TT, 2 * k, 2), :]
                    ub.done(tt(x, ub.bank(f"b2{k}").rearrange("p (a d) -> p a d", a=2), x, ALU.add), f"b2{k}")

            steps = {"A.xT": a_xT, "A.out": a_out, "A.r0": a_r0, "A.ex": a_ex, "A.up": a_up, "A.r1": a_r1, "A.x2": a_x2,
                     "A.k": a_k, "A.v0": lambda i: a_v(i, (0, 1)), "A.v1": lambda i: a_v(i, (2, 3)),
                     "B.s0": lambda i: b_s(i, 0), "B.s1": lambda i: b_s(i, 1), "B.m0": lambda i: b_m(i, 0),
                     "B.m1": lambda i: b_m(i, 1), "B.p0": lambda i: b_p(i, 0), "B.p1": lambda i: b_p(i, 1), "B.o": b_o,
                     "B.r2": b_r2, "B.f2a": lambda i: b_f2(i, 0), "B.f2b": lambda i: b_f2(i, 1), "B.r3": b_r3, "B.h4": b_h4, "C.lg": c_lg, "C.rk": c_rk, "C.ct": c_ct}

            v.memset(vec, 0.0).then_inc(sem("vec_cleared"), 1)
            v.memset(mhalf[:, :], -0.5).then_inc(sem("mhalf_ready"), 1)
            v.memset(ones[:, :], 1.0)
            v.memset(vbd, 0.0)
            v.wait_ge(sem("iota_ready"), 1)
            cp(pidx[:, :], pidx_i[:, 0:1])
            link(ts(pidx_i[:, 1:2], pidx_i[:, 0:1], 4, 1, ALU.logical_shift_right, ALU.bitwise_and))
            link(cp(head_half[:, 1:2], pidx_i[:, 1:2]))
            link(ts(head_half[:, 0:1], head_half[:, 1:2], -1.0, 1.0, ALU.mult, ALU.add))
            v.wait_ge(sem("ints_loaded"), 64)
            ts(eoff[:, :], iot[:, 0, 0:NE], float(CAP), None, ALU.mult)
            ts(base[:, :], iot[:, 0, 0:NE], float(CAP), None, ALU.mult)
            link(cp(idf[:, :, :], ints[:, :, :]))
            for k in range(3):
                last = ts(mcond[:, k, :], idf[:, 0, :], float(k), None, ALU.is_equal)
            last.then_inc(sem("mcond_ready"), 1)
            v.wait_ge(sem("mcond_ready"), 1)
            v.wait_ge(sem("setup_filled"), 1)
            cp(colv[:, :], PB[:, 0, 0:NROWS]).then_inc(sem("setup_read"), 1)
            v.wait_ge(sem("setup_read"), 1)
            ts(bq4[:, :], colv[:, ROW["L2_cond_bq"]:ROW["L2_cond_bq"] + 2], HD ** -0.5, None, ALU.mult).then_inc(sem("bq4_ready"), 1)
            for c in range(2):
                last = ts(bsel0[:, c, :], mcond[:, 0, :], col("L0_cond_b2_nr", c), None, ALU.mult)
            link(last)
            for k, name in ((1, "L0_cond_b2_tsr"), (2, "L0_cond_b3_sr")):
                for c in range(2):
                    last = stt(bsel0[:, c, :], mcond[:, k, :], col(name, c), bsel0[:, c, :], ALU.mult, ALU.add)
                last.then_inc(sem("bsel0_ready"), 1)
                v.wait_ge(sem("bsel0_ready"), k)

            def setup_l1():
                clip = scr(16)
                ts(clip, idf[:, 1, :], 0.0, float(ND - 1), ALU.max, ALU.min)
                link(ts(scr(17), idf[:, 3, :], 0.0, float(NSUB - 1), ALU.max, ALU.min))
                ts(sce[:, 0, 0:B], idf[:, 1, :], pidx[:, 0:1], None, ALU.is_equal)
                ts(sce[:, 1, 0:B], clip, pidx[:, 0:1], None, ALU.is_equal)
                ts(sce[:, 2, 0:B], scr(17), pidx[:, 0:1], None, ALU.is_equal).then_inc(sem("onehot_ready"), 1)
                link(tt(scr(18), clip, idf[:, 1, :], ALU.is_equal))
                link(ts(scr(19), clip, -float(ND), None, ALU.add))
                link(tt(scr(18), scr(18), scr(19), ALU.mult))
                link(ts(scr(18), scr(18), float(ND), None, ALU.add))
                cp(widx[:, :], scr(18)[0:1, :]).then_inc(sem("widx_ready"), 1)
                v.wait_ge(sem("setup_filled"), 3)
                cp(eb1[:, :], PB[:, 1, 0:NE * FC])
                cp(downT[:, :, :], PB[:, 1, P:2 * P].rearrange("p (k a) -> p k a", k=2))
                cp(upT[:, :], PB[0:A1, 1, 2 * P:4 * P]).then_inc(sem("setup_read"), 1)
                v.wait_ge(sem("setup_filled"), 4)
                cp(expT[:, 0:ND, :], PB[0:A1, 2:4, :].rearrange("p a (b c) -> p (a b) c", c=A1))
                cp(expT[:, ND, :], ident[0:A1, 0:A1]).then_inc(sem("setup_read"), 1)
                v.wait_ge(sem("setup_filled"), 5)
                cp(bsel1[:, :], PB[0:A1, 0, P:P + B]).then_inc(sem("setup_read"), 1)

            def setup_angles():
                link(ts(scr(20), idf[:, 2, :], 0.01, 4000.0, ALU.mult, ALU.mult))
                link(ts(scr(21), scr(20), col("freqs"), None, ALU.mult))
                ts(scr(22), scr(21), INV2PI, MAGIC, ALU.mult, ALU.add)
                link(ts(scr(23), scr(21), INV2PI, 0.25, ALU.mult, ALU.add))
                link(ts(scr(23), scr(23), MAGIC, None, ALU.add))
                link(ts(scr(22, 2 * B), scr(22, 2 * B), MAGIC, None, ALU.subtract))
                both = lambda k: scr(k, 2 * B).rearrange("p (a b) -> p a b", a=2)
                two = scr(21).unsqueeze(1).broadcast_to([P, 2, B])
                link(stt(both(0), both(22), -C1, two, ALU.mult, ALU.add))
                link(stt(both(0), both(22), -C2, both(0), ALU.mult, ALU.add))
                link(ts(scr(1), scr(1), PI / 2, None, ALU.add))
                link(stt(both(0), both(22), -C3, both(0), ALU.mult, ALU.add))
                ts(scr(0, 2 * B), scr(0, 2 * B), -3.1415925, 3.1415925, ALU.max, ALU.min).then_inc(sem("angle_ready"), 1)
                v.wait_ge(sem("mask_loaded"), 32)
                ts(mneg[:, :, :], mask8[:, :, :], NEG, None, ALU.mult).then_inc(sem("mneg_ready"), 1)

            def setup_ada():
                v.wait_ge(sem("silu_exp"), 1)
                link(ts(scr(10, 2 * B), scr(10, 2 * B), 1.0, None, ALU.add))
                link(v.reciprocal(scr(10, 2 * B), scr(10, 2 * B)))
                tt(scr(2, 2 * B), scr(8, 2 * B), scr(10, 2 * B), ALU.mult).then_inc(sem("emb_ready"), 1)
                v.wait_ge(sem("setup_filled"), 6)
                for m in range(4):
                    last = ts(ada[:, m, :], PB[:, 1, m * B:(m + 1) * B], col("L2_cond_b_ada", m), 1.0 if m < 2 else 0.0,
                              ALU.add, ALU.add)
                last.then_inc(sem("setup_read"), 1)

            def setup_sty(n):
                v.wait_ge(sem("setup_filled"), 7 + n)
                if n == 0:
                    last = cp(scr(4)[0:SE, :], PB[0:SE, 2, 0:B])
                if n == 1:
                    last = ts(scr(5), PB[:, 2, 0:B], col("L3_cond_hyp_b1"), 0.0, ALU.add, ALU.max)
                if n == 2:
                    last = ts(scr(6), PB[:, 2, 0:B], col("L3_cond_hyp_b2"), None, ALU.add)
                if n == 3:
                    last = ts(scr(7)[0:SE, :], PB[0:SE, 2, 0:B], col("L3_cond_sty_b1", parts=SE), 0.0, ALU.add, ALU.max)
                if n < 4:
                    last.then_inc(sem("sty_step"), 1)
                    return
                for m in range(4):
                    last = ts(sty[:, m, :], PB[:, 3, m * B:(m + 1) * B], col("L3_cond_sty_b2", m), None, ALU.add)
                last.then_inc(sem("setup_read"), 1)
                v.wait_ge(sem("setup_read"), 6)
                g = sty[:, 0:2, :].rearrange("p a b -> p (a b)")
                link(ts(scr(12, 2 * B), g, -1.0, None, ALU.mult))
                tt(scr(12, 2 * B), scr(12, 2 * B), g, ALU.max).then_inc(sem("abs_ready"), 1)
                v.wait_ge(sem("sp_ln"), 1)
                link(stt(g, g, 0.0, scr(14, 2 * B), ALU.max, ALU.add))
                ts(g, g, 1e-8, None, ALU.add).then_inc(sem("setup_read"), 1)
                v.wait_ge(sem("setup_read"), 7)

            setup = {"A.xT": setup_l1, "A.hid0": setup_angles, "A.sr2": setup_ada, "A.out": lambda: setup_sty(0),
                     "A.r0": lambda: setup_sty(1), "A.x1": lambda: setup_sty(2), "A.ex": lambda: setup_sty(3),
                     "A.v1": lambda: setup_sty(4)}
            v.wait_ge(sem("ident_ready"), 1)
            for s in ORDER:
                if s in steps and s[0] == "A":
                    if s == "A.ex" or s == "A.v0":
                        v.wait_ge(sem("rows_loaded"), 48)
                    steps[s](0)
                if s in setup:
                    setup[s]()
            rounds(steps, 1, "AB")
            rounds(steps, 2)
            with v.Fori(3, NG) as i:
                rounds(steps, i)
            rounds(steps, NG, "BC")
            rounds(steps, NG + 1, "C")

            v.wait_ge(*ub.read(NG, "rk"))
            v.memset(zrow, 0.0).then_inc(sem("zrow_ready"), 1)
            link(tt(cnt[:, :], base[:, :], eoff[:, :], ALU.subtract))
            link(ts(padp[:, :], base[:, :], pidx[:, 0:1], None, ALU.add))
            cp(padu[:, :], padp[:, :]).then_inc(sem("pads_ready"), 1)
            n8, incl = pl8["n"][:, :], pl8["incl"][:, :]
            v.memset(pl8["one"][:, :], 1.0)
            link(ts(n8, cnt[:, :], float(P - 1), 1.0 / P, ALU.add, ALU.mult))
            link(ts(n8, n8, -255.0 / 512, MAGIC, ALU.add, ALU.add))
            link(ts(n8, n8, MAGIC, None, ALU.subtract))
            link(v.tensor_tensor_scan(incl, pl8["one"][:, :], n8, 0.0, ALU.mult, ALU.add))
            tile = iot[:, 0, :]
            e, start, over, src = (plan[k] for k in ("e", "start", "over", "src"))
            seven = lambda a: a[:, 0:NE - 1].unsqueeze(1).broadcast_to([P, MTP, NE - 1])
            ge7 = pge[:, :, 0:NE - 1]
            link(tt(ge7, tile.unsqueeze(2).broadcast_to([P, MTP, NE - 1]), seven(pl8["incl"][:, :]), ALU.is_ge))
            link(v.reduce_sum(e, ge7, axis=AX.X))
            link(tt(ge7, ge7, seven(pl8["n"][:, :]), ALU.mult))
            link(v.reduce_sum(start, ge7, axis=AX.X))
            link(ts(pl1[:, 0:1], pl8["incl"][:, NE - 1:NE], -1.0, None, ALU.add))
            link(tt(pl1[:, 1:2], pl1[:, 0:1], pl8["incl"][:, NE - 2:NE - 1], ALU.max))
            link(ts(over, tile, pl1[:, 1:2], 0.0, ALU.subtract, ALU.max))
            link(tt(start, tile, start, ALU.subtract))
            link(tt(start, start, over, ALU.subtract))
            link(ts(src, e, float(CAP), None, ALU.mult))
            link(stt(src, start, float(P), src, ALU.mult, ALU.add))
            cp(meta[:, 0, :], e)
            link(cp(meta[:, 1, :], src))
            shift, step = pl8["shift"][:, :], pl8["step"][:, :]
            link(ts(shift, n8, float(P), -float(CAP), ALU.mult, ALU.add))
            cp(step[:, 1:NE], shift[:, 0:NE - 1])
            link(v.memset(step[:, 0:1], 0.0))
            slots = slot[:, :, :].rearrange("p n k -> p (n k)")
            wide = lambda a: a.unsqueeze(1).broadcast_to([P, NT * TOPK, NE])
            link(tt(later, slots.unsqueeze(2).broadcast_to([P, NT * TOPK, NE]), wide(eoff[:, :]), ALU.is_ge))
            link(tt(later, later, wide(step), ALU.mult))
            link(v.reduce_sum(slot2[:, :], later, axis=AX.X))
            link(tt(slot2[:, :], slot2[:, :], slots, ALU.add))
            cp(slot_u[:, :, :].rearrange("p n k -> p (n k)"), slot2[:, :]).then_inc(sem("plan_ready"), 1)

            bank8 = lambda k: (PA if k < 4 else PB)[:, k % 4, :]

            def turn(t_, k, first=False):
                v.wait_ge(sem("xsT_filled"), t_ + 1)
                if not first:
                    v.wait_ge(sem("g1_filled"), 2 * (t_ - 1))
                cp(xsT[:, k, :], bank8(k)[:, 0:D]).then_inc(sem("xsT_copied"), 1)

            def take(t_, k, first=False):
                v.wait_ge(sem("y_filled"), t_ + 1)
                if not first:
                    v.wait_ge(sem(f"y_stored{k}"), 8 * (t_ - k))
                cp(ys[:, k, :], bank8(6 + k)[:, 0:D]).then_inc(sem("y_copied"), 1)

            turn(0, 0, True)
            turn(1, 1, True)
            take(0, 0, True)
            turn(2, 0)
            take(1, 1, True)
            with v.Fori(1, (MT - 1) // 2) as j:
                for k in range(2):
                    turn(2 * j + (k + 1), 1 - k)
                    take(2 * j + k, k)
            take(MT - 1, 0)

            def mix(g, k):
                v.wait_ge(sem(f"gathered{k}"), 32 * g + 32)
                if not (isinstance(g, int) and g == 0):
                    v.wait_ge(sem(f"out_stored{k}"), 16 * g)
                stt(part1[:, k, :], got[:, k, 0, :], gate[:, part(g, 4, k, 1), 0:1].rearrange("p a b -> p (a b)"),
                    xres[:, part(g, 4, k, 1), :].rearrange("p a b -> p (a b)"), ALU.mult, ALU.add).then_inc(sem("mixed_first"), 1)
                v.wait_ge(sem("mixed_first"), 4 * g + (k + 1))
                stt(fin[:, k, :], got[:, k, 1, :], gate[:, part(g, 4, k, 1), 1:2].rearrange("p a b -> p (a b)"),
                    part1[:, k, :], ALU.mult, ALU.add).then_inc(sem("mixed"), 1)

            for k in range(4):
                mix(0, k)
            with v.Fori(1, NT // 4) as g:
                for k in range(4):
                    mix(g, k)

        @block.gpsimd
        def _(g):
            g.memset(ident[:, :], 0.0).then_inc(sem("pool_setup"), 1)
            g.memset(upper[:, :], 1.0).then_inc(sem("pool_setup"), 1)
            g.wait_ge(sem("pool_setup"), 2)
            g.affine_select(out=ident[:, :], in_=ident[:, :], compare_op=ALU.not_equal, fill=1.0, base=0,
                            pattern=[[-1, P]], channel_multiplier=1).then_inc(sem("ident_ready"), 1)
            g.affine_select(out=upper[:, :], in_=upper[:, :], compare_op=ALU.is_gt, fill=0.0, base=0,
                            pattern=[[1, P]], channel_multiplier=-1).then_inc(sem("upper_ready"), 1)
            g.iota(pidx_i[:, 0:1], [[1, 1]], base=0, channel_multiplier=1)
            g.iota(iot[:, 0, :], [[1, MTP]], base=0, channel_multiplier=0, allow_small_or_imprecise_dtypes=True)\
                .then_inc(sem("iota_ready"), 1)

            def rstd(s, i, tag):
                g.wait_ge(sem(f"{tag}_var"), i + 1)
                g.tensor_tensor(rs[s][:, :], ve[s][:, :], mhalf[:, 0:TT], ALU.pow).then_inc(sem(f"{tag}_rstd"), 1)

            def masked(i, ap, k):
                return g.tensor_tensor(by_seq(ap), by_seq(ap), over_tokens(mcond[:, k, part(i, GB)]), ALU.mult)

            def a_xb(i):
                if isinstance(i, int):
                    g.wait_ge(sem("bsel0_ready"), 2)
                wait_apart(g, *ua.read(i, "xT1"))
                for c in range(2):
                    last = g.tensor_tensor(by_seq(xb[:, c, :]), by_seq(xT[:, c, :]), over_tokens(bsel0[:, c, part(i, GB)]), ALU.add)
                last.then_inc(sem("xb_ready"), 1)

            def a_mask0(i):
                for name, h, k in (("nr", hn, 0), ("ts", ht, 1)):
                    for c in range(2):
                        wait_apart(g, *ua.read(i, f"{name}{c}"))
                        last = masked(i, h[:, c, :], k)
                last.then_inc(sem("hidden_masked"), 1)

            def a_mask1(i):
                for c in range(2):
                    wait_apart(g, *ua.read(i, f"su{c}"))
                    last = masked(i, hs2[:, c, :], 2)
                last.then_inc(sem("hidden_masked"), 1)

            def a_wsel(i):
                if isinstance(i, int):
                    g.wait_ge(sem("widx_ready"), 1)
                    g.wait_ge(sem("setup_read"), 3)
                else:
                    g.wait_ge(*ua.filled(i - 1, "ex"))
                for b in range(GB):
                    e = g.value_load(widx[0:1, part(i, GB, b, 1)], min_val=0, max_val=ND)
                    last = g.tensor_copy(wsel[:, b:b + 1, :], expT[:, bass.ds(e, 1), :])
                last.then_inc(sem("wsel_ready"), 1)

            def a_r1(i):
                rstd("A", i, "l1")
                g.wait_ge(*ua.read(i, "r11"))
                wide = lambda r: r[:, :].unsqueeze(1).broadcast_to([P, TT, D])
                g.tensor_tensor(x2row, nrow, wide(g1row), ALU.mult).then_inc(sem("x2_scaled"), 1)
                g.wait_ge(sem("x2_scaled"), i + 1)
                g.tensor_tensor(x2row, x2row, wide(be1row), ALU.add).then_inc(sem("x2_ready"), 1)
                rstd("A", i, "l2")

            def bias_mask(i, duo):
                wait_apart(g, sem(f"bias_loaded{duo}"), 64 * i + 64)
                for pr in range(2):
                    m = mneg[:, part(i, TT, 2 * duo + pr, 1), :]
                    last = g.tensor_tensor(bias[:, duo, pr, :, :], bias[:, duo, pr, :, :], m.broadcast_to([P, H, S]), ALU.add)
                last.then_inc(sem("bias_masked"), 1)

            def b_s(i, duo):
                bias_mask(i, duo)
                g.wait_ge(sem("scored"), 2 * i + (duo + 1))
                wide = smx[:, :, :].unsqueeze(3).broadcast_to([P, 2, H, S])
                g.tensor_tensor(sc[:, :, :, :], sc[:, :, :, :], wide, ALU.subtract).then_inc(sem("centered"), 1)

            def b_m(i, duo):
                g.wait_ge(sem("rsum_ready"), 2 * i + (duo + 1))
                wide = rsum[:, :, :].unsqueeze(3).broadcast_to([P, 2, H, S])
                g.tensor_tensor(sc[:, :, :, :], sc[:, :, :, :], wide, ALU.mult).then_inc(sem("probs_ready"), 1)

            def b_h4(i):
                g.wait_ge(sem("t_var"), i + 1)
                f = lambda k: tst[k][:, :, :].rearrange("p a b -> p (a b)")
                g.tensor_tensor(f("rstd"), f("var"), mhalf[:, :], ALU.pow).then_inc(sem("t_rstd"), 1)

            def c_rk(i):
                wait_apart(g, *ub.read(i + 1, "hr1"))
                g.wait_ge(sem("idx_ready"), i + 1)
                for n in range(TT):
                    for k in range(TOPK):
                        g.indirect_dma_start(out=rows_in, out_offset=bass.IndirectOffsetOnAxis(ap=idx[:, n, k:k + 1], axis=0),
                                             in_=hrow[:, n, :], in_offset=None).then_inc(sem("scattered"), 16)

            steps = {"A.xT": a_xb, "A.hid0": a_mask0, "A.sr2": a_mask1, "A.r0": lambda i: rstd("A", i, "l0"),
                     "A.x1": a_wsel, "A.r1": a_r1, "B.s0": lambda i: b_s(i, 0), "B.s1": lambda i: b_s(i, 1),
                     "B.m0": lambda i: b_m(i, 0), "B.m1": lambda i: b_m(i, 1), "B.r2": lambda i: rstd("B", i, "l3"),
                     "B.r3": lambda i: rstd("B", i, "l4"), "B.h4": b_h4, "C.rk": c_rk}
            for s in ORDER:
                if s in steps and s[0] == "A":
                    if s == "A.r0":
                        g.wait_ge(sem("mhalf_ready"), 1)
                    if s == "A.r1":
                        g.wait_ge(sem("rows_loaded"), 48)
                    steps[s](0)
            g.wait_ge(sem("mneg_ready"), 1)
            rounds(steps, 1, "AB")
            rounds(steps, 2)
            with g.Fori(3, NG) as i:
                rounds(steps, i)
            rounds(steps, NG, "BC")
            rounds(steps, NG + 1, "C")
            g.wait_ge(sem("zrow_ready"), 1)
            g.wait_ge(sem("pads_ready"), 1)
            for e in range(NE):
                g.indirect_dma_start(out=rows_in, out_offset=bass.IndirectOffsetOnAxis(ap=padu[:, e:e + 1], axis=0),
                                     in_=zrow, in_offset=None).then_inc(sem("scattered"), 16)
            g.wait_ge(sem("plan_ready"), 1)

            def bias_of(t_, k, first=False):
                e = g.value_load(meta[0:1, 0, part(t_, 1)], min_val=0, max_val=NE - 1)
                if not first:
                    g.wait_ge(sem("hid_done1"), t_ - 1)
                g.tensor_copy(b1c[:, k, :], eb1[:, bass.ds(e * FC, FC)]).then_inc(sem("b1_ready"), 1)

            bias_of(0, 0, True)
            bias_of(1, 1, True)
            with g.Fori(1, (MT - 1) // 2) as j:
                for k in range(2):
                    bias_of(2 * j + k, k)
            bias_of(MT - 1, 0)

            g.wait_ge(sem("y_stored0"), 16 * (MT // 2 + 1))
            g.wait_ge(sem("y_stored1"), 16 * (MT // 2))

            def gather(q, k):
                if not (isinstance(q, int) and q == 0):
                    g.wait_ge(sem("mixed"), 4 * q + (k - 3))
                    g.wait_ge(sem(f"gathered{k}"), 32 * q)
                g.tensor_copy(idxc[:, k:k + 1, :], slot_u[:, part(q, 4, k, 1), :]).then_inc(sem("idxc_ready"), 1)
                wait_apart(g, sem("idxc_ready"), 4 * q + (k + 1))
                for m in range(TOPK):
                    g.indirect_dma_start(out=got[:, k, m, :], out_offset=None, in_=rows_out,
                                         in_offset=bass.IndirectOffsetOnAxis(ap=idxc[:, k, m:m + 1], axis=0))\
                        .then_inc(sem(f"gathered{k}"), 16)

            for k in range(4):
                gather(0, k)
            with g.Fori(1, NT // 4) as q:
                for k in range(4):
                    gather(q, k)


def kernel(**inputs):
    import numpy as np
    import concourse.bacc as bacc
    from concourse.bass_utils import run_bass_kernel_spmd

    nc = bacc.Bacc("TRN2", target_bir_lowering=False, num_devices=1)
    arrays, tensors = {}, {}
    for name in inputs:
        a = np.ascontiguousarray(inputs[name])
        arrays[name] = a
        tensors[name] = nc.dram_tensor(name, a.shape, mybir.dt.from_np(a.dtype), kind="ExternalInput").ap()
    half = D // 2
    arrays["freqs"] = np.exp(np.arange(half, dtype=np.float32) * np.float32(-np.log(10000.0) / (half - 1)))
    tensors["freqs"] = nc.dram_tensor("freqs", (half,), F32, kind="ExternalInput").ap()
    tensors["out"] = nc.dram_tensor("out", (B, S, D), F32, kind="ExternalOutput").ap()
    build(nc, tensors)
    r = run_bass_kernel_spmd(nc, [arrays], core_ids=[0])
    return r.results[0]["out"]
```

```python
import concourse.bass as bass
from concourse import mybir
from contextlib import ExitStack

F32 = mybir.dt.float32
BF16 = mybir.dt.bfloat16
I32 = mybir.dt.int32
U32 = mybir.dt.uint32
U8 = mybir.dt.uint8
ALU = mybir.AluOpType
ACT = mybir.ActivationFunctionType
AX = mybir.AxisListType

B, S, D = 64, 64, 256
P = 128
DC = D // P
GB = 8
GT = GB * S
NG = B // GB
TT = GT // P
NT = B * S // P
H, HD = 16, 16
FF = 1024
FC = FF // P
A1 = 64
ND = 16
NE, TOPK = 8, 2
NSUB, SE, SH = 32, 64, 128
CAP = B * S + P
MT = TOPK * B * S // P + NE - 1
MTP = MT + 1
EPS, EPS_T = 1e-5, 1e-8
NEG = -1e30
DX = D + 2
MAGIC = 12582912.0
INV2PI, PI = 0.15915494309189535, 3.141592653589793
C1, C2, C3 = 6.28125, 0.0019350051879882812, 3.0199159819e-07

A_UNITS = ([(f"xT{c}", "dve", (c,)) for c in range(2)]
           + [(n, "act", (k % 4,)) for k, n in enumerate(["nr0", "nr1", "ts0", "ts1", "sr0", "sr1", "sr2", "sr3"])]
           + [("su0", "act", (0,)), ("su1", "act", (1,)), ("y0", "dve", (2,)), ("y1", "dve", (3,)),
              ("r00", "dve", (0,)), ("r01", "dve", (1,)), ("x10", "act", (2,)), ("x11", "act", (3,)),
              ("dn", "act", (0,)), ("ex", "dve", (1,)), ("u0", "dve", (2,)), ("u1", "dve", (3,)),
              ("r10", "dve", (0,)), ("r11", "dve", (1,)), ("x20", "dve", (2,)), ("x21", "dve", (3,)),
              ("q0", "act", (0,)), ("q1", "act", (1,)), ("k0", "dve", (2,)), ("k1", "dve", (3,)),
              ("v0", "dve", (0,)), ("v1", "dve", (1,)), ("v2", "dve", (2,)), ("v3", "dve", (3,))])
B_TAIL = [("h40", "act", (1,)), ("h41", "act", (2,)), ("lg", "dve", (2,)), ("hr0", "act", (3,)), ("hr1", "act", (0,)),
          ("rk", "dve", (1,)), ("ct", "dve", (2,)), ("b20", "dve", (1,)), ("b21", "dve", (2,))]
B_UNITS = (B_TAIL[:2] + [("sc0", "dve", (0, 1, 2, 3))] + B_TAIL[2:5]
           + [(f"pt0{k}", "act" if k % 2 else "dve", (k,)) for k in range(4)] + [("cx0", "act", (0,))] + B_TAIL[5:7]
           + [("sc1", "dve", (0, 1, 2, 3))]
           + [(f"pt1{k}", "act" if k % 2 else "dve", (k,)) for k in range(4)] + [("cx1", "act", (0,))]
           + [("o0", "dve", (1,)), ("o1", "dve", (2,)), ("r20", "dve", (3,)), ("r21", "dve", (0,))] + B_TAIL[7:]
           + [("h30", "act", (3,)), ("h31", "act", (0,))]
           + [(f"f{c}", "act", ((c + 1) % 4,)) for c in range(FC)]
           + [("g0", "dve", (1,)), ("g1", "dve", (2,)), ("r30", "dve", (3,)), ("r31", "dve", (0,))])

ORDER = ["A.xT", "C.h4", "B.s0", "A.hid0", "B.e0", "C.tok", "A.hid1a", "B.m0", "C.hf", "A.mask0", "A.hid1b", "C.lg",
         "B.t0", "B.bias", "C.ge", "B.p0", "C.rk", "C.ct", "B.s1", "A.sr2", "B.e1", "A.mask1", "B.m1", "A.out", "B.t1",
         "A.r0", "B.p1", "B.o", "A.x1", "B.r2", "A.dn", "C.b2", "A.ex", "C.scat", "B.h3", "A.up", "B.f1a", "B.f1b",
         "A.r1", "B.f1c", "B.f1d", "B.f2a", "A.x2", "B.f2b", "A.q", "B.r3", "A.k", "A.v0", "A.v1", "A.bias"]


class Units:

    def __init__(self, units, banks, filled, read_by, late=(), end=NG):
        self.units, self.banks, self.filled_sem, self.read_by = units, banks, filled, read_by
        self.late, self.end = {n for n, _, _ in late}, end
        self.at = {n: k for k, (n, _, _) in enumerate(units)}

    def present(self, i, name):
        if isinstance(i, int) and i in (0, self.end):
            return (name in self.late) == (i == self.end)
        return True

    def count(self, i, names, name):
        here = len([n for n in names[:names.index(name) + 1] if self.present(i, n)])
        if isinstance(i, int) and i == 0:
            return here
        return i * len(names) + (here - len([n for n in names if n in self.late]))

    def filled(self, i, name):
        return self.filled_sem, self.count(i, [n for n, _, _ in self.units], name)

    def read(self, i, name):
        who = self.units[self.at[name]][1]
        return self.read_by[who], self.count(i, [n for n, w, _ in self.units if w == who], name)

    def wait_free(self, pe, i, name):
        k, last = self.at[name], {}
        for bank in self.units[k][2]:
            here = [j for j, u in enumerate(self.units[:k]) if bank in u[2] and self.present(i, u[0])]
            if here:
                before = (1, here[-1])
            elif isinstance(i, int) and i == 0:
                continue
            else:
                before = (0, max(j for j, u in enumerate(self.units) if bank in u[2] and self.present(i - 1, u[0])))
            who = self.units[before[1]][1]
            last[who] = max(last.get(who, before), before)
        for same, j in last.values():
            pe.wait_ge(*self.read(i if same else i - 1, self.units[j][0]))

    def bank(self, name):
        return self.banks[:, self.units[self.at[name]][2][0], :]

    def fill(self, ins):
        ins.then_inc(self.filled_sem, 1)

    def done(self, ins, name):
        ins.then_inc(self.read_by[self.units[self.at[name]][1]], 1)


VECS = [("L0_cond_b1_nr", 2), ("L0_cond_b2_nr", 2), ("L0_cond_b1_tsr", 2), ("L0_cond_b2_tsr", 2),
        ("L0_cond_b1_sr", 4), ("L0_cond_b2_sr", 2), ("L0_cond_b3_sr", 2), ("L0_cond_gamma", 2),
        ("L0_cond_beta", 2), ("L1_cond_up_b", 2), ("L2_cond_b_ada", 4), ("L2_cond_bq", 2), ("L2_cond_bk", 2),
        ("L2_cond_bo", 2), ("L2_cond_b1", 8), ("L2_cond_b2", 2), ("L2_cond_g2", 2), ("L2_cond_beta2", 2),
        ("L3_cond_ln_g", 2), ("L3_cond_ln_b", 2), ("L3_cond_hyp_b1", 1), ("L3_cond_hyp_b2", 1),
        ("L3_cond_sty_b2", 4), ("freqs", 1)]
HALVES = ["L1_cond_down_b", "L3_cond_sty_b1"]
ROW, NROWS = {}, 0
for _name, _n in VECS:
    ROW[_name] = NROWS
    NROWS += _n
for _name in HALVES:
    ROW[_name] = NROWS
    NROWS += 1


def part(i, n, at=0, size=None):
    size = n if size is None else size
    if isinstance(i, int):
        return slice(i * n + at, i * n + at + size)
    return bass.ds(i * n + at, size)


def wait_apart(engine, semaphore, value):
    if not isinstance(value, int):
        value = engine.to_reg(value)
        engine.wait_ge(semaphore, 1)
    engine.wait_ge(semaphore, value)


def build(nc, t):
    ctx = ExitStack()
    with ctx:
        def sb(name, shape, dt=F32):
            return ctx.enter_context(nc.sbuf_tensor(name, shape, dt))

        sems = {}

        def sem(name):
            if name not in sems:
                sems[name] = ctx.enter_context(nc.semaphore(name))
            return sems[name]

        def dram(name):
            return nc.dram_tensor(name, DRAMS[name], F32, kind="Internal").ap()

        DRAMS = {"rows_in": [NE * CAP, DX], "sums": [B * S + P, D]}
        rows_in = dram("rows_in")
        sums = dram("sums")

        ident = sb("ident", [P, P])
        upper = sb("upper", [P, P], BF16)
        ones = sb("ones", [P, P], BF16)
        head_half = sb("head_half", [P, 2])
        pidx = sb("pidx", [P, 1])
        pidx_i = sb("pidx_i", [P, 2], I32)
        iot = sb("iot", [P, 2, MTP])
        eoff = sb("eoff", [P, NE])
        mhalf = sb("mhalf", [P, DC * GB])
        colv = sb("colv", [P, NROWS])
        bq4 = sb("bq4", [P, DC])
        eb1 = sb("eb1", [P, NE * FC])
        wl0 = sb("wl0", [P, 18 * D])
        w0 = lambda a, k, n: wl0[:, a * D:a * D + k * n].rearrange("p (k n) -> p k n", k=k)
        w1nr, w2nr, w1ts, w2ts = w0(0, 2, D), w0(2, 2, D), w0(4, 2, D), w0(6, 2, D)
        w1sr, w2sr, w3sr = w0(8, 2, 2 * D), w0(12, 4, D), w0(16, 2, D)
        w1slot = [wl0[:, k * 2048:(k + 1) * 2048].rearrange("p (k n) -> p k n", k=2) for k in range(2)]
        downT = sb("downT", [P, DC, A1])
        upT = sb("upT", [A1, D])
        expT = sb("expT", [A1, ND + 1, A1])
        wsel = sb("wsel", [A1, GB, A1])
        wat = sb("wat", [P, 4 * DC * D])
        wq, wk, wv, wo = (wat[:, k * 512:(k + 1) * 512].rearrange("p (k n) -> p k n", k=2) for k in range(4))
        hid = wat[:, :].rearrange("p (a c n) -> p a c n", a=2, c=FC)
        wff = sb("wff", [P, 16 * D])
        wf1 = wff[:, 0:8 * D].rearrange("p (k n) -> p k n", k=2)
        wf2 = wff[:, 8 * D:16 * D].rearrange("p (k n) -> p k n", k=FC)
        xs = wff[:, 0:2 * DX].rearrange("p (a n) -> p a n", a=2)
        xsT = wff[:, 3 * D:5 * D].rearrange("p (a n) -> p a n", a=2)
        ys = wff[:, 5 * D:7 * D].rearrange("p (a n) -> p a n", a=2)
        wrt = sb("wrt", [P, DC, NE])
        b2e = sb("b2e", [NE, D])
        g1row, be1row, bvrow = (sb(n, [P, D]) for n in ("g1row", "be1row", "bvrow"))
        mneg = sb("mneg", [P, B // 2, S], BF16)
        ints = sb("ints", [P, 4, B], I32)
        idf = sb("idf", [P, 4, B])
        mcond = sb("mcond", [P, 3, B])
        bsel0 = sb("bsel0", [P, DC, B])
        bsel1 = sb("bsel1", [A1, B])
        widx = sb("widx", [1, B], I32)
        ada = sb("ada", [P, 4, B])
        sty = sb("sty", [P, 4, B])
        tok = sb("tok", [P, TT])
        base = sb("base", [P, NE])

        early = sb("early", [P, NE * FC * D])
        w2all = early[:, :].rearrange("p (e n) -> p e n", n=D)

        def cut(k, n, shape, whole=early, parts=P):
            v = whole[0:parts, k * 512:k * 512 + n]
            names = "abcd"[:len(shape)]
            if len(shape) == 1:
                return v
            return v.rearrange(f"p ({' '.join(names)}) -> p {' '.join(names)}", **dict(zip(names, shape)))

        xin = cut(0, 1024, [TT, D])
        xb = cut(0, 1024, [DC, GT])
        xT = cut(2, 1024, [DC, GT])
        hn, ht = cut(4, 1024, [DC, GT]), cut(6, 1024, [DC, GT])
        hs, hs2 = cut(8, 2048, [4, GT]), cut(12, 1024, [DC, GT])
        nrow = cut(4, 1024, [TT, D])
        x1T, x2row = cut(8, 1024, [DC, GT]), cut(10, 1024, [TT, D])
        hd, he = cut(12, 512, [GT], parts=A1), cut(13, 512, [GT], parts=A1)
        qT = cut(14, 1024, [DC, GT])
        kbd = cut(16, 2048, [DC, GB, 2, S])
        vbd = cut(20, 2048, [GB, H // 2, 2 * HD])
        bias = cut(24, 4096, [2, 2, H, S])
        xmT = sb("xmT", [P, DC, GT])
        sc = sb("sc", [P, 2, H, S])
        late = sb("late", [P, 8 * 512])
        pT = sb("pT", [P, 4, GT])
        x3T = pT[:, 2:4, :]
        h3T = pT[:, 0:2, :]
        fT = late[:, 0:4096].rearrange("p (a b) -> p a b", a=FC)
        ctxT = cut(0, 1024, [DC, GT], late)
        n3row = cut(2, 1024, [TT, D], late)
        n4row = cut(0, 1024, [TT, D], late)
        h4T = cut(2, 1024, [DC, GT], late)
        hfT = cut(4, 1024, [DC, GT], late)
        xres = sb("xres", [P, TT, D])
        hrow = sb("hrow", [P, TT, TOPK, DX])
        slot = sb("slot", [P, TT, TOPK])
        smx, ssum, rsum = (sb(n, [P, 2, H]) for n in ("smx", "ssum", "rsum"))
        st = {k: sb(f"st_{k}", [P, TT, 6]) for k in "AB"}
        mv = {k: sb(f"mv_{k}", [P, TT, 2]) for k in "AB"}
        ve = {k: sb(f"ve_{k}", [P, TT]) for k in "AB"}
        rs = {k: sb(f"rs_{k}", [P, TT]) for k in "AB"}
        st4 = sb("st4", [P, DC, GB, 6])
        tst = {n: sb(f"t_{n}", [P, DC, GB]) for n in ("sum", "dif", "sq", "var", "rstd", "mul", "mm", "add")}
        lgs = sb("lgs", [P, TT, NE])
        mx8 = sb("mx8", [P, TT, NE])
        mi8 = sb("mi8", [P, TT, NE], U32)
        mif = sb("mif", [P, TT, TOPK])
        oh = sb("oh", [P, TOPK, TT, NE])
        picked = sb("picked", [P, TT, NE], BF16)
        gd, ge, gp = (sb(n, [P, TT]) for n in ("gd", "ge", "gp"))
        cm = sb("cm", [P, TOPK, TT, NE])
        cmix = sb("cmix", [P, TT, NE])
        pos = sb("pos", [P, TT, NE])
        posk = sb("posk", [P, TOPK, TT, NE])
        idx = sb("idx", [P, TT, TOPK], U32)
        ctT = cut(6, 512, [GT], late, NE)
        cnt = sb("cnt", [P, NE])
        plan_space = sc[:, :, :, :].rearrange("p a h k -> p (a h k)")
        plan = {n: plan_space[:, k * MTP:(k + 1) * MTP]
                for k, n in enumerate(("e", "start", "idle", "src"))}
        pl8 = {n: sb(f"pl8_{n}", [P, NE]) for n in ("n", "incl", "one")}
        pge = plan_space[:, 4 * MTP:(4 + NE) * MTP].rearrange("p (t e) -> p t e", e=NE)
        meta = sb("meta", [P, 2, MTP], I32)
        padp = sb("padp", [P, NE])
        padu = sb("padu", [P, NE], U32)
        b1c = sb("b1c", [P, 2, FC])
        info = sb("info", [P, MTP, 2])
        idxc = sb("idxc", [P, 2], U32)

        zrow = plan_space[:, 900:900 + DX]

        vec = sc[:, 0, 0:2, :].rearrange("p a b -> p (a b)")
        eb1r = sc[0:NE * FC, 0, 2:4, :].rearrange("p a b -> p (a b)")
        upW = sc[:, 0, 4:6, :]
        downW = sc[0:A1, 0, 6:10, :].rearrange("p a b -> p (a b)")
        expW = sc[0:A1, 1, :, :]
        mask8 = pT[:, 2, :].bitcast(U8).rearrange("p (n k) -> p n k", k=S)
        semb = sc[0:NSUB, 0, 10, :]
        expb = sc[0:ND, 0, 11, :]
        demb = sc[0:ND, 0, 12, :]
        hw1 = pT[0:SE, 0, 0:SH]
        hw2 = pT[:, 0, SH:2 * SH]
        sw1 = pT[:, 0, 2 * SH:2 * SH + SH // 2]
        sw2 = pT[0:SH // 2, 1, :]
        wada = late[:, 0:1024].rearrange("p (k n) -> p k n", k=2)
        scr = lambda k, n=B: late[:, 1024 + 64 * k:1024 + 64 * k + n]
        sce = late[:, 3072:3072 + 512].rearrange("p (a b) -> p a b", a=8)

        PA = ctx.enter_context(nc.psum_tensor("banks_a", [P, 4, 512], F32))
        PB = ctx.enter_context(nc.psum_tensor("banks_b", [P, 4, 512], F32))
        ua = Units(A_UNITS, PA, sem("a_filled"), {"act": sem("a_read_by_act"), "dve": sem("a_read_by_dve")})
        ub = Units(B_UNITS, PB, sem("b_filled"), {"act": sem("b_read_by_act"), "dve": sem("b_read_by_dve")},
                   B_TAIL)

        col = lambda name, c=0, parts=P: colv[0:parts, ROW[name] + c:ROW[name] + c + 1]
        v_seqs = lambda n: [4 * (n % 2) + 2 * h + n // 2 for h in range(2)]
        by_seq = lambda ap: ap.rearrange("p (b s) -> p b s", s=S)

        def over_tokens(ap, n=GB):
            return ap.unsqueeze(2).broadcast_to([ap.shape[0], n, S])

        half = lambda i, duo, pr: 4 * i + (2 * duo + pr + 1)

        def rounds(steps, i, streams="ABC"):
            for s in ORDER:
                if s in steps and s[0] in streams:
                    k = "ABC".index(s[0])
                    steps[s](i - k if k else i)

        def added(k):
            return sem(f"added{k}"), 16 * ((MT + 1 - k) // 2)

        def copy_out(engine, parts):
            out_v = t["out"].rearrange("b s d -> (b s) d")
            for n in parts:
                rows = slice(n * GT, (n + 1) * GT)
                engine.dma_start(out_v[rows, :].rearrange("(a b) d -> a (b d)", b=S // 2),
                                 sums[rows, :].rearrange("(a b) d -> a (b d)", b=S // 2)).then_inc(sem("out_stored"), 16)

        block = ctx.enter_context(nc.Block())
        NVEC = len(VECS) + len(HALVES)
        W_A = [("w1nr", w1nr, "L0_cond_w1_nr"), ("w1ts", w1ts, "L0_cond_w1_tsr"), ("w1sr", w1sr, "L0_cond_w1_sr"),
               ("w2sr", w2sr, "L0_cond_w2_sr"), ("w2nr", w2nr, "L0_cond_w2_nr"), ("w2ts", w2ts, "L0_cond_w2_tsr"),
               ("w3sr", w3sr, "L0_cond_w3_sr")]
        W_L2 = [(wq, "L2_cond_Wq"), (wk, "L2_cond_Wk"), (wv, "L2_cond_Wv"), (wo, "L2_cond_Wo"),
                (wf1, "L2_cond_W1"), (wf2, "L2_cond_W2")]
        kview = lambda name: t[name].rearrange("(k p) n -> p k n", p=P)

        @block.sync
        def _(sp):
            x_v = t["x"].rearrange("b s d -> (b s) d").rearrange("(n p) d -> p n d", p=P)
            mask_v = t["mask_Bx1xSxS_bk0"].rearrange("(n two) o q k -> two q (n o) k", two=2)
            bias_v = t["fside_Bx16xSxS_0"].rearrange("(g b) h q k -> b q g h k", b=GB)
            sp.dma_start(xin, x_v[:, 0:TT, :]).then_inc(sem("x_loaded"), 16)
            sp.wait_ge(sem("vec_cleared"), 1)
            for name, n in VECS + [(h, 0) for h in HALVES]:
                r = ROW[name]
                if n:
                    sp.dma_start(vec[r:r + n, :], t[name].rearrange("(c p) -> c p", p=P)).then_inc(sem("vec_loaded"), 16)
                else:
                    sp.dma_start(vec[r:r + 1, 0:A1], t[name].rearrange("(c p) -> c p", p=A1)).then_inc(sem("vec_loaded"), 16)
            for k, name in enumerate(["itok_B_0_2", "itok_B_0_15", "itok_B_34_63", "itok_B_6_14"]):
                sp.dma_start(ints[:, k, :], t[name].partition_broadcast(P)).then_inc(sem("ints_loaded"), 16)
            sp.dma_start(downW, t["L1_cond_down_W"]).then_inc(sem("l1_loaded"), 16)
            sp.dma_start(upW, t["L1_cond_up_W"].rearrange("(k p) a -> p k a", p=P)).then_inc(sem("l1_loaded"), 16)
            sp.dma_start(expW, t["L1_cond_expert_W"].rearrange("e o a -> o e a")).then_inc(sem("l1_loaded"), 16)
            sp.dma_start(expb, t["L1_cond_expert_b"]).then_inc(sem("l1_loaded"), 16)
            sp.dma_start(demb, t["L1_cond_domain_emb"]).then_inc(sem("l1_loaded"), 16)
            sp.dma_start(eb1r, t["L3_cond_exp_b1"].rearrange("e (c p) -> (e c) p", p=P)).then_inc(sem("l1_loaded"), 16)
            for row, name in ((g1row, "L1_cond_ln_gamma"), (be1row, "L1_cond_ln_beta"), (bvrow, "L2_cond_bv")):
                sp.dma_start(row[:, :], t[name].partition_broadcast(P)).then_inc(sem("rows_loaded"), 16)
            for two in range(2):
                sp.dma_start(mask8[two * S:(two + 1) * S, :, :], mask_v[two]).then_inc(sem("mask_loaded"), 16)
            sp.dma_start(wada, kview("L2_cond_W_ada")).then_inc(sem("tab_loaded"), 16)
            for dst, name in ((semb, "L3_cond_subj_emb"), (hw1, "L3_cond_hyp_w1"), (hw2, "L3_cond_hyp_w2"),
                              (sw1, "L3_cond_sty_w1"), (sw2, "L3_cond_sty_w2")):
                sp.dma_start(dst, t[name]).then_inc(sem("tab_loaded"), 16)
            for dst, name in W_L2:
                sp.dma_start(dst, kview(name)).then_inc(sem("l2_loaded"), 16)
            sp.dma_start(wrt[:, :, :], kview("L3_cond_router_w")).then_inc(sem("l3_loaded"), 16)
            sp.dma_start(b2e[:, :], t["L3_cond_exp_b2"]).then_inc(sem("l3_loaded"), 16)

            def load_bias(i, duo):
                for b in range(4):
                    sp.dma_start(bias[(b % 2) * S:(b % 2 + 1) * S, duo, b // 2, :, :],
                                 bias_v[4 * duo + b, :, part(i, 1), :, :].rearrange("q g h k -> q (g h) k"))\
                        .then_inc(sem(f"bias_loaded{duo}"), 16)

            for duo in range(2):
                load_bias(0, duo)

            sums_v = sums[0:B * S, :].rearrange("(n p) d -> p n d", p=P)

            def load_group(i):
                sp.wait_ge(*ua.read(i - 1, "y1"))
                sp.dma_start(xin, x_v[:, part(i, TT), :]).then_inc(sem("x_loaded"), 16)
                for duo in range(2):
                    sp.wait_ge(sem("scored"), half(i - 1, duo, 1))
                    load_bias(i, duo)

            def store_x(i):
                sp.wait_ge(*ub.read(i + 1, "b21"))
                sp.dma_start(sums_v[:, part(i, TT), :], xres[:, :, :]).then_inc(sem("x_stored"), 16)

            load_group(1)
            with sp.Fori(2, NG) as i:
                load_group(i)
                store_x(i - 2)
            sp.wait_ge(*ub.read(NG - 1, "cx1"))
            sp.wait_ge(*ub.filled(NG - 1, "cx1"))
            for e in range(NE):
                sp.dma_start(w2all[:, e * FC:(e + 1) * FC, :],
                             t["L3_cond_exp_w2"][e].rearrange("(c p) n -> p c n", p=P)).then_inc(sem("w2_loaded"), 16)
            store_x(NG - 2)
            store_x(NG - 1)
            sp.wait_ge(sem("plan_ready"), 1)
            sp.wait_ge(sem("scattered"), 16 * (NG * TT * TOPK + NE))

            def load_tile(t_, k):
                e = sp.value_load(meta[0:1, 0, part(t_, 1)], min_val=0, max_val=NE - 1)
                sp.dma_start(w1slot[k], t["L3_cond_exp_w1"][bass.ds(e, 1), :, :].rearrange("e (k p) n -> p (e k) n", p=P))\
                    .then_inc(sem(f"w1_loaded{k}"), 16)

            def load_rows(t_, k):
                r = sp.value_load(meta[0:1, 1, part(t_, 1)], min_val=0, max_val=(NE * CAP) - P)
                sp.dma_start(xs[:, k, :], rows_in[bass.ds(r, P), :]).then_inc(sem(f"xs_loaded{k}"), 16)

            load_rows(0, 0)
            load_tile(0, 0)
            load_rows(1, 1)
            load_tile(1, 1)
            sp.wait_ge(sem("info_kept"), 1)
            load_rows(2, 0)
            with sp.Fori(1, (MT - 1) // 2) as j:
                for k in range(2):
                    sp.wait_ge(sem("g1_filled"), 4 * j + 2 * (k - 1))
                    load_tile(2 * j + k, k)
                    sp.wait_ge(sem("info_kept"), 2 * j + k)
                    load_rows(2 * j + (k + 1), 1 - k)
            sp.wait_ge(sem("g1_filled"), 2 * (MT - 2))
            load_tile(MT - 1, 0)
            for k in range(2):
                sp.wait_ge(*added(k))
            copy_out(sp, range(0, 4))
            sp.wait_ge(sem("out_stored"), 16 * 8)

        @block.tensor
        def _(pe):
            mm = nc.tensor.matmul

            def dense(u, i, name, pairs, rows=P, cols=slice(0, GT)):
                u.wait_free(pe, i, name)
                o = u.bank(name)[0:rows, cols]
                for k, (a, b) in enumerate(pairs):
                    last = mm(o, a, b, start=(k == 0), stop=(k == len(pairs) - 1))
                u.fill(last)

            def to_rows(u, i, names, src):
                for n, name in enumerate(names):
                    u.wait_free(pe, i, name)
                    for h in range(2):
                        for c in range(DC):
                            at = (2 * n + h) * P
                            last = nc.tensor.transpose(u.bank(name)[:, h * D + c * P:h * D + (c + 1) * P],
                                                       src[:, c, at:at + P], ident[:, :])
                    u.fill(last)

            def from_rows(u, i, names, src):
                for c, name in enumerate(names):
                    u.wait_free(pe, i, name)
                    for n in range(TT):
                        last = nc.tensor.transpose(u.bank(name)[:, n * P:(n + 1) * P],
                                                   src[:, n, c * P:(c + 1) * P], ident[:, :])
                    u.fill(last)

            ck = lambda c: slice(c * P, (c + 1) * P)
            ready0 = lambda i: isinstance(i, int) and i == 0

            def a_xT(i):
                if ready0(i):
                    pe.wait_ge(sem("ident_ready"), 1)
                pe.wait_ge(sem("x_loaded"), 16 * i + 16)
                from_rows(ua, i, ["xT0", "xT1"], xin)

            def a_hid0(i):
                pe.wait_ge(*ua.read(i, "xT1"))
                if ready0(i):
                    pe.wait_ge(sem("w1nr_loaded"), 16)
                for c in range(2):
                    dense(ua, i, f"nr{c}", [(w1nr[:, k, ck(c)], xT[:, k, :]) for k in range(2)])
                if ready0(i):
                    pe.wait_ge(sem("w1ts_loaded"), 16)
                for c in range(2):
                    dense(ua, i, f"ts{c}", [(w1ts[:, k, ck(c)], xT[:, k, :]) for k in range(2)])

            def a_hid1(i, chunks):
                if ready0(i):
                    pe.wait_ge(sem("w1sr_loaded"), 16)
                for c in chunks:
                    dense(ua, i, f"sr{c}", [(w1sr[:, k, ck(c)], xT[:, k, :]) for k in range(2)])

            def a_sr2(i):
                if ready0(i):
                    pe.wait_ge(sem("w2sr_loaded"), 16)
                pe.wait_ge(*ua.read(i, "sr3"))
                for c in range(2):
                    dense(ua, i, f"su{c}", [(w2sr[:, k, ck(c)], hs[:, k, :]) for k in range(4)])

            def a_out(i):
                if ready0(i):
                    for n in ("w2nr", "w2ts", "w3sr"):
                        pe.wait_ge(sem(f"{n}_loaded"), 16)
                pe.wait_ge(sem("hidden_masked"), 2 * i + 1)
                for c in range(2):
                    ua.wait_free(pe, i, f"y{c}")
                    for n, (w, h) in enumerate(((w2nr, hn), (w2ts, ht))):
                        for k in range(2):
                            mm(ua.bank(f"y{c}"), w[:, k, ck(c)], h[:, k, :], start=(n + k == 0), stop=False)
                pe.wait_ge(sem("hidden_masked"), 2 * i + 2)
                for c in range(2):
                    for k in range(2):
                        last = mm(ua.bank(f"y{c}"), w3sr[:, k, ck(c)], hs2[:, k, :], start=False, stop=(k == 1))
                    ua.fill(last)

            def a_r0(i):
                pe.wait_ge(*ua.read(i, "y1"))
                to_rows(ua, i, ["r00", "r01"], xT)

            def a_x1(i):
                pe.wait_ge(*ua.read(i, "r01"))
                from_rows(ua, i, ["x10", "x11"], nrow)

            def a_dn(i):
                if ready0(i):
                    pe.wait_ge(sem("setup_read"), 3)
                pe.wait_ge(*ua.read(i, "x11"))
                dense(ua, i, "dn", [(downT[:, k, :], x1T[:, k, :]) for k in range(2)], A1)

            def a_ex(i):
                pe.wait_ge(sem("wsel_ready"), i + 1)
                ua.wait_free(pe, i, "ex")
                wait_apart(pe, *ua.read(i, "dn"))
                for b in range(GB):
                    at = slice(b * S, (b + 1) * S)
                    last = mm(ua.bank("ex")[0:A1, at], wsel[:, b, :], hd[:, at], start=True, stop=True)
                ua.fill(last)

            def a_up(i):
                pe.wait_ge(*ua.read(i, "ex"))
                for c in range(2):
                    dense(ua, i, f"u{c}", [(upT[:, ck(c)], he[:, :])])

            def a_r1(i):
                pe.wait_ge(*ua.read(i, "u1"))
                to_rows(ua, i, ["r10", "r11"], x1T)

            def a_x2(i):
                pe.wait_ge(sem("n2_ready"), i + 1)
                from_rows(ua, i, ["x20", "x21"], nrow)

            def a_q(i):
                if ready0(i):
                    pe.wait_ge(sem("l2_loaded"), 16 * len(W_L2))
                pe.wait_ge(sem("xm_ready"), i + 1)
                for c in range(2):
                    dense(ua, i, f"q{c}", [(wq[:, k, ck(c)], xmT[:, k, :]) for k in range(2)])

            def a_k(i):
                for c in range(2):
                    dense(ua, i, f"k{c}", [(wk[:, k, ck(c)], xmT[:, k, :]) for k in range(2)])

            def a_v(i, units):
                for n in units:
                    ua.wait_free(pe, i, f"v{n}")
                    for h, b in enumerate(v_seqs(n)):
                        o = ua.bank(f"v{n}")[:, h * D:(h + 1) * D]
                        for k in range(2):
                            if b + 1 < GB:
                                last = mm(o, xmT[:, k, b * S:(b + 2) * S], wv[:, k, :], start=(k == 0), stop=(k == 1))
                        if b + 1 == GB:
                            for j, bj in enumerate((b, 0)):
                                for k in range(2):
                                    last = mm(o[j * S:(j + 1) * S, :], xmT[:, k, bj * S:(bj + 1) * S], wv[:, k, :],
                                              start=(k == 0), stop=(k == 1))
                    ua.fill(last)

            def b_s(i, duo):
                if duo == 0:
                    pe.wait_ge(*ua.read(i, "q1"))
                    pe.wait_ge(*ua.read(i, "k1"))
                ub.wait_free(pe, i, f"sc{duo}")
                for pr in range(2):
                    for b in range(2):
                        g = 4 * duo + 2 * pr + b
                        for c in range(DC):
                            for r in range(4):
                                rows = slice(32 * r, 32 * r + 32)
                                last = mm(PB[b * S:(b + 1) * S, r, pr * D + c * P:pr * D + (c + 1) * P],
                                          qT[rows, c, g * S:(g + 1) * S],
                                          kbd[rows, c, g, :, :].rearrange("p j s -> p (j s)"), start=True, stop=True)
                ub.fill(last)

            def b_t(i, duo):
                for k in range(4):
                    if k % 2 == 0:
                        pe.wait_ge(sem("probs_ready"), half(i, duo, k // 2))
                    ub.wait_free(pe, i, f"pt{duo}{k}")
                    for m in range(4):
                        n = 4 * k + m
                        last = nc.tensor.transpose(ub.bank(f"pt{duo}{k}")[:, m * P:(m + 1) * P],
                                                   sc[:, n // 8, 2 * (n % 8):2 * (n % 8) + 2, :].rearrange("p a b -> p (a b)"),
                                                   ident[:, :])
                    ub.fill(last)

            def b_p(i, duo):
                pe.wait_ge(*ub.read(i, f"pt{duo}2"))
                pe.wait_ge(*ub.read(i, f"pt{duo}3"))
                if duo == 0:
                    pe.wait_ge(*ua.read(i, "v3"))
                ub.wait_free(pe, i, f"cx{duo}")
                for pr in range(2):
                    for b in range(2):
                        for c in range(DC):
                            for r in range(4):
                                n = 8 * pr + 4 * c + r
                                at = c * D + pr * P + b * S
                                last = mm(ub.bank(f"cx{duo}")[32 * r:32 * r + 32, at:at + S],
                                          vbd[:, 4 * duo + 2 * pr + b, 4 * c + r, :],
                                          pT[:, n // 4, (n % 4) * P + b * S:(n % 4) * P + (b + 1) * S], start=True, stop=True)
                ub.fill(last)

            def b_o(i):
                pe.wait_ge(*ub.read(i, "cx1"))
                for c in range(2):
                    dense(ub, i, f"o{c}", [(wo[:, k, ck(c)], ctxT[:, k, :]) for k in range(2)])

            def b_r2(i):
                pe.wait_ge(*ub.read(i, "o1"))
                to_rows(ub, i, ["r20", "r21"], x3T)

            def b_h3(i):
                pe.wait_ge(*ub.read(i, "r21"))
                from_rows(ub, i, ["h30", "h31"], n3row)

            def b_f1(i, chunks):
                pe.wait_ge(*ub.read(i, "h31"))
                for f in chunks:
                    dense(ub, i, f"f{f}", [(wf1[:, k, ck(f)], h3T[:, k, :]) for k in range(2)])

            def b_f2(i, c):
                pe.wait_ge(*ub.read(i, "f6"))
                ub.wait_free(pe, i, f"g{c}")
                for k in range(FC):
                    if k == FC - 1:
                        pe.wait_ge(*ub.read(i, "f7"))
                    last = mm(ub.bank(f"g{c}"), wf2[:, k, ck(c)], fT[:, k, :], start=(k == 0), stop=(k == FC - 1))
                ub.fill(last)

            def b_r3(i):
                pe.wait_ge(*ub.read(i, "g1"))
                to_rows(ub, i, ["r30", "r31"], x3T)

            def c_h4(i):
                pe.wait_ge(*ub.read(i, "r31"))
                from_rows(ub, i + 1, ["h40", "h41"], n4row)

            def c_lg(i):
                pe.wait_ge(sem("hf_ready"), i + 1)
                ub.wait_free(pe, i + 1, "lg")
                for n in range(TT):
                    for k in range(2):
                        last = mm(ub.bank("lg")[:, n * NE:(n + 1) * NE], hfT[:, k, n * P:(n + 1) * P], wrt[:, k, :],
                                  start=(k == 0), stop=(k == 1))
                ub.fill(last)
                to_rows(ub, i + 1, ["hr0", "hr1"], hfT)

            def c_rk(i):
                pe.wait_ge(sem("picked_ready"), i + 1)
                ub.wait_free(pe, i + 1, "rk")
                for n in range(TT + 1):
                    o = ub.bank("rk")[:, n * NE:(n + 1) * NE]
                    for m in range(min(n, TT)):
                        last = mm(o, ones[:, :], picked[:, m, :], start=(m == 0), stop=(m == min(n, TT) - 1 and n == TT))
                    if n < TT:
                        last = mm(o, upper[:, :], picked[:, n, :], start=(n == 0), stop=True)
                ub.fill(last)

            def c_ct(i):
                pe.wait_ge(sem("cmix_ready"), i + 1)
                ub.wait_free(pe, i + 1, "ct")
                for n in range(TT):
                    last = nc.tensor.transpose(ub.bank("ct")[0:NE, n * P:(n + 1) * P], cmix[:, n, :], ident[:, :])
                ub.fill(last)

            def c_b2(i):
                pe.wait_ge(*ub.read(i + 1, "ct"))
                for k in range(2):
                    ub.wait_free(pe, i + 1, f"b2{k}")
                    for h in range(2):
                        n = 2 * k + h
                        last = mm(ub.bank(f"b2{k}")[:, h * D:(h + 1) * D], ctT[:, n * P:(n + 1) * P], b2e[:, :],
                                  start=True, stop=True)
                    ub.fill(last)

            steps = {"A.xT": a_xT, "A.hid0": a_hid0, "A.hid1a": lambda i: a_hid1(i, (0, 1)), "A.hid1b": lambda i: a_hid1(i, (2, 3)), "A.sr2": a_sr2, "A.out": a_out, "A.r0": a_r0,
                     "A.x1": a_x1, "A.dn": a_dn, "A.ex": a_ex, "A.up": a_up, "A.r1": a_r1, "A.x2": a_x2, "A.q": a_q,
                     "A.k": a_k, "A.v0": lambda i: a_v(i, (0, 1)), "A.v1": lambda i: a_v(i, (2, 3)),
                     "B.s0": lambda i: b_s(i, 0), "B.s1": lambda i: b_s(i, 1), "B.p0": lambda i: b_p(i, 0),
                     "B.p1": lambda i: b_p(i, 1), "B.t0": lambda i: b_t(i, 0), "B.t1": lambda i: b_t(i, 1),
                     "B.o": b_o, "B.r2": b_r2, "B.h3": b_h3,
                     **{f"B.f1{n}": (lambda i, k=k: b_f1(i, (2 * k, 2 * k + 1))) for k, n in enumerate("abcd")},
                     "B.f2a": lambda i: b_f2(i, 0), "B.f2b": lambda i: b_f2(i, 1), "B.r3": b_r3, 
                     "C.h4": c_h4, "C.lg": c_lg, "C.rk": c_rk, "C.ct": c_ct, "C.b2": c_b2}

            def setup_cols():
                pe.wait_ge(sem("ident_ready"), 1)
                pe.wait_ge(sem("vec_loaded"), 16 * NVEC)
                nc.tensor.transpose(PB[:, 0, 0:P], vec, ident[:, :]).then_inc(sem("setup_filled"), 1)

            def setup_l1():
                pe.wait_ge(sem("l1_loaded"), 16 * 6)
                nc.tensor.transpose(PB[:, 1, 0:NE * FC], eb1r, ident[0:64, 0:64])
                for k in range(2):
                    nc.tensor.transpose(PB[:, 1, P + k * A1:P + (k + 1) * A1], downW[:, ck(k)], ident[0:64, 0:64])
                    nc.tensor.transpose(PB[0:A1, 1, (2 + k) * P:(3 + k) * P], upW[:, k, :], ident[:, :])\
                        .then_inc(sem("setup_filled"), 1)
                for e in range(ND):
                    last = nc.tensor.transpose(PB[0:A1, 2 + e // 8, (e % 8) * A1:(e % 8 + 1) * A1], expW[:, e, :],
                                               ident[0:64, 0:64])
                last.then_inc(sem("setup_filled"), 1)
                pe.wait_ge(sem("onehot_ready"), 1)
                pe.wait_ge(sem("setup_read"), 1)
                mm(PB[0:A1, 0, P:P + B], expb, sce[0:ND, 0, 0:B], start=True, stop=False)
                mm(PB[0:A1, 0, P:P + B], demb, sce[0:ND, 1, 0:B], start=False, stop=True).then_inc(sem("setup_filled"), 1)

            def setup_ada():
                pe.wait_ge(sem("tab_loaded"), 16 * 6)
                pe.wait_ge(sem("emb_ready"), 1)
                pe.wait_ge(sem("setup_read"), 4)
                for m in range(4):
                    for k in range(2):
                        last = mm(PB[:, 1, m * B:(m + 1) * B], wada[:, k, ck(m)], scr(2 + k), start=(k == 0), stop=(k == 1))
                last.then_inc(sem("setup_filled"), 1)

            def setup_sty(n):
                if n == 0:
                    mm(PB[0:SE, 2, 0:B], semb, sce[0:NSUB, 2, 0:B], start=True, stop=True).then_inc(sem("setup_filled"), 1)
                    return
                pe.wait_ge(sem("sty_step"), n)
                if n == 1:
                    last = mm(PB[:, 2, 0:B], hw1, scr(4)[0:SE, :], start=True, stop=True)
                if n == 2:
                    last = mm(PB[:, 2, 0:B], hw2, scr(5), start=True, stop=True)
                if n == 3:
                    last = mm(PB[0:SE, 2, 0:B], sw1, scr(6), start=True, stop=True)
                if n == 4:
                    for m in range(4):
                        last = mm(PB[:, 3, m * B:(m + 1) * B], sw2[:, ck(m)], scr(7)[0:SE, :], start=True, stop=True)
                last.then_inc(sem("setup_filled"), 1)

            setup = {"A.xT": setup_cols, "A.hid0": setup_l1, "A.sr2": setup_ada, "A.out": lambda: setup_sty(0),
                     "A.r0": lambda: setup_sty(1), "A.x1": lambda: setup_sty(2), "A.ex": lambda: setup_sty(3),
                     "A.up": lambda: setup_sty(4)}
            for s in ORDER:
                if s[0] == "A" and s in steps:
                    steps[s](0)
                    if s in setup:
                        setup[s]()
            pe.wait_ge(sem("setup_read"), 7)
            pe.wait_ge(sem("l3_loaded"), 32)
            rounds(steps, 1, "AB")
            rounds(steps, 2)
            with pe.Fori(3, NG) as i:
                rounds(steps, i)
            rounds(steps, NG, "BC")
            rounds(steps, NG + 1, "C")

            bank8 = lambda k: (PA if k < 4 else PB)[:, k % 4, :]

            def lay(t_, k):
                pe.wait_ge(sem(f"xs_loaded{k}"), 8 * (t_ - k) + 16)
                for c in range(DC):
                    last = nc.tensor.transpose(bank8(k)[:, ck(c)], xs[:, k, ck(c)], ident[:, :])
                last.then_inc(sem("xsT_filled"), 1)

            def up(t_, k, first=False):
                pe.wait_ge(sem("xsT_copied"), t_ + 1)
                pe.wait_ge(sem(f"w1_loaded{k}"), 8 * (t_ - k) + 16)
                for h in range(2):
                    if not first:
                        pe.wait_ge(sem(f"hid_done{h}"), t_ - 1)
                    for f in range(4 * h, 4 * h + 4):
                        for c in range(DC):
                            last = mm(bank8(2 + 2 * k + h)[:, ck(f % 4)], w1slot[k][:, c, ck(f)], xsT[:, k, ck(c)],
                                      start=(c == 0), stop=(c == 1))
                    last.then_inc(sem("g1_filled"), 1)

            def down(t_, k, first=False):
                e = pe.value_load(meta[0:1, 0, part(t_, 1)], min_val=0, max_val=NE - 1)
                if not first:
                    pe.wait_ge(sem("y_copied"), t_ - 1)
                for f in range(FC):
                    if f % 4 == 0:
                        pe.wait_ge(sem(f"hid_done{f // 4}"), t_ + 1)
                    last = mm(bank8(6 + k)[:, 0:D], hid[:, k, f, :],
                              w2all[:, bass.ds(e * FC + f, 1), :].rearrange("p a n -> p (a n)"),
                              start=(f == 0), stop=(f == FC - 1))
                last.then_inc(sem("y_filled"), 1)

            pe.wait_ge(*ub.read(NG, "b21"))
            pe.wait_ge(*ub.read(NG, "hr1"))
            pe.wait_ge(sem("plan_ready"), 1)
            pe.wait_ge(sem("w2_loaded"), 16 * NE)
            lay(0, 0)
            lay(1, 1)
            up(0, 0, True)
            up(1, 1, True)
            for t_ in range(2):
                if t_:
                    up(t_ + 1, 1 - t_)
                lay(t_ + 2, t_)
                down(t_, t_, True)
            with pe.Fori(1, (MT - 3) // 2) as j:
                for k in range(2):
                    up(2 * j + (k + 1), 1 - k)
                    lay(2 * j + (k + 2), k)
                    down(2 * j + k, k)
            for t_ in range(MT - 3, MT):
                if t_ + 1 < MT:
                    up(t_ + 1, (t_ + 1) % 2)
                if t_ + 2 < MT:
                    lay(t_ + 2, t_ % 2)
                down(t_, t_ % 2)

        @block.scalar
        def _(act):
            def acts(out, src, func, **kw):
                return nc.scalar.activation(out, src, func, **kw)

            for n, dst, name in W_A:
                act.dma_start(dst, kview(name)).then_inc(sem(f"{n}_loaded"), 16)

            def gelu(u, i, name, out, bias_col, func=ACT.Gelu, rows=P):
                act.wait_ge(*u.filled(i, name))
                u.done(acts(out, u.bank(name)[0:rows, :], func, bias=bias_col), name)

            def affine(u, i, name, out, g, b):
                act.wait_ge(*u.filled(i, name))
                u.done(acts(out, u.bank(name), ACT.Identity, bias=b, scale=g), name)

            def a_hid0(i):
                if isinstance(i, int):
                    act.wait_ge(sem("setup_read"), 1)
                for n, h, b in (("nr", hn, "L0_cond_b1_nr"), ("ts", ht, "L0_cond_b1_tsr")):
                    for c in range(2):
                        gelu(ua, i, f"{n}{c}", h[:, c, :], col(b, c))

            def a_hid1(i, chunks):
                for c in chunks:
                    gelu(ua, i, f"sr{c}", hs[:, c, :], col("L0_cond_b1_sr", c))

            def a_sr2(i):
                for c in range(2):
                    gelu(ua, i, f"su{c}", hs2[:, c, :], col("L0_cond_b2_sr", c))

            def a_x1(i):
                for c in range(2):
                    affine(ua, i, f"x1{c}", x1T[:, c, :], col("L0_cond_gamma", c), col("L0_cond_beta", c))

            def a_dn(i):
                gelu(ua, i, "dn", hd[:, :], col("L1_cond_down_b", parts=A1), rows=A1)

            def a_q(i):
                if isinstance(i, int):
                    act.wait_ge(sem("bq4_ready"), 1)
                for c in range(2):
                    act.wait_ge(*ua.filled(i, f"q{c}"))
                    ua.done(acts(qT[:, c, :], ua.bank(f"q{c}"), ACT.Identity, bias=bq4[:, c:c + 1], scale=HD ** -0.5), f"q{c}")

            def b_e(i, duo):
                for pr in range(2):
                    act.wait_ge(sem("centered"), half(i, duo, pr))
                    acts(sc[:, pr, :, :], sc[:, pr, :, :], ACT.Exp).then_inc(sem("exped"), 1)

            def b_t(i, duo):
                for k in (1, 3):
                    act.wait_ge(*ub.filled(i, f"pt{duo}{k}"))
                    ub.done(acts(pT[:, k, :], ub.bank(f"pt{duo}{k}"), ACT.Copy), f"pt{duo}{k}")

            def b_p(i, duo):
                act.wait_ge(*ub.filled(i, f"cx{duo}"))
                ub.done(acts(ctxT[:, :, duo * D:(duo + 1) * D], ub.bank(f"cx{duo}").rearrange("p (c n) -> p c n", c=2),
                             ACT.Copy), f"cx{duo}")

            def b_h3(i):
                for c in range(2):
                    affine(ub, i, f"h3{c}", h3T[:, c, :], col("L2_cond_g2", c), col("L2_cond_beta2", c))

            def b_f1(i, chunks):
                for f in chunks:
                    gelu(ub, i, f"f{f}", fT[:, f, :], col("L2_cond_b1", f), ACT.Gelu_apprx_sigmoid)

            def c_h4(i):
                for c in range(2):
                    affine(ub, i + 1, f"h4{c}", h4T[:, c, :], col("L3_cond_ln_g", c), col("L3_cond_ln_b", c))

            def c_lg(i):
                if not (isinstance(i, int) and i == 0):
                    act.wait_ge(sem("scattered"), 16 * TT * TOPK * i)
                for n in range(2):
                    act.wait_ge(*ub.filled(i + 1, f"hr{n}"))
                    for k in range(TOPK):
                        last = acts(hrow[:, 2 * n:2 * n + 2, k, 0:D], ub.bank(f"hr{n}").rearrange("p (a d) -> p a d", a=2),
                                    ACT.Copy)
                    ub.done(last, f"hr{n}")

            def c_ge(i):
                act.wait_ge(sem("gate_diff"), i + 1)
                acts(ge[:, :], gd[:, :], ACT.Exp).then_inc(sem("gate_exp"), 1)

            steps = {"A.hid0": a_hid0, "A.hid1a": lambda i: a_hid1(i, (0, 1)), "A.hid1b": lambda i: a_hid1(i, (2, 3)), "A.sr2": a_sr2, "A.x1": a_x1, "A.dn": a_dn, "A.q": a_q,
                     "B.e0": lambda i: b_e(i, 0), "B.e1": lambda i: b_e(i, 1), "B.p0": lambda i: b_p(i, 0),
                     "B.p1": lambda i: b_p(i, 1), "B.t0": lambda i: b_t(i, 0), "B.t1": lambda i: b_t(i, 1), "B.h3": b_h3, 
                     **{f"B.f1{n}": (lambda i, k=k: b_f1(i, (2 * k, 2 * k + 1))) for k, n in enumerate("abcd")}, "C.h4": c_h4, "C.lg": c_lg, "C.ge": c_ge}

            def setup_ada():
                act.wait_ge(sem("angle_ready"), 1)
                acts(scr(8, 2 * B), scr(0, 2 * B), ACT.Sin).then_inc(sem("sin_done"), 1)
                act.wait_ge(sem("sin_done"), 1)
                acts(scr(10, 2 * B), scr(8, 2 * B), ACT.Exp, scale=-1.0).then_inc(sem("silu_exp"), 1)

            def setup_sty():
                act.wait_ge(sem("abs_ready"), 1)
                acts(scr(12, 2 * B), scr(12, 2 * B), ACT.Exp, scale=-1.0).then_inc(sem("sp_exp"), 1)
                act.wait_ge(sem("sp_exp"), 1)
                acts(scr(14, 2 * B), scr(12, 2 * B), ACT.Ln, bias=1.0).then_inc(sem("sp_ln"), 1)

            setup = {"A.sr2": setup_ada, "A.v1": setup_sty}
            for s in ORDER:
                if s in steps and s[0] == "A":
                    steps[s](0)
                if s in setup:
                    setup[s]()
            rounds(steps, 1, "AB")
            rounds(steps, 2)
            with act.Fori(3, NG) as i:
                rounds(steps, i)
            rounds(steps, NG, "BC")
            rounds(steps, NG + 1, "C")

            bank8 = lambda k: (PA if k < 4 else PB)[:, k % 4, :]

            def relu(t_, k, first=False):
                act.wait_ge(sem("b1_ready"), t_ + 1)
                if not first:
                    act.wait_ge(sem("y_filled"), t_ - 1)
                for h in range(2):
                    act.wait_ge(sem("g1_filled"), 2 * t_ + (h + 1))
                    for f in range(4 * h, 4 * h + 4):
                        last = acts(hid[:, k, f, :], bank8(2 + 2 * k + h)[:, (f % 4) * P:(f % 4 + 1) * P], ACT.Relu,
                                    bias=b1c[:, k, f:f + 1])
                    last.then_inc(sem(f"hid_done{h}"), 1)

            relu(0, 0, True)
            relu(1, 1, True)
            with act.Fori(1, (MT - 1) // 2) as j:
                for k in range(2):
                    relu(2 * j + k, k)
            relu(MT - 1, 0)
            for k in range(2):
                act.wait_ge(*added(k))
            copy_out(act, range(4, 8))

        @block.vector
        def _(v):
            ts, tt, stt, cp = v.tensor_scalar, v.tensor_tensor, v.scalar_tensor_tensor, v.tensor_copy

            once = [0]

            def link(ins):
                once[0] += 1
                ins.then_inc(sem("dve_setup"), 1)
                v.wait_ge(sem("dve_setup"), once[0])

            def after(ins, name, value):
                ins.then_inc(sem(name), 1)
                wait_apart(v, sem(name), value)

            def stats(i, s, srcs, tag, eps, wait=None):
                for n in range(TT):
                    if wait:
                        wait(n)
                    last = v.bn_stats(st[s][:, n, :], srcs[n])
                after(last, f"{tag}_stats", i + 1)
                for n in range(TT):
                    last = v.bn_aggr(mv[s][:, n, :], st[s][:, n, :])
                after(last, f"{tag}_aggr", i + 1)
                ts(ve[s][:, :], mv[s][:, :, 1], eps, None, ALU.add).then_inc(sem(f"{tag}_var"), 1)

            def normalise(i, u, units, s, tag, out, eps, before=None):
                srcs = [u.bank(units[n // 2])[:, (n % 2) * D:(n % 2 + 1) * D] for n in range(TT)]

                def wait(n):
                    if n % 2 == 0:
                        v.wait_ge(*u.filled(i, units[n // 2]))
                stats(i, s, srcs, tag, eps, wait)
                if before:
                    before()
                v.wait_ge(sem(f"{tag}_rstd"), i + 1)
                for n in range(TT):
                    last = ts(out[:, n, :], srcs[n], mv[s][:, n, 0:1], rs[s][:, n:n + 1], ALU.subtract, ALU.mult)
                    if n % 2:
                        u.done(last, units[n // 2])

            def a_xT(i):
                for c in range(2):
                    v.wait_ge(*ua.filled(i, f"xT{c}"))
                    ua.done(cp(xT[:, c, :], ua.bank(f"xT{c}")), f"xT{c}")

            def a_out(i):
                v.wait_ge(sem("xb_ready"), i + 1)
                for c in range(2):
                    v.wait_ge(*ua.filled(i, f"y{c}"))
                    ua.done(tt(xT[:, c, :], ua.bank(f"y{c}"), xb[:, c, :], ALU.add), f"y{c}")

            def a_r0(i):
                normalise(i, ua, ["r00", "r01"], "A", "l0", nrow, EPS)

            def a_ex(i):
                v.wait_ge(*ua.filled(i, "ex"))
                ua.done(tt(by_seq(he[:, :]), by_seq(ua.bank("ex")[0:A1, :]), over_tokens(bsel1[:, part(i, GB)]), ALU.add), "ex")

            def a_up(i):
                for c in range(2):
                    v.wait_ge(*ua.filled(i, f"u{c}"))
                    ua.done(stt(x1T[:, c, :], ua.bank(f"u{c}"), col("L1_cond_up_b", c), x1T[:, c, :], ALU.add, ALU.add), f"u{c}")

            def a_r1(i):
                normalise(i, ua, ["r10", "r11"], "A", "l1", nrow, EPS)
                v.wait_ge(sem("x2_ready"), i + 1)
                stats(i, "A", [x2row[:, n, :] for n in range(TT)], "l2", EPS)
                v.wait_ge(sem("l2_rstd"), i + 1)
                for n in range(TT):
                    last = ts(nrow[:, n, :], x2row[:, n, :], mv["A"][:, n, 0:1], rs["A"][:, n:n + 1], ALU.subtract, ALU.mult)
                last.then_inc(sem("n2_ready"), 1)

            def a_x2(i):
                for c in range(2):
                    v.wait_ge(*ua.filled(i, f"x2{c}"))
                    ua.done(tt(by_seq(xmT[:, c, :]), by_seq(ua.bank(f"x2{c}")), over_tokens(ada[:, c, part(i, GB)]), ALU.mult), f"x2{c}")
                for c in range(2):
                    v.wait_ge(*ua.read(i, f"x2{c}"))
                    last = tt(by_seq(xmT[:, c, :]), by_seq(xmT[:, c, :]), over_tokens(ada[:, 2 + c, part(i, GB)]), ALU.add)
                last.then_inc(sem("xm_ready"), 1)

            def a_k(i):
                for c in range(2):
                    v.wait_ge(*ua.filled(i, f"k{c}"))
                    src = by_seq(ua.bank(f"k{c}"))
                    for j in range(2):
                        last = ts(kbd[:, c, :, j, :], src, col("L2_cond_bk", c), head_half[:, j:j + 1], ALU.add, ALU.mult)
                    ua.done(last, f"k{c}")

            def a_v(i, units):
                for n in units:
                    v.wait_ge(*ua.filled(i, f"v{n}"))
                    for j in range(2):
                        rows = slice(j * S, (j + 1) * S)
                        src = ua.bank(f"v{n}")[rows, :].rearrange("p (b a j d) -> p b a j d", b=2, j=2, d=HD)[:, :, :, j, :]
                        bv = bvrow[rows, :].rearrange("p (a j d) -> p a j d", j=2, d=HD)[:, :, j, :]
                        b0, b1 = (b + j for b in v_seqs(n))
                        if b1 < GB:
                            last = tt(vbd[rows, b0:b1 + 1:2, :, j * HD:(j + 1) * HD], src,
                                      bv.unsqueeze(1).broadcast_to([S, 2, H // 2, HD]), ALU.add)
                        else:
                            for h, b in enumerate((b0, 0)):
                                last = tt(vbd[rows, b, :, j * HD:(j + 1) * HD], src[:, h], bv, ALU.add)
                    ua.done(last, f"v{n}")

            def b_s(i, duo):
                v.wait_ge(sem("bias_masked"), 2 * i + (duo + 1))
                v.wait_ge(*ub.filled(i, f"sc{duo}"))
                nat = lambda a: a.rearrange("p (c r j) k -> p r c (j k)", c=2, r=4)
                for pr in range(2):
                    last = tt(nat(sc[:, pr, :, :]), PB[:, :, pr * D:(pr + 1) * D].rearrange("p r (c x) -> p r c x", c=2),
                              nat(bias[:, duo, pr, :, :]), ALU.add)
                    if pr == 0:
                        last.then_inc(sem("half_added"), 1)
                ub.done(last, f"sc{duo}")
                v.wait_ge(sem("half_added"), 2 * i + (duo + 1))
                v.reduce_max(smx[:, 0, :], sc[:, 0, :, :], axis=AX.X).then_inc(sem("scored"), 1)
                v.wait_ge(*ub.read(i, f"sc{duo}"))
                v.reduce_max(smx[:, 1, :], sc[:, 1, :, :], axis=AX.X).then_inc(sem("scored"), 1)

            def b_m(i, duo):
                for pr in range(2):
                    v.wait_ge(sem("exped"), half(i, duo, pr))
                    v.reduce_sum(ssum[:, pr, :], sc[:, pr, :, :], axis=AX.X).then_inc(sem("summed"), 1)
                for pr in range(2):
                    wait_apart(v, sem("summed"), half(i, duo, pr))
                    v.reciprocal(rsum[:, pr, :], ssum[:, pr, :]).then_inc(sem("rsum_ready"), 1)

            def b_t(i, duo):
                for k in (0, 2):
                    v.wait_ge(*ub.filled(i, f"pt{duo}{k}"))
                    ub.done(cp(pT[:, k, :], ub.bank(f"pt{duo}{k}")), f"pt{duo}{k}")

            def b_o(i):
                for c in range(2):
                    v.wait_ge(*ub.filled(i, f"o{c}"))
                    ub.done(stt(x3T[:, c, :], ub.bank(f"o{c}"), col("L2_cond_bo", c), xmT[:, c, :], ALU.add, ALU.add), f"o{c}")

            def b_r2(i):
                normalise(i, ub, ["r20", "r21"], "B", "l3", n3row, EPS)

            def b_f2(i, c):
                v.wait_ge(*ub.filled(i, f"g{c}"))
                ub.done(stt(x3T[:, c, :], ub.bank(f"g{c}"), col("L2_cond_b2", c), x3T[:, c, :], ALU.add, ALU.add), f"g{c}")

            def b_r3(i):
                def keep():
                    if not (isinstance(i, int) and i == 0):
                        wait_apart(v, sem("x_stored"), 16 * i)
                    for k in range(2):
                        last = cp(xres[:, 2 * k:2 * k + 2, :], ub.bank(f"r3{k}").rearrange("p (a d) -> p a d", a=2))
                    last.then_inc(sem("xres_ready"), 1)
                normalise(i, ub, ["r30", "r31"], "B", "l4", n4row, EPS, keep)

            def c_tok(i):
                for c in range(2):
                    v.wait_ge(*ub.read(i + 1, f"h4{c}"))
                    for b in range(GB):
                        last = v.bn_stats(st4[:, c, b, :], h4T[:, c, b * S:(b + 1) * S])
                after(last, "t_stats", i + 1)
                f = lambda k: st4[:, :, :, k]
                tt(tst["sum"][:, :, :], f(1), f(4), ALU.add)
                tt(tst["dif"][:, :, :], f(1), f(4), ALU.subtract)
                after(tt(tst["var"][:, :, :], f(2), f(5), ALU.add), "t_halves", i + 1)
                tt(tst["sq"][:, :, :], tst["dif"][:, :, :], tst["dif"][:, :, :], ALU.mult)
                after(ts(tst["var"][:, :, :], tst["var"][:, :, :], 1.0 / S, EPS_T, ALU.mult, ALU.add), "t_within", i + 1)
                stt(tst["var"][:, :, :], tst["sq"][:, :, :], 0.25, tst["var"][:, :, :], ALU.mult, ALU.add)\
                    .then_inc(sem("t_var"), 1)

            def c_hf(i):
                v.wait_ge(sem("t_rstd"), i + 1)
                after(tt(tst["mul"][:, :, :], tst["rstd"][:, :, :], sty[:, 0:2, part(i, GB)], ALU.mult), "t_mul", i + 1)
                after(stt(tst["mm"][:, :, :], tst["sum"][:, :, :], 0.5, tst["mul"][:, :, :], ALU.mult, ALU.mult), "t_mm", i + 1)
                tt(tst["add"][:, :, :], sty[:, 2:4, part(i, GB)], tst["mm"][:, :, :], ALU.subtract)
                for c in range(2):
                    last = tt(by_seq(hfT[:, c, :]), by_seq(h4T[:, c, :]), over_tokens(tst["mul"][:, c, :]), ALU.mult)
                after(last, "t_scaled", i + 1)
                for c in range(2):
                    last = tt(by_seq(hfT[:, c, :]), by_seq(hfT[:, c, :]), over_tokens(tst["add"][:, c, :]), ALU.add)
                last.then_inc(sem("hf_ready"), 1)

            def c_lg(i):
                v.wait_ge(*ub.filled(i + 1, "lg"))
                ub.done(cp(lgs[:, :, :], ub.bank("lg")[:, 0:TT * NE].rearrange("p (n e) -> p n e", e=NE)), "lg")
                wait_apart(v, *ub.read(i + 1, "lg"))
                for n in range(TT):
                    last = v.max(mx8[:, n, :], lgs[:, n, :])
                after(last, "top_values", i + 1)
                for n in range(TT):
                    last = v.max_index(mi8[:, n, :], mx8[:, n, :], lgs[:, n, :])
                tt(gd[:, :], mx8[:, :, 1], mx8[:, :, 0], ALU.subtract).then_inc(sem("gate_diff"), 1)
                v.wait_ge(sem("gate_diff"), i + 1)
                after(cp(mif[:, :, :], mi8[:, :, 0:TOPK]), "top_index", i + 1)
                for k in range(TOPK):
                    last = tt(oh[:, k, :, :], iot[:, 0, 0:NE].unsqueeze(1).broadcast_to([P, TT, NE]),
                              mif[:, :, k:k + 1].broadcast_to([P, TT, NE]), ALU.is_equal)
                after(last, "onehots", i + 1)
                tt(picked[:, :, :], oh[:, 0, :, :], oh[:, 1, :, :], ALU.add).then_inc(sem("picked_ready"), 1)

            def c_ge(i):
                wait_apart(v, sem("gate_exp"), i + 1)
                after(ts(gp[:, :], ge[:, :], 1.0, None, ALU.add), "gate_sum", i + 1)
                after(v.reciprocal(gp[:, :], gp[:, :]), "gate_recip", i + 1)
                after(tt(gd[:, :], gp[:, :], ge[:, :], ALU.mult), "gate_second", i + 1)
                if not (isinstance(i, int) and i == 0):
                    wait_apart(v, sem("scattered"), 16 * TT * TOPK * i)
                for k, a in enumerate((gp, gd)):
                    cp(hrow[:, :, k, D:D + 1], tok[:, :].unsqueeze(2))
                    cp(hrow[:, :, k, D + 1:DX], a[:, :].unsqueeze(2))
                after(ts(tok[:, :], tok[:, :], float(GT), None, ALU.add), "tok_moved", i + 1)
                for k, a in enumerate((gp, gd)):
                    last = tt(cm[:, k, :, :], oh[:, k, :, :], a[:, :].unsqueeze(2).broadcast_to([P, TT, NE]), ALU.mult)
                after(last, "gates_placed", i + 1)
                tt(cmix[:, :, :], cm[:, 0, :, :], cm[:, 1, :, :], ALU.add).then_inc(sem("cmix_ready"), 1)

            def c_rk(i):
                v.wait_ge(*ub.filled(i + 1, "rk"))
                bank = ub.bank("rk")
                last = tt(pos[:, :, :], bank[:, 0:TT * NE].rearrange("p (n e) -> p n e", e=NE),
                          base[:, :].unsqueeze(1).broadcast_to([P, TT, NE]), ALU.add)
                after(last, "ranked", i + 1)
                ub.done(tt(base[:, :], bank[:, TT * NE:(TT + 1) * NE], base[:, :], ALU.add), "rk")
                for k in range(TOPK):
                    last = tt(posk[:, k, :, :], oh[:, k, :, :], pos[:, :, :], ALU.mult)
                after(last, "rank_picked", i + 1)
                for k in range(TOPK):
                    last = v.reduce_sum(slot[:, :, k], posk[:, k, :, :], axis=AX.X)
                after(last, "slots", i + 1)
                if not (isinstance(i, int) and i == 0):
                    wait_apart(v, sem("scattered"), 16 * TT * TOPK * i)
                cp(idx[:, :, :], slot[:, :, :]).then_inc(sem("idx_ready"), 1)

            def c_ct(i):
                v.wait_ge(*ub.filled(i + 1, "ct"))
                ub.done(cp(ctT, ub.bank("ct")[0:NE, :]), "ct")

            def c_b2(i):
                v.wait_ge(sem("xres_ready"), i + 1)
                for k in range(2):
                    v.wait_ge(*ub.filled(i + 1, f"b2{k}"))
                    x = xres[:, 2 * k:2 * k + 2, :]
                    ub.done(tt(x, ub.bank(f"b2{k}").rearrange("p (a d) -> p a d", a=2), x, ALU.add), f"b2{k}")

            steps = {"A.xT": a_xT, "A.out": a_out, "A.r0": a_r0, "A.ex": a_ex, "A.up": a_up, "A.r1": a_r1, "A.x2": a_x2,
                     "A.k": a_k, "A.v0": lambda i: a_v(i, (0, 1)), "A.v1": lambda i: a_v(i, (2, 3)),
                     "B.s0": lambda i: b_s(i, 0), "B.s1": lambda i: b_s(i, 1), "B.m0": lambda i: b_m(i, 0),
                     "B.m1": lambda i: b_m(i, 1), "B.t0": lambda i: b_t(i, 0), "B.t1": lambda i: b_t(i, 1), "B.o": b_o,
                     "B.r2": b_r2, "B.f2a": lambda i: b_f2(i, 0), "B.f2b": lambda i: b_f2(i, 1), "B.r3": b_r3, 
                     "C.tok": c_tok, "C.hf": c_hf, "C.lg": c_lg, "C.ge": c_ge, "C.rk": c_rk, "C.ct": c_ct, "C.b2": c_b2}

            v.memset(vec, 0.0).then_inc(sem("vec_cleared"), 1)
            v.memset(mhalf[:, :], -0.5).then_inc(sem("mhalf_ready"), 1)
            v.memset(ones[:, :], 1.0)
            v.memset(vbd, 0.0)
            v.wait_ge(sem("iota_ready"), 1)
            cp(pidx[:, :], pidx_i[:, 0:1])
            link(ts(pidx_i[:, 1:2], pidx_i[:, 0:1], 4, 1, ALU.logical_shift_right, ALU.bitwise_and))
            link(cp(head_half[:, 1:2], pidx_i[:, 1:2]))
            link(ts(head_half[:, 0:1], head_half[:, 1:2], -1.0, 1.0, ALU.mult, ALU.add))
            v.wait_ge(sem("ints_loaded"), 64)
            ts(eoff[:, :], iot[:, 0, 0:NE], float(CAP), None, ALU.mult)
            ts(base[:, :], iot[:, 0, 0:NE], float(CAP), None, ALU.mult)
            ts(tok[:, :], iot[:, 0, 0:TT], float(P), pidx[:, 0:1], ALU.mult, ALU.add)
            link(cp(idf[:, :, :], ints[:, :, :]))
            for k in range(3):
                last = ts(mcond[:, k, :], idf[:, 0, :], float(k), None, ALU.is_equal)
            last.then_inc(sem("mcond_ready"), 1)
            v.wait_ge(sem("mcond_ready"), 1)
            v.wait_ge(sem("setup_filled"), 1)
            cp(colv[:, :], PB[:, 0, 0:NROWS]).then_inc(sem("setup_read"), 1)
            v.wait_ge(sem("setup_read"), 1)
            ts(bq4[:, :], colv[:, ROW["L2_cond_bq"]:ROW["L2_cond_bq"] + 2], HD ** -0.5, None, ALU.mult).then_inc(sem("bq4_ready"), 1)
            for c in range(2):
                last = ts(bsel0[:, c, :], mcond[:, 0, :], col("L0_cond_b2_nr", c), None, ALU.mult)
            link(last)
            for k, name in ((1, "L0_cond_b2_tsr"), (2, "L0_cond_b3_sr")):
                for c in range(2):
                    last = stt(bsel0[:, c, :], mcond[:, k, :], col(name, c), bsel0[:, c, :], ALU.mult, ALU.add)
                last.then_inc(sem("bsel0_ready"), 1)
                v.wait_ge(sem("bsel0_ready"), k)

            def setup_l1():
                clip = scr(16)
                ts(clip, idf[:, 1, :], 0.0, float(ND - 1), ALU.max, ALU.min)
                link(ts(scr(17), idf[:, 3, :], 0.0, float(NSUB - 1), ALU.max, ALU.min))
                ts(sce[:, 0, 0:B], idf[:, 1, :], pidx[:, 0:1], None, ALU.is_equal)
                ts(sce[:, 1, 0:B], clip, pidx[:, 0:1], None, ALU.is_equal)
                ts(sce[:, 2, 0:B], scr(17), pidx[:, 0:1], None, ALU.is_equal).then_inc(sem("onehot_ready"), 1)
                link(tt(scr(18), clip, idf[:, 1, :], ALU.is_equal))
                link(ts(scr(19), clip, -float(ND), None, ALU.add))
                link(tt(scr(18), scr(18), scr(19), ALU.mult))
                link(ts(scr(18), scr(18), float(ND), None, ALU.add))
                cp(widx[:, :], scr(18)[0:1, :]).then_inc(sem("widx_ready"), 1)
                v.wait_ge(sem("setup_filled"), 3)
                cp(eb1[:, :], PB[:, 1, 0:NE * FC])
                cp(downT[:, :, :], PB[:, 1, P:2 * P].rearrange("p (k a) -> p k a", k=2))
                cp(upT[:, :], PB[0:A1, 1, 2 * P:4 * P]).then_inc(sem("setup_read"), 1)
                v.wait_ge(sem("setup_filled"), 4)
                cp(expT[:, 0:ND, :], PB[0:A1, 2:4, :].rearrange("p a (b c) -> p (a b) c", c=A1))
                cp(expT[:, ND, :], ident[0:A1, 0:A1]).then_inc(sem("setup_read"), 1)
                v.wait_ge(sem("setup_filled"), 5)
                cp(bsel1[:, :], PB[0:A1, 0, P:P + B]).then_inc(sem("setup_read"), 1)

            def setup_angles():
                link(ts(scr(20), idf[:, 2, :], 0.01, 4000.0, ALU.mult, ALU.mult))
                link(ts(scr(21), scr(20), col("freqs"), None, ALU.mult))
                ts(scr(22), scr(21), INV2PI, MAGIC, ALU.mult, ALU.add)
                link(ts(scr(23), scr(21), INV2PI, 0.25, ALU.mult, ALU.add))
                link(ts(scr(23), scr(23), MAGIC, None, ALU.add))
                link(ts(scr(22, 2 * B), scr(22, 2 * B), MAGIC, None, ALU.subtract))
                both = lambda k: scr(k, 2 * B).rearrange("p (a b) -> p a b", a=2)
                two = scr(21).unsqueeze(1).broadcast_to([P, 2, B])
                link(stt(both(0), both(22), -C1, two, ALU.mult, ALU.add))
                link(stt(both(0), both(22), -C2, both(0), ALU.mult, ALU.add))
                link(ts(scr(1), scr(1), PI / 2, None, ALU.add))
                link(stt(both(0), both(22), -C3, both(0), ALU.mult, ALU.add))
                ts(scr(0, 2 * B), scr(0, 2 * B), -3.1415925, 3.1415925, ALU.max, ALU.min).then_inc(sem("angle_ready"), 1)
                v.wait_ge(sem("mask_loaded"), 32)
                ts(mneg[:, :, :], mask8[:, :, :], NEG, None, ALU.mult).then_inc(sem("mneg_ready"), 1)

            def setup_ada():
                v.wait_ge(sem("silu_exp"), 1)
                link(ts(scr(10, 2 * B), scr(10, 2 * B), 1.0, None, ALU.add))
                link(v.reciprocal(scr(10, 2 * B), scr(10, 2 * B)))
                tt(scr(2, 2 * B), scr(8, 2 * B), scr(10, 2 * B), ALU.mult).then_inc(sem("emb_ready"), 1)
                v.wait_ge(sem("setup_filled"), 6)
                for m in range(4):
                    last = ts(ada[:, m, :], PB[:, 1, m * B:(m + 1) * B], col("L2_cond_b_ada", m), 1.0 if m < 2 else 0.0,
                              ALU.add, ALU.add)
                last.then_inc(sem("setup_read"), 1)

            def setup_sty(n):
                v.wait_ge(sem("setup_filled"), 7 + n)
                if n == 0:
                    last = cp(scr(4)[0:SE, :], PB[0:SE, 2, 0:B])
                if n == 1:
                    last = ts(scr(5), PB[:, 2, 0:B], col("L3_cond_hyp_b1"), 0.0, ALU.add, ALU.max)
                if n == 2:
                    last = ts(scr(6), PB[:, 2, 0:B], col("L3_cond_hyp_b2"), None, ALU.add)
                if n == 3:
                    last = ts(scr(7)[0:SE, :], PB[0:SE, 2, 0:B], col("L3_cond_sty_b1", parts=SE), 0.0, ALU.add, ALU.max)
                if n < 4:
                    last.then_inc(sem("sty_step"), 1)
                    return
                for m in range(4):
                    last = ts(sty[:, m, :], PB[:, 3, m * B:(m + 1) * B], col("L3_cond_sty_b2", m), None, ALU.add)
                last.then_inc(sem("setup_read"), 1)
                v.wait_ge(sem("setup_read"), 6)
                g = sty[:, 0:2, :].rearrange("p a b -> p (a b)")
                link(ts(scr(12, 2 * B), g, -1.0, None, ALU.mult))
                tt(scr(12, 2 * B), scr(12, 2 * B), g, ALU.max).then_inc(sem("abs_ready"), 1)
                v.wait_ge(sem("sp_ln"), 1)
                link(stt(g, g, 0.0, scr(14, 2 * B), ALU.max, ALU.add))
                ts(g, g, 1e-8, None, ALU.add).then_inc(sem("setup_read"), 1)
                v.wait_ge(sem("setup_read"), 7)

            setup = {"A.xT": setup_l1, "A.hid0": setup_angles, "A.sr2": setup_ada, "A.out": lambda: setup_sty(0),
                     "A.r0": lambda: setup_sty(1), "A.x1": lambda: setup_sty(2), "A.ex": lambda: setup_sty(3),
                     "A.v1": lambda: setup_sty(4)}
            v.wait_ge(sem("ident_ready"), 1)
            for s in ORDER:
                if s in steps and s[0] == "A":
                    if s == "A.ex" or s == "A.v0":
                        v.wait_ge(sem("rows_loaded"), 48)
                    steps[s](0)
                if s in setup:
                    setup[s]()
            rounds(steps, 1, "AB")
            rounds(steps, 2)
            with v.Fori(3, NG) as i:
                rounds(steps, i)
            rounds(steps, NG, "BC")
            rounds(steps, NG + 1, "C")

            v.wait_ge(*ub.read(NG, "rk"))
            link(v.memset(zrow, 0.0))
            ts(zrow[:, D:D + 1], pidx[:, 0:1], float(B * S), None, ALU.add).then_inc(sem("zrow_ready"), 1)
            link(tt(cnt[:, :], base[:, :], eoff[:, :], ALU.subtract))
            link(ts(padp[:, :], base[:, :], pidx[:, 0:1], None, ALU.add))
            cp(padu[:, :], padp[:, :]).then_inc(sem("pads_ready"), 1)
            n8, incl = pl8["n"][:, :], pl8["incl"][:, :]
            v.memset(pl8["one"][:, :], 1.0)
            link(ts(n8, cnt[:, :], float(P - 1), 1.0 / P, ALU.add, ALU.mult))
            link(ts(n8, n8, -255.0 / 512, MAGIC, ALU.add, ALU.add))
            link(ts(n8, n8, MAGIC, None, ALU.subtract))
            link(v.tensor_tensor_scan(incl, pl8["one"][:, :], n8, 0.0, ALU.mult, ALU.add))
            tile = iot[:, 0, :]
            e, start, idle, src = (plan[k] for k in ("e", "start", "idle", "src"))
            seven = lambda a: a[:, 0:NE - 1].unsqueeze(1).broadcast_to([P, MTP, NE - 1])
            ge7 = pge[:, :, 0:NE - 1]
            link(tt(ge7, tile.unsqueeze(2).broadcast_to([P, MTP, NE - 1]), seven(pl8["incl"][:, :]), ALU.is_ge))
            link(v.reduce_sum(e, ge7, axis=AX.X))
            link(tt(ge7, ge7, seven(pl8["n"][:, :]), ALU.mult))
            link(v.reduce_sum(start, ge7, axis=AX.X))
            link(tt(start, tile, start, ALU.subtract))
            link(ts(src, e, float(CAP), None, ALU.mult))
            link(stt(src, start, float(P), src, ALU.mult, ALU.add))
            link(ts(idle, tile, pl8["incl"][:, NE - 1:NE], None, ALU.is_ge))
            link(stt(idle, src, base[:, NE - 1:NE], idle, ALU.subtract, ALU.mult))
            link(tt(src, src, idle, ALU.subtract))
            cp(meta[:, 0, :], e)
            cp(meta[:, 1, :], src).then_inc(sem("plan_ready"), 1)

            bank8 = lambda k: (PA if k < 4 else PB)[:, k % 4, :]

            def turn(t_, k, first=False):
                v.wait_ge(sem("xsT_filled"), t_ + 1)
                if not first:
                    v.wait_ge(sem("g1_filled"), 2 * (t_ - 1))
                cp(xsT[:, k, :], bank8(k)[:, 0:D]).then_inc(sem("xsT_copied"), 1)
                cp(info[:, part(t_, 1), :], xs[:, k:k + 1, D:DX]).then_inc(sem("info_kept"), 1)

            def take(t_, k, first=False):
                wait_apart(v, sem("y_filled"), t_ + 1)
                if not first:
                    v.wait_ge(sem(f"added{k}"), 8 * (t_ - k))
                v.wait_ge(sem("info_kept"), t_ + 1)
                ts(ys[:, k, :], bank8(6 + k)[:, 0:D], info[:, part(t_, 1), 1:2].rearrange("p a b -> p (a b)"), None, ALU.mult)\
                    .then_inc(sem("y_copied"), 1)

            turn(0, 0, True)
            turn(1, 1, True)
            for t_ in range(2):
                turn(t_ + 2, t_)
                take(t_, t_, True)
            with v.Fori(1, (MT - 3) // 2) as j:
                for k in range(2):
                    turn(2 * j + (k + 2), k)
                    take(2 * j + k, k)
            turn(MT - 1, 0)
            for t_ in range(MT - 3, MT):
                take(t_, t_ % 2)

        @block.gpsimd
        def _(g):
            g.memset(ident[:, :], 0.0).then_inc(sem("pool_setup"), 1)
            g.memset(upper[:, :], 1.0).then_inc(sem("pool_setup"), 1)
            g.wait_ge(sem("pool_setup"), 2)
            g.affine_select(out=ident[:, :], in_=ident[:, :], compare_op=ALU.not_equal, fill=1.0, base=0,
                            pattern=[[-1, P]], channel_multiplier=1).then_inc(sem("ident_ready"), 1)
            g.affine_select(out=upper[:, :], in_=upper[:, :], compare_op=ALU.is_gt, fill=0.0, base=0,
                            pattern=[[1, P]], channel_multiplier=-1).then_inc(sem("upper_ready"), 1)
            g.iota(pidx_i[:, 0:1], [[1, 1]], base=0, channel_multiplier=1)
            g.iota(iot[:, 0, :], [[1, MTP]], base=0, channel_multiplier=0, allow_small_or_imprecise_dtypes=True)\
                .then_inc(sem("iota_ready"), 1)

            def rstd(s, i, tag):
                g.wait_ge(sem(f"{tag}_var"), i + 1)
                g.tensor_tensor(rs[s][:, :], ve[s][:, :], mhalf[:, 0:TT], ALU.pow).then_inc(sem(f"{tag}_rstd"), 1)

            def masked(i, ap, k):
                return g.tensor_tensor(by_seq(ap), by_seq(ap), over_tokens(mcond[:, k, part(i, GB)]), ALU.mult)

            def a_xb(i):
                if isinstance(i, int):
                    g.wait_ge(sem("bsel0_ready"), 2)
                wait_apart(g, *ua.read(i, "xT1"))
                for c in range(2):
                    last = g.tensor_tensor(by_seq(xb[:, c, :]), by_seq(xT[:, c, :]), over_tokens(bsel0[:, c, part(i, GB)]), ALU.add)
                last.then_inc(sem("xb_ready"), 1)

            def a_mask0(i):
                for name, h, k in (("nr", hn, 0), ("ts", ht, 1)):
                    for c in range(2):
                        wait_apart(g, *ua.read(i, f"{name}{c}"))
                        last = masked(i, h[:, c, :], k)
                last.then_inc(sem("hidden_masked"), 1)

            def a_mask1(i):
                for c in range(2):
                    wait_apart(g, *ua.read(i, f"su{c}"))
                    last = masked(i, hs2[:, c, :], 2)
                last.then_inc(sem("hidden_masked"), 1)

            def a_wsel(i):
                if isinstance(i, int):
                    g.wait_ge(sem("widx_ready"), 1)
                    g.wait_ge(sem("setup_read"), 3)
                else:
                    g.wait_ge(*ua.filled(i - 1, "ex"))
                for b in range(GB):
                    e = g.value_load(widx[0:1, part(i, GB, b, 1)], min_val=0, max_val=ND)
                    last = g.tensor_copy(wsel[:, b:b + 1, :], expT[:, bass.ds(e, 1), :])
                last.then_inc(sem("wsel_ready"), 1)

            def a_r1(i):
                rstd("A", i, "l1")
                g.wait_ge(*ua.read(i, "r11"))
                wide = lambda r: r[:, :].unsqueeze(1).broadcast_to([P, TT, D])
                g.tensor_tensor(x2row, nrow, wide(g1row), ALU.mult).then_inc(sem("x2_scaled"), 1)
                g.wait_ge(sem("x2_scaled"), i + 1)
                g.tensor_tensor(x2row, x2row, wide(be1row), ALU.add).then_inc(sem("x2_ready"), 1)
                rstd("A", i, "l2")

            def bias_mask(i, duo):
                wait_apart(g, sem(f"bias_loaded{duo}"), 64 * i + 64)
                for pr in range(2):
                    m = mneg[:, part(i, TT, 2 * duo + pr, 1), :]
                    last = g.tensor_tensor(bias[:, duo, pr, :, :], bias[:, duo, pr, :, :], m.broadcast_to([P, H, S]), ALU.add)
                last.then_inc(sem("bias_masked"), 1)

            def b_s(i, duo):
                for pr in range(2):
                    g.wait_ge(sem("scored"), half(i, duo, pr))
                    wide = smx[:, pr, :].unsqueeze(2).broadcast_to([P, H, S])
                    g.tensor_tensor(sc[:, pr, :, :], sc[:, pr, :, :], wide, ALU.subtract).then_inc(sem("centered"), 1)

            def b_m(i, duo):
                for pr in range(2):
                    g.wait_ge(sem("rsum_ready"), half(i, duo, pr))
                    wide = rsum[:, pr, :].unsqueeze(2).broadcast_to([P, H, S])
                    g.tensor_tensor(sc[:, pr, :, :], sc[:, pr, :, :], wide, ALU.mult).then_inc(sem("probs_ready"), 1)

            def c_tok(i):
                g.wait_ge(sem("t_var"), i + 1)
                f = lambda k: tst[k][:, :, :].rearrange("p a b -> p (a b)")
                g.tensor_tensor(f("rstd"), f("var"), mhalf[:, :], ALU.pow).then_inc(sem("t_rstd"), 1)

            def c_scat(i):
                wait_apart(g, *ub.read(i + 1, "hr1"))
                g.wait_ge(sem("idx_ready"), i + 1)
                for n in range(TT):
                    for k in range(TOPK):
                        g.indirect_dma_start(out=rows_in, out_offset=bass.IndirectOffsetOnAxis(ap=idx[:, n, k:k + 1], axis=0),
                                             in_=hrow[:, n, k, :], in_offset=None).then_inc(sem("scattered"), 16)

            steps = {"A.xT": a_xb, "A.mask0": a_mask0, "A.mask1": a_mask1, "A.r0": lambda i: rstd("A", i, "l0"),
                     "A.x1": a_wsel, "A.r1": a_r1, "B.s0": lambda i: b_s(i, 0), "B.s1": lambda i: b_s(i, 1),
                     "B.m0": lambda i: b_m(i, 0), "B.m1": lambda i: b_m(i, 1), "B.r2": lambda i: rstd("B", i, "l3"),
                     "B.r3": lambda i: rstd("B", i, "l4"), "C.tok": c_tok, "C.scat": c_scat,
                     "A.bias": lambda i: bias_mask(i, 0), "B.bias": lambda i: bias_mask(i, 1)}
            for s in ORDER:
                if s in steps and s[0] == "A":
                    if s == "A.r0":
                        g.wait_ge(sem("mhalf_ready"), 1)
                    if s == "A.r1":
                        g.wait_ge(sem("rows_loaded"), 48)
                    if s == "A.bias":
                        g.wait_ge(sem("mneg_ready"), 1)
                    steps[s](0)
            rounds(steps, 1, "AB")
            rounds(steps, 2)
            with g.Fori(3, NG) as i:
                rounds(steps, i)
            rounds(steps, NG, "BC")
            rounds(steps, NG + 1, "C")
            g.wait_ge(sem("zrow_ready"), 1)
            g.wait_ge(sem("pads_ready"), 1)
            for e in range(NE):
                g.indirect_dma_start(out=rows_in, out_offset=bass.IndirectOffsetOnAxis(ap=padu[:, e:e + 1], axis=0),
                                     in_=zrow, in_offset=None).then_inc(sem("scattered"), 16)
            g.wait_ge(sem("plan_ready"), 1)

            def bias_of(t_, k, first=False):
                e = g.value_load(meta[0:1, 0, part(t_, 1)], min_val=0, max_val=NE - 1)
                if not first:
                    g.wait_ge(sem("hid_done1"), t_ - 1)
                g.tensor_copy(b1c[:, k, :], eb1[:, bass.ds(e * FC, FC)]).then_inc(sem("b1_ready"), 1)

            def add(t_, k, first=False):
                g.wait_ge(sem("y_copied"), t_ + 1)
                if not first:
                    g.wait_ge(sem(f"added{1 - k}"), 8 * t_ + 8 * k)
                g.tensor_copy(idxc[:, k:k + 1], info[:, part(t_, 1), 0:1].rearrange("p a b -> p (a b)")).then_inc(sem("idxc_ready"), 1)
                wait_apart(g, sem("idxc_ready"), t_ + 1)
                g.indirect_dma_start(out=sums, out_offset=bass.IndirectOffsetOnAxis(ap=idxc[:, k:k + 1], axis=0),
                                     in_=ys[:, k, :], in_offset=None, compute_op=ALU.add).then_inc(sem(f"added{k}"), 16)

            bias_of(0, 0, True)
            bias_of(1, 1, True)
            g.wait_ge(sem("x_stored"), 16 * NG)
            bias_of(2, 0)
            add(0, 0, True)
            bias_of(3, 1)
            add(1, 1)
            with g.Fori(1, (MT - 3) // 2) as j:
                for k in range(2):
                    bias_of(2 * j + (k + 2), k)
                    add(2 * j + k, k)
            bias_of(MT - 1, 0)
            for t_ in range(MT - 3, MT):
                add(t_, t_ % 2)


def kernel(**inputs):
    import numpy as np
    import concourse.bacc as bacc
    from concourse.bass_utils import run_bass_kernel_spmd

    nc = bacc.Bacc("TRN2", target_bir_lowering=False, num_devices=1)
    arrays, tensors = {}, {}
    for name in inputs:
        a = np.ascontiguousarray(inputs[name])
        arrays[name] = a
        tensors[name] = nc.dram_tensor(name, a.shape, mybir.dt.from_np(a.dtype), kind="ExternalInput").ap()
    half = D // 2
    arrays["freqs"] = np.exp(np.arange(half, dtype=np.float32) * np.float32(-np.log(10000.0) / (half - 1)))
    tensors["freqs"] = nc.dram_tensor("freqs", (half,), F32, kind="ExternalInput").ap()
    tensors["out"] = nc.dram_tensor("out", (B, S, D), F32, kind="ExternalOutput").ap()
    build(nc, tensors)
    r = run_bass_kernel_spmd(nc, [arrays], core_ids=[0])
    return r.results[0]["out"]
```

```python
import concourse.bass as bass
from concourse import mybir
from contextlib import ExitStack

F32 = mybir.dt.float32
F32R = mybir.dt.float32r
BF16 = mybir.dt.bfloat16
I32 = mybir.dt.int32
U32 = mybir.dt.uint32
U8 = mybir.dt.uint8
ALU = mybir.AluOpType
ACT = mybir.ActivationFunctionType
AX = mybir.AxisListType

B, S, D = 64, 64, 256
P = 128
DC = D // P
GB = 8
GT = GB * S
NG = B // GB
TT = GT // P
H, HD = 16, 16
FF = 1024
FC = FF // P
A1 = 64
ND = 16
NE, TOPK = 8, 2
NSUB, SE, SH = 32, 64, 128
CAP = B * S + P
MT = TOPK * B * S // P + NE - 1
MTP = MT + 1
EPS, EPS_T = 1e-5, 1e-8
NEG = -1e30
DX = D + 2
MAGIC = 12582912.0
INV2PI, PI = 0.15915494309189535, 3.141592653589793
C1, C2, C3 = 6.28125, 0.0019350051879882812, 3.0199159819e-07

A_UNITS = ([(f"xT{c}", "dve", (c,)) for c in range(2)]
           + [(n, "act", (k % 4,)) for k, n in enumerate(["nr0", "nr1", "ts0", "ts1", "sr0", "sr1", "sr2", "sr3"])]
           + [("su0", "act", (0,)), ("su1", "act", (1,)), ("y0", "dve", (2,)), ("y1", "dve", (3,)),
              ("r00", "dve", (0,)), ("r01", "dve", (1,)), ("x10", "act", (2,)), ("x11", "act", (3,)),
              ("dn", "act", (0,)), ("ex", "dve", (1,)), ("u0", "dve", (2,)), ("u1", "dve", (3,)),
              ("r10", "dve", (0,)), ("r11", "dve", (1,)), ("x20", "dve", (2,)), ("x21", "dve", (3,)),
              ("q0", "act", (0,)), ("q1", "act", (1,)), ("k0", "dve", (2,)), ("k1", "dve", (3,)),
              ("v0", "dve", (0,)), ("v1", "dve", (1,)), ("v2", "dve", (2,)), ("v3", "dve", (3,))])
B_TAIL = [("h40", "act", (1,)), ("h41", "act", (2,)), ("lg", "dve", (1,)), ("hr0", "act", (2,)), ("hr1", "act", (3,)),
          ("rk", "dve", (1,)), ("ct", "dve", (1,)), ("b20", "dve", (1,)), ("b21", "dve", (2,))]
B_UNITS = (B_TAIL[:2] + [("sc0", "dve", (0, 1, 2, 3))]
           + [(f"pt0{k}", "act" if k % 2 else "dve", (k,)) for k in range(4)] + [("cx0", "act", (0,)), B_TAIL[2]]
           + [("sc1", "dve", (0, 1, 2, 3))] + B_TAIL[3:6]
           + [(f"pt1{k}", "act" if k % 2 else "dve", (k,)) for k in range(4)] + [("cx1", "act", (0,))]
           + [("o0", "dve", (1,)), ("o1", "dve", (2,)), B_TAIL[6], ("r20", "dve", (3,)), ("r21", "dve", (0,))]
           + B_TAIL[7:] + [("h30", "act", (3,)), ("h31", "act", (0,))]
           + [(f"f{c}", "act", ((c + 1) % 4,)) for c in range(FC)]
           + [("g0", "dve", (1,)), ("g1", "dve", (2,)), ("r30", "dve", (3,)), ("r31", "dve", (0,))])

ORDER = ["A.xT", "C.h4", "B.s0", "A.hid0", "B.e0", "C.tok", "A.hid1a", "B.m0", "C.hf", "A.mask0",
         "A.hid1b", "A.sr2a", "B.t0", "B.bias", "B.p0", "C.lg", "B.s1", "A.sr2b", "B.e1", "C.ge", "C.hr",
         "A.mask1", "B.m1", "C.rk", "A.out", "B.t1", "A.r0", "B.p1", "B.o", "C.ct", "A.x1", "B.r2",
         "A.dn", "C.b2", "A.ex", "B.h3", "C.scat", "A.up", "B.f1a", "A.r1", "B.f1b", "B.f1c", "B.f1d",
         "B.f2a", "A.x2", "B.f2b", "A.q", "B.r3", "A.k", "A.v0", "A.v1", "A.bias"]

class Units:

    def __init__(self, units, banks, filled, read_by, late=(), end=NG):
        self.units, self.banks, self.filled_sem, self.read_by = units, banks, filled, read_by
        self.late, self.end = {n for n, _, _ in late}, end
        self.at = {n: k for k, (n, _, _) in enumerate(units)}

    def present(self, i, name):
        if isinstance(i, int) and i in (0, self.end):
            return (name in self.late) == (i == self.end)
        return True

    def count(self, i, names, name):
        here = len([n for n in names[:names.index(name) + 1] if self.present(i, n)])
        if isinstance(i, int) and i == 0:
            return here
        return i * len(names) + (here - len([n for n in names if n in self.late]))

    def filled(self, i, name):
        return self.filled_sem, self.count(i, [n for n, _, _ in self.units], name)

    def read(self, i, name):
        who = self.units[self.at[name]][1]
        return self.read_by[who], self.count(i, [n for n, w, _ in self.units if w == who], name)

    def wait_free(self, pe, i, name):
        k, last = self.at[name], {}
        for bank in self.units[k][2]:
            here = [j for j, u in enumerate(self.units[:k]) if bank in u[2] and self.present(i, u[0])]
            if here:
                before = (1, here[-1])
            elif isinstance(i, int) and i == 0:
                continue
            else:
                before = (0, max(j for j, u in enumerate(self.units) if bank in u[2] and self.present(i - 1, u[0])))
            who = self.units[before[1]][1]
            last[who] = max(last.get(who, before), before)
        for same, j in last.values():
            pe.wait_ge(*self.read(i if same else i - 1, self.units[j][0]))

    def bank(self, name):
        return self.banks[:, self.units[self.at[name]][2][0], :]

    def fill(self, ins):
        ins.then_inc(self.filled_sem, 1)

    def done(self, ins, name):
        ins.then_inc(self.read_by[self.units[self.at[name]][1]], 1)


VECS = [("L0_cond_b1_nr", 2), ("L0_cond_b2_nr", 2), ("L0_cond_b1_tsr", 2), ("L0_cond_b2_tsr", 2),
        ("L0_cond_b1_sr", 4), ("L0_cond_b2_sr", 2), ("L0_cond_b3_sr", 2), ("L0_cond_gamma", 2),
        ("L0_cond_beta", 2), ("L1_cond_up_b", 2), ("L2_cond_b_ada", 4), ("L2_cond_bq", 2), ("L2_cond_bk", 2),
        ("L2_cond_bo", 2), ("L2_cond_b1", 8), ("L2_cond_b2", 2), ("L2_cond_g2", 2), ("L2_cond_beta2", 2),
        ("L3_cond_ln_g", 2), ("L3_cond_ln_b", 2), ("L3_cond_hyp_b1", 1), ("L3_cond_hyp_b2", 1),
        ("L3_cond_sty_b2", 4), ("freqs", 1)]
HALVES = ["L1_cond_down_b", "L3_cond_sty_b1"]
ROW, NROWS = {}, 0
for _name, _n in VECS:
    ROW[_name] = NROWS
    NROWS += _n
for _name in HALVES:
    ROW[_name] = NROWS
    NROWS += 1


def part(i, n, at=0, size=None):
    size = n if size is None else size
    if isinstance(i, int):
        return slice(i * n + at, i * n + at + size)
    return bass.ds(i * n + at, size)


def wait_apart(engine, semaphore, value):
    if not isinstance(value, int):
        value = engine.to_reg(value)
        engine.wait_ge(semaphore, 1)
    engine.wait_ge(semaphore, value)


def build(nc, t):
    ctx = ExitStack()
    with ctx:
        def sb(name, shape, dt=F32, of=ctx):
            return of.enter_context(nc.sbuf_tensor(name, shape, dt))

        sems = {}

        def sem(name):
            if name not in sems:
                sems[name] = ctx.enter_context(nc.semaphore(name))
            return sems[name]

        def dram(name):
            return nc.dram_tensor(name, DRAMS[name], F32, kind="Internal").ap()

        DRAMS = {"rows_in": [NE * CAP, DX], "sums": [B * S + P, D]}
        rows_in = dram("rows_in")
        sums = dram("sums")

        ident = sb("ident", [P, P])
        upper = sb("upper", [P, P], BF16)
        ones = sb("ones", [P, P], BF16)
        head_half = sb("head_half", [P, 2])
        pidx = sb("pidx", [P, 1])
        pidx_i = sb("pidx_i", [P, 2], I32)
        iot = sb("iot", [P, MTP])
        eoff = sb("eoff", [P, NE])
        mhalf = sb("mhalf", [P, DC * GB])
        colv = sb("colv", [P, NROWS])
        bq4 = sb("bq4", [P, DC])
        eb1 = sb("eb1", [P, NE * FC])
        wrt = sb("wrt", [P, DC, NE])
        b2e = sb("b2e", [NE, D])
        g1row, be1row, bvrow = (sb(n, [P, D]) for n in ("g1row", "be1row", "bvrow"))
        mneg = sb("mneg", [P, B // 2, S], BF16)
        mcond = sb("mcond", [P, 3, B])
        bsel0 = sb("bsel0", [P, DC, B])
        bsel1 = sb("bsel1", [A1, B])
        widx = sb("widx", [1, B], I32)
        ada = sb("ada", [P, 4, B])
        sty = sb("sty", [P, 4, B])
        tok = sb("tok", [P, TT])
        base = sb("base", [P, NE])

        sc = sb("sc", [P, 2, H, S])
        slot = sb("slot", [P, TT, TOPK])
        smx, ssum, rsum = (sb(n, [P, 2, H]) for n in ("smx", "ssum", "rsum"))
        st = {k: sb(f"st_{k}", [P, TT, 6]) for k in "AB"}
        mv = {k: sb(f"mv_{k}", [P, TT, 2]) for k in "AB"}
        ve = {k: sb(f"ve_{k}", [P, TT]) for k in "AB"}
        rs = {k: sb(f"rs_{k}", [P, TT]) for k in "AB"}
        st4 = sb("st4", [P, DC, GB, 6])
        tst = {n: sb(f"t_{n}", [P, DC, GB]) for n in ("sum", "dif", "sq", "var", "rstd", "mul", "mm", "add")}
        lgs = sb("lgs", [P, TT, NE])
        mx8 = sb("mx8", [P, TT, NE])
        mi8 = sb("mi8", [P, TT, NE], U32)
        mif = sb("mif", [P, TT, TOPK])
        oh = sb("oh", [P, TOPK, TT, NE])
        picked = sb("picked", [P, TT, NE], BF16)
        gd, ge, gp = (sb(n, [P, TT]) for n in ("gd", "ge", "gp"))
        cm = sb("cm", [P, TOPK, TT, NE])
        cmix = sb("cmix", [P, TT, NE])
        pos = sb("pos", [P, TT, NE])
        posk = sb("posk", [P, TOPK, TT, NE])
        idx = sb("idx", [P, TT, TOPK], U32)
        cnt = sb("cnt", [P, NE])
        plan_space = sc[:, :, :, :].rearrange("p a h k -> p (a h k)")
        plan = {n: plan_space[:, k * MTP:(k + 1) * MTP]
                for k, n in enumerate(("e", "start", "idle", "src"))}
        pl8 = {n: sb(f"pl8_{n}", [P, NE]) for n in ("n", "incl", "one")}
        pge = plan_space[:, 4 * MTP:(4 + NE) * MTP].rearrange("p (t e) -> p t e", e=NE)
        meta = plan_space[:, 1400:1400 + 2 * MTP].bitcast(I32).rearrange("p (a t) -> p a t", a=2)
        padi = sb("padi", [P, NE], I32)
        b1c = sb("b1c", [P, 2, FC])
        info = plan_space[:, 1200:1200 + 2 * MTP].rearrange("p (t a) -> p t a", a=2)
        idxc = sb("idxc", [P, 2], U32)

        zrow = plan_space[:, 900:900 + DX]

        groups = ExitStack()
        gsb = lambda name, shape, dt=F32: sb(name, shape, dt, groups)
        early = gsb("early", [P, NE * FC * D])

        def cut(k, n, shape, whole=early, parts=P):
            v = whole[0:parts, k * 512:k * 512 + n]
            names = "abcd"[:len(shape)]
            if len(shape) == 1:
                return v
            return v.rearrange(f"p ({' '.join(names)}) -> p {' '.join(names)}", **dict(zip(names, shape)))

        wl0 = gsb("wl0", [P, 10 * D])
        w0 = lambda a, k, n: wl0[:, a * D:a * D + k * n].rearrange("p (k n) -> p k n", k=k)
        w2nr, w2ts, w2sr, w3sr = w0(0, 2, D), w0(2, 2, D), w0(4, 4, D), w0(8, 2, D)
        whigh, wlow = (gsb(n, [P, 20 * D], F32R) for n in ("whigh", "wlow"))
        both = lambda a, n: [w[:, a * D:a * D + 2 * n].rearrange("p (k n) -> p k n", k=2) for w in (whigh, wlow)]
        w1nr, w1ts, w1sr, wq, wk, wf1 = both(0, D), both(2, D), both(4, 2 * D), both(8, D), both(10, D), both(12, FF)
        downT = gsb("downT", [P, DC, A1])
        upT = gsb("upT", [A1, D])
        expT = gsb("expT", [A1, ND + 1, A1])
        wsel = gsb("wsel", [A1, GB, A1])
        wat = gsb("wat", [P, 2 * DC * D])
        wv, wo = (wat[:, k * 512:(k + 1) * 512].rearrange("p (k n) -> p k n", k=2) for k in range(2))
        wff = gsb("wff", [P, 8 * D])
        wf2 = wff[:, :].rearrange("p (k n) -> p k n", k=FC)
        xin = cut(0, 1024, [TT, D])
        xb = cut(0, 1024, [DC, GT])
        xT = cut(2, 1024, [DC, GT])
        hn, ht = cut(4, 1024, [DC, GT]), cut(6, 1024, [DC, GT])
        hs, hs2 = cut(8, 2048, [4, GT]), cut(12, 1024, [DC, GT])
        nrow = cut(4, 1024, [TT, D])
        x1T, x2row = cut(8, 1024, [DC, GT]), cut(10, 1024, [TT, D])
        hd, he = cut(12, 512, [GT], parts=A1), cut(13, 512, [GT], parts=A1)
        qT = cut(14, 1024, [DC, GT])
        kbd = cut(16, 2048, [DC, GB, 2, S])
        vbd = cut(20, 2048, [GB, H // 2, 2 * HD])
        bias = cut(24, 4096, [2, 2, H, S])
        xmT = gsb("xmT", [P, DC, GT])
        late = gsb("late", [P, 8 * 512])
        pT = gsb("pT", [P, 4, GT])
        x3T = pT[:, 2:4, :]
        h3T = pT[:, 0:2, :]
        thigh, tlow = (gsb(n, [P, DC, GT], F32R) for n in ("thigh", "tlow"))
        fT = late[:, 0:4096].rearrange("p (a b) -> p a b", a=FC)
        ctxT = cut(0, 1024, [DC, GT], late)
        n3row = cut(2, 1024, [TT, D], late)
        n4row = cut(0, 1024, [TT, D], late)
        h4T = cut(2, 1024, [DC, GT], late)
        hfT = cut(4, 1024, [DC, GT], late)
        ctT = cut(6, 512, [GT], late, NE)
        xres = gsb("xres", [P, TT, D])
        hspace = gsb("hrow", [P, TT * TOPK * DX])
        hrow = hspace[:, :].rearrange("p (n k d) -> p n k d", n=TT, k=TOPK)
        groups.close()
        with ExitStack() as whole:
            w2raw = sb("w2raw", [P, NE * FC * D], F32, whole)
        w2low, w2high = (sb(n, [P, NE * FC, D], F32R) for n in ("w2low", "w2high"))
        w2all = w2raw[:, :].rearrange("p (e n) -> p e n", n=D)
        w1slot = [sb(f"w1slot{k}", [P, DC, FF]) for k in range(2)]
        hid = sb("hid", [P, 2, FC, P])
        hid_h, hid_l = (sb(n, [P, 2, FC, P], F32R) for n in ("hid_h", "hid_l"))
        xs = sb("xs", [P, 2, DX])
        xsT = sb("xsT", [P, 2, D])
        ys = sb("ys", [P, 2, D])

        raw = lambda a, n: hspace[:, a * D:a * D + 2 * n].rearrange("p (k n) -> p k n", k=2)
        raw_qk = [xres[:, 2 * k:2 * k + 2, :] for k in range(2)]
        vec = sc[:, 0, 0:2, :].rearrange("p a b -> p (a b)")
        eb1r = sc[0:NE * FC, 0, 2:4, :].rearrange("p a b -> p (a b)")
        upW = sc[:, 0, 4:6, :]
        downW = sc[0:A1, 0, 6:10, :].rearrange("p a b -> p (a b)")
        expW = sc[0:A1, 1, :, :]
        mask8 = pT[:, 2, :].bitcast(U8).rearrange("p (n k) -> p n k", k=S)
        semb = sc[0:NSUB, 0, 10, :]
        expb = sc[0:ND, 0, 11, :]
        demb = sc[0:ND, 0, 12, :]
        hw1 = pT[0:SE, 0, 0:SH]
        hw2 = pT[:, 0, SH:2 * SH]
        sw1 = pT[:, 0, 2 * SH:2 * SH + SH // 2]
        sw2 = pT[0:SH // 2, 1, :]
        wada = late[:, 0:1024].rearrange("p (k n) -> p k n", k=2)
        scr = lambda k, n=B: late[:, 1024 + 64 * k:1024 + 64 * k + n]
        ints = late[:, 3584:3584 + 4 * B].bitcast(I32).rearrange("p (a b) -> p a b", a=4)
        idf = late[:, 3840:3840 + 4 * B].rearrange("p (a b) -> p a b", a=4)
        sce = late[:, 3072:3072 + 512].rearrange("p (a b) -> p a b", a=8)

        PA = ctx.enter_context(nc.psum_tensor("banks_a", [P, 4, 512], F32))
        PB = ctx.enter_context(nc.psum_tensor("banks_b", [P, 4, 512], F32))
        ua = Units(A_UNITS, PA, sem("a_filled"), {"act": sem("a_read_by_act"), "dve": sem("a_read_by_dve")})
        ub = Units(B_UNITS, PB, sem("b_filled"), {"act": sem("b_read_by_act"), "dve": sem("b_read_by_dve")},
                   B_TAIL)

        col = lambda name, c=0, parts=P: colv[0:parts, ROW[name] + c:ROW[name] + c + 1]
        v_seqs = lambda n: [4 * (n % 2) + 2 * h + n // 2 for h in range(2)]
        by_seq = lambda ap: ap.rearrange("p (b s) -> p b s", s=S)

        def over_tokens(ap, n=GB):
            return ap.unsqueeze(2).broadcast_to([ap.shape[0], n, S])

        half = lambda i, duo, pr: 4 * i + (2 * duo + pr + 1)

        def rounds(steps, i, streams="ABC", then={}):
            for s in ORDER:
                if s in steps and s[0] in streams:
                    k = "ABC".index(s[0])
                    steps[s](i - k if k else i)
                    if s in then:
                        then[s]()

        def added(k):
            return sem(f"added{k}"), 16 * ((MT + 1 - k) // 2)

        NVEC, NVEC_SP = len(VECS) + len(HALVES), 17

        def load_vecs(engine, first, last, loaded):
            for name, n in (VECS + [(h, 0) for h in HALVES])[first:last]:
                r, w = ROW[name], P if n else A1
                engine.dma_start(vec[r:r + max(n, 1), 0:w], t[name].rearrange("(c p) -> c p", p=w))\
                    .then_inc(sem(loaded), 16)

        def copy_out(engine, parts):
            out_v = t["out"].rearrange("b s d -> (b s) d")
            for n in parts:
                rows = slice(2 * n * GT, 2 * (n + 1) * GT)
                engine.dma_start(out_v[rows, :].rearrange("(a b) d -> a (b d)", b=S // 2),
                                 sums[rows, :].rearrange("(a b) d -> a (b d)", b=S // 2))\
                    .then_inc(sem("out_stored"), 16)

        block = ctx.enter_context(nc.Block())
        W_A = [("w1nr", raw(0, D), "L0_cond_w1_nr"), ("w1ts", raw(2, D), "L0_cond_w1_tsr"),
               ("w1sr", raw(4, 2 * D), "L0_cond_w1_sr"),
               ("w2sr", w2sr, "L0_cond_w2_sr"), ("w2nr", w2nr, "L0_cond_w2_nr"), ("w2ts", w2ts, "L0_cond_w2_tsr"),
               ("w3sr", w3sr, "L0_cond_w3_sr")]
        W_L2 = [(raw_qk[0], "L2_cond_Wq"), (raw_qk[1], "L2_cond_Wk"), (wv, "L2_cond_Wv"), (wo, "L2_cond_Wo"),
                (wf2, "L2_cond_W2")]
        kview = lambda name: t[name].rearrange("(k p) n -> p k n", p=P)

        @block.sync
        def _(sp):
            x_v = t["x"].rearrange("b s d -> (b s) d").rearrange("(n p) d -> p n d", p=P)
            mask_v = t["mask_Bx1xSxS_bk0"].rearrange("(n two) o q k -> two q (n o) k", two=2)
            bias_v = t["fside_Bx16xSxS_0"].rearrange("(g b) h q k -> b q g h k", b=GB)
            sp.dma_start(xin, x_v[:, 0:TT, :]).then_inc(sem("x_loaded"), 16)
            sp.wait_ge(sem("vec_cleared"), 1)
            load_vecs(sp, 0, NVEC_SP, "vec_loaded")
            for k, name in enumerate(["itok_B_0_2", "itok_B_0_15", "itok_B_34_63", "itok_B_6_14"]):
                sp.dma_start(ints[:, k, :], t[name].partition_broadcast(P)).then_inc(sem("ints_loaded"), 16)
            sp.dma_start(downW, t["L1_cond_down_W"]).then_inc(sem("l1_loaded"), 16)
            sp.dma_start(upW, t["L1_cond_up_W"].rearrange("(k p) a -> p k a", p=P)).then_inc(sem("l1_loaded"), 16)
            sp.dma_start(expW, t["L1_cond_expert_W"].rearrange("e o a -> o e a")).then_inc(sem("l1_loaded"), 16)
            sp.dma_start(expb, t["L1_cond_expert_b"]).then_inc(sem("l1_loaded"), 16)
            sp.dma_start(demb, t["L1_cond_domain_emb"]).then_inc(sem("l1_loaded"), 16)
            sp.dma_start(eb1r, t["L3_cond_exp_b1"].rearrange("e (c p) -> (e c) p", p=P))\
                .then_inc(sem("l1_loaded"), 16)
            for row, name in ((g1row, "L1_cond_ln_gamma"), (be1row, "L1_cond_ln_beta"), (bvrow, "L2_cond_bv")):
                sp.dma_start(row[:, :], t[name].partition_broadcast(P)).then_inc(sem("rows_loaded"), 16)
            for two in range(2):
                sp.dma_start(mask8[two * S:(two + 1) * S, :, :], mask_v[two]).then_inc(sem("mask_loaded"), 16)
            sp.dma_start(wada, kview("L2_cond_W_ada")).then_inc(sem("tab_loaded"), 16)
            for dst, name in ((semb, "L3_cond_subj_emb"), (hw1, "L3_cond_hyp_w1"), (hw2, "L3_cond_hyp_w2"),
                              (sw1, "L3_cond_sty_w1"), (sw2, "L3_cond_sty_w2")):
                sp.dma_start(dst, t[name]).then_inc(sem("tab_loaded"), 16)
            for dst, name in W_L2:
                sp.dma_start(dst, kview(name)).then_inc(sem("l2_loaded"), 16)
            sp.dma_start(wrt[:, :, :], kview("L3_cond_router_w")).then_inc(sem("l3_loaded"), 16)
            sp.dma_start(b2e[:, :], t["L3_cond_exp_b2"]).then_inc(sem("l3_loaded"), 16)

            def load_bias(i, duo):
                for b in range(4):
                    sp.dma_start(bias[(b % 2) * S:(b % 2 + 1) * S, duo, b // 2, :, :],
                                 bias_v[4 * duo + b, :, part(i, 1), :, :].rearrange("q g h k -> q (g h) k"))\
                        .then_inc(sem(f"bias_loaded{duo}"), 16)

            for duo in range(2):
                load_bias(0, duo)

            sums_v = sums[0:B * S, :].rearrange("(n p) d -> p n d", p=P)

            def load_group(i):
                sp.wait_ge(*ua.read(i - 1, "y1"))
                sp.dma_start(xin, x_v[:, part(i, TT), :]).then_inc(sem("x_loaded"), 16)
                for duo in range(2):
                    sp.wait_ge(sem("scored"), half(i - 1, duo, 1))
                    load_bias(i, duo)

            def store_x(i):
                sp.wait_ge(*ub.read(i + 1, "b21"))
                sp.dma_start(sums_v[:, part(i, TT), :], xres[:, :, :]).then_inc(sem("x_stored"), 16)

            load_group(1)
            with sp.Fori(2, NG) as i:
                load_group(i)
                store_x(i - 2)
            sp.wait_ge(*ub.read(NG - 1, "cx1"))
            sp.wait_ge(*ub.filled(NG - 1, "cx1"))
            for e in range(NE):
                sp.dma_start(w2all[:, e * FC:(e + 1) * FC, :],
                             t["L3_cond_exp_w2"][e].rearrange("(c p) n -> p c n", p=P))\
                                 .then_inc(sem("w2_loaded"), 16)
            store_x(NG - 2)
            store_x(NG - 1)
            sp.wait_ge(sem("pads_ready"), 1)
            for e in range(NE):
                r = sp.value_load(padi[0:1, e:e + 1], min_val=0, max_val=NE * CAP - P)
                sp.dma_start(rows_in[bass.ds(r, P), :], zrow).then_inc(sem("padded"), 16)
            sp.wait_ge(sem("plan_ready"), 1)
            sp.wait_ge(sem("padded"), 16 * NE)
            sp.wait_ge(sem("scattered"), 16 * NG * TT * TOPK)
            sp.wait_ge(sem("x_stored"), 16 * NG)

            def load_tile(t_, k):
                e = sp.value_load(meta[0:1, 0, part(t_, 1)], min_val=0, max_val=NE - 1)
                sp.dma_start(w1slot[k][:, :, :], t["L3_cond_exp_w1"][bass.ds(e, 1), :, :].rearrange("e (k p) n -> p (e k) n", p=P))\
                    .then_inc(sem(f"w1_loaded{k}"), 16)

            def load_rows(t_, k):
                r = sp.value_load(meta[0:1, 1, part(t_, 1)], min_val=0, max_val=(NE * CAP) - P)
                sp.dma_start(xs[:, k, :], rows_in[bass.ds(r, P), :]).then_inc(sem(f"xs_loaded{k}"), 16)

            load_rows(0, 0)
            load_rows(1, 1)
            load_tile(0, 0)
            load_tile(1, 1)
            sp.wait_ge(sem("info_kept"), 1)
            load_rows(2, 0)
            with sp.Fori(1, (MT - 1) // 2) as j:
                for k in range(2):
                    sp.wait_ge(sem("g1_filled"), 4 * j + 2 * (k - 1))
                    load_tile(2 * j + k, k)
                    sp.wait_ge(sem("info_kept"), 2 * j + k)
                    load_rows(2 * j + (k + 1), 1 - k)
            sp.wait_ge(sem("g1_filled"), 2 * (MT - 2))
            load_tile(MT - 1, 0)
            for k in range(2):
                sp.wait_ge(*added(k))
            copy_out(sp, range(0, NG // 4))
            sp.wait_ge(sem("out_stored"), 16 * (NG // 2))

        @block.tensor
        def _(pe):
            mm = nc.tensor.matmul

            def dense(u, i, name, pairs, rows=P, cols=slice(0, GT)):
                u.wait_free(pe, i, name)
                o = u.bank(name)[0:rows, cols]
                for k, (a, b) in enumerate(pairs):
                    last = mm(o, a, b, start=(k == 0), stop=(k == len(pairs) - 1))
                u.fill(last)

            def in_parts(w, c):
                return [(a[:, k, ck(c)], b[:, k, :]) for a, b in ((w[0], thigh), (w[0], tlow), (w[1], thigh))
                        for k in range(2)]

            def to_rows(u, i, names, src):
                for n, name in enumerate(names):
                    u.wait_free(pe, i, name)
                    for h in range(2):
                        for c in range(DC):
                            at = (2 * n + h) * P
                            last = nc.tensor.transpose(u.bank(name)[:, h * D + c * P:h * D + (c + 1) * P],
                                                       src[:, c, at:at + P], ident[:, :])
                    u.fill(last)

            def from_rows(u, i, names, src):
                for c, name in enumerate(names):
                    u.wait_free(pe, i, name)
                    for n in range(TT):
                        last = nc.tensor.transpose(u.bank(name)[:, n * P:(n + 1) * P],
                                                   src[:, n, c * P:(c + 1) * P], ident[:, :])
                    u.fill(last)

            ck = lambda c: slice(c * P, (c + 1) * P)
            ready0 = lambda i: isinstance(i, int) and i == 0

            def a_xT(i):
                if ready0(i):
                    pe.wait_ge(sem("ident_ready"), 1)
                pe.wait_ge(sem("x_loaded"), 16 * i + 16)
                from_rows(ua, i, ["xT0", "xT1"], xin)

            def a_hid0(i):
                pe.wait_ge(*ua.read(i, "xT1"))
                if ready0(i):
                    pe.wait_ge(sem("w_split"), 1)
                for c in range(2):
                    dense(ua, i, f"nr{c}", in_parts(w1nr, c))
                if ready0(i):
                    pe.wait_ge(sem("w_split"), 2)
                for c in range(2):
                    dense(ua, i, f"ts{c}", in_parts(w1ts, c))

            def a_hid1(i, chunks):
                if ready0(i):
                    pe.wait_ge(sem("w_split"), 3)
                for c in chunks:
                    dense(ua, i, f"sr{c}", in_parts(w1sr, c))

            def a_sr2(i, c):
                if ready0(i):
                    pe.wait_ge(sem("w2sr_loaded"), 16)
                ua.wait_free(pe, i, f"su{c}")
                for k in range(4):
                    if c == 0:
                        pe.wait_ge(*ua.read(i, f"sr{k}"))
                    last = mm(ua.bank(f"su{c}"), w2sr[:, k, ck(c)], hs[:, k, :], start=(k == 0), stop=(k == 3))
                ua.fill(last)

            def a_out(i):
                if ready0(i):
                    for n in ("w2nr", "w2ts", "w3sr"):
                        pe.wait_ge(sem(f"{n}_loaded"), 16)
                pe.wait_ge(sem("hidden_masked"), 2 * i + 1)
                for c in range(2):
                    ua.wait_free(pe, i, f"y{c}")
                    for n, (w, h) in enumerate(((w2nr, hn), (w2ts, ht))):
                        for k in range(2):
                            mm(ua.bank(f"y{c}"), w[:, k, ck(c)], h[:, k, :], start=(n + k == 0), stop=False)
                pe.wait_ge(sem("hidden_masked"), 2 * i + 2)
                for c in range(2):
                    for k in range(2):
                        last = mm(ua.bank(f"y{c}"), w3sr[:, k, ck(c)], hs2[:, k, :], start=False, stop=(k == 1))
                    ua.fill(last)

            def a_r0(i):
                pe.wait_ge(*ua.read(i, "y1"))
                to_rows(ua, i, ["r00", "r01"], xT)

            def a_x1(i):
                pe.wait_ge(*ua.read(i, "r01"))
                from_rows(ua, i, ["x10", "x11"], nrow)

            def a_dn(i):
                if ready0(i):
                    pe.wait_ge(sem("setup_read"), 3)
                pe.wait_ge(*ua.read(i, "x11"))
                dense(ua, i, "dn", [(downT[:, k, :], x1T[:, k, :]) for k in range(2)], A1)

            def a_ex(i):
                pe.wait_ge(sem("wsel_ready"), i + 1)
                ua.wait_free(pe, i, "ex")
                wait_apart(pe, *ua.read(i, "dn"))
                for b in range(GB):
                    at = slice(b * S, (b + 1) * S)
                    last = mm(ua.bank("ex")[0:A1, at], wsel[:, b, :], hd[:, at], start=True, stop=True)
                ua.fill(last)

            def a_up(i):
                pe.wait_ge(*ua.read(i, "ex"))
                for c in range(2):
                    dense(ua, i, f"u{c}", [(upT[:, ck(c)], he[:, :])])

            def a_r1(i):
                pe.wait_ge(*ua.read(i, "u1"))
                to_rows(ua, i, ["r10", "r11"], x1T)

            def a_x2(i):
                pe.wait_ge(sem("n2_ready"), i + 1)
                from_rows(ua, i, ["x20", "x21"], nrow)

            def a_q(i):
                if ready0(i):
                    pe.wait_ge(sem("l2_loaded"), 16 * len(W_L2))
                    pe.wait_ge(sem("w_split"), 5)
                pe.wait_ge(sem("xm_ready"), i + 1)
                for c in range(2):
                    dense(ua, i, f"q{c}", in_parts(wq, c))

            def a_k(i):
                for c in range(2):
                    dense(ua, i, f"k{c}", in_parts(wk, c))

            def a_v(i, units):
                for n in units:
                    ua.wait_free(pe, i, f"v{n}")
                    for h, b in enumerate(v_seqs(n)):
                        o = ua.bank(f"v{n}")[:, h * D:(h + 1) * D]
                        for k in range(2):
                            if b + 1 < GB:
                                last = mm(o, xmT[:, k, b * S:(b + 2) * S], wv[:, k, :], start=(k == 0), stop=(k == 1))
                        if b + 1 == GB:
                            for j, bj in enumerate((b, 0)):
                                for k in range(2):
                                    last = mm(o[j * S:(j + 1) * S, :], xmT[:, k, bj * S:(bj + 1) * S], wv[:, k, :],
                                              start=(k == 0), stop=(k == 1))
                    ua.fill(last)

            def b_s(i, duo):
                if duo == 0:
                    pe.wait_ge(*ua.read(i, "q1"))
                    pe.wait_ge(*ua.read(i, "k1"))
                ub.wait_free(pe, i, f"sc{duo}")
                for pr in range(2):
                    for b in range(2):
                        g = 4 * duo + 2 * pr + b
                        for c in range(DC):
                            for r in range(4):
                                rows = slice(32 * r, 32 * r + 32)
                                last = mm(PB[b * S:(b + 1) * S, r, pr * D + c * P:pr * D + (c + 1) * P],
                                          qT[rows, c, g * S:(g + 1) * S],
                                          kbd[rows, c, g, :, :].rearrange("p j s -> p (j s)"), start=True, stop=True)
                ub.fill(last)

            def b_t(i, duo):
                for k in range(4):
                    if k % 2 == 0:
                        pe.wait_ge(sem("probs_ready"), half(i, duo, k // 2))
                    ub.wait_free(pe, i, f"pt{duo}{k}")
                    for m in range(4):
                        n = 4 * k + m
                        last = nc.tensor.transpose(ub.bank(f"pt{duo}{k}")[:, m * P:(m + 1) * P],
                                                   sc[:, n // 8, 2 * (n % 8):2 * (n % 8) + 2, :].rearrange("p a b -> p (a b)"),
                                                   ident[:, :])
                    ub.fill(last)

            def b_p(i, duo):
                pe.wait_ge(*ub.read(i, f"pt{duo}2"))
                pe.wait_ge(*ub.read(i, f"pt{duo}3"))
                if duo == 0:
                    pe.wait_ge(*ua.read(i, "v3"))
                ub.wait_free(pe, i, f"cx{duo}")
                for pr in range(2):
                    for b in range(2):
                        for c in range(DC):
                            for r in range(4):
                                n = 8 * pr + 4 * c + r
                                at = c * D + pr * P + b * S
                                last = mm(ub.bank(f"cx{duo}")[32 * r:32 * r + 32, at:at + S],
                                          vbd[:, 4 * duo + 2 * pr + b, 4 * c + r, :],
                                          pT[:, n // 4, (n % 4) * P + b * S:(n % 4) * P + (b + 1) * S], start=True, stop=True)
                ub.fill(last)

            def b_o(i):
                pe.wait_ge(*ub.read(i, "cx1"))
                for c in range(2):
                    dense(ub, i, f"o{c}", [(wo[:, k, ck(c)], ctxT[:, k, :]) for k in range(2)])

            def b_r2(i):
                pe.wait_ge(*ub.read(i, "o1"))
                to_rows(ub, i, ["r20", "r21"], x3T)

            def b_h3(i):
                pe.wait_ge(*ub.read(i, "r21"))
                from_rows(ub, i, ["h30", "h31"], n3row)

            def b_f1(i, chunks):
                if ready0(i):
                    pe.wait_ge(sem("w_split"), 6)
                pe.wait_ge(sem("h3_split"), i + 1)
                for f in chunks:
                    dense(ub, i, f"f{f}", in_parts(wf1, f))

            def b_f2(i, c):
                pe.wait_ge(*ub.read(i, "f6"))
                ub.wait_free(pe, i, f"g{c}")
                for k in range(FC):
                    if k == FC - 1:
                        pe.wait_ge(*ub.read(i, "f7"))
                    last = mm(ub.bank(f"g{c}"), wf2[:, k, ck(c)], fT[:, k, :], start=(k == 0), stop=(k == FC - 1))
                ub.fill(last)

            def b_r3(i):
                pe.wait_ge(*ub.read(i, "g1"))
                to_rows(ub, i, ["r30", "r31"], x3T)

            def c_h4(i):
                pe.wait_ge(*ub.read(i, "r31"))
                from_rows(ub, i + 1, ["h40", "h41"], n4row)

            def c_lg(i):
                pe.wait_ge(sem("hf_ready"), i + 1)
                ub.wait_free(pe, i + 1, "lg")
                for n in range(TT):
                    for k in range(2):
                        last = mm(ub.bank("lg")[:, n * NE:(n + 1) * NE], hfT[:, k, n * P:(n + 1) * P], wrt[:, k, :],
                                  start=(k == 0), stop=(k == 1))
                ub.fill(last)

            def c_hr(i):
                to_rows(ub, i + 1, ["hr0", "hr1"], hfT)

            def c_rk(i):
                pe.wait_ge(sem("picked_ready"), i + 1)
                ub.wait_free(pe, i + 1, "rk")
                for n in range(TT + 1):
                    o = ub.bank("rk")[:, n * NE:(n + 1) * NE]
                    for m in range(min(n, TT)):
                        last = mm(o, ones[:, :], picked[:, m, :], start=(m == 0), stop=(m == min(n, TT) - 1 and n == TT))
                    if n < TT:
                        last = mm(o, upper[:, :], picked[:, n, :], start=(n == 0), stop=True)
                ub.fill(last)

            def c_ct(i):
                pe.wait_ge(sem("cmix_ready"), i + 1)
                ub.wait_free(pe, i + 1, "ct")
                for n in range(TT):
                    last = nc.tensor.transpose(ub.bank("ct")[0:NE, n * P:(n + 1) * P], cmix[:, n, :], ident[:, :])
                ub.fill(last)

            def c_b2(i):
                pe.wait_ge(*ub.read(i + 1, "ct"))
                for k in range(2):
                    ub.wait_free(pe, i + 1, f"b2{k}")
                    for h in range(2):
                        n = 2 * k + h
                        last = mm(ub.bank(f"b2{k}")[:, h * D:(h + 1) * D], ctT[:, n * P:(n + 1) * P], b2e[:, :],
                                  start=True, stop=True)
                    ub.fill(last)

            steps = {"A.xT": a_xT, "A.hid0": a_hid0, "A.hid1a": lambda i: a_hid1(i, (0, 1)),
                     "A.hid1b": lambda i: a_hid1(i, (2, 3)), "A.sr2a": lambda i: a_sr2(i, 0),
                     "A.sr2b": lambda i: a_sr2(i, 1), "A.out": a_out, "A.r0": a_r0,
                     "A.x1": a_x1, "A.dn": a_dn, "A.ex": a_ex, "A.up": a_up, "A.r1": a_r1, "A.x2": a_x2, "A.q": a_q,
                     "A.k": a_k, "A.v0": lambda i: a_v(i, (0, 1)), "A.v1": lambda i: a_v(i, (2, 3)),
                     "B.s0": lambda i: b_s(i, 0), "B.s1": lambda i: b_s(i, 1), "B.p0": lambda i: b_p(i, 0),
                     "B.p1": lambda i: b_p(i, 1), "B.t0": lambda i: b_t(i, 0), "B.t1": lambda i: b_t(i, 1),
                     "B.o": b_o, "B.r2": b_r2, "B.h3": b_h3,
                     **{f"B.f1{n}": (lambda i, k=k: b_f1(i, (2 * k, 2 * k + 1))) for k, n in enumerate("abcd")},
                     "B.f2a": lambda i: b_f2(i, 0), "B.f2b": lambda i: b_f2(i, 1), "B.r3": b_r3,
                     "C.h4": c_h4, "C.lg": c_lg, "C.hr": c_hr, "C.rk": c_rk, "C.ct": c_ct, "C.b2": c_b2}

            def setup_cols():
                pe.wait_ge(sem("ident_ready"), 1)
                pe.wait_ge(sem("upper_ready"), 1)
                pe.wait_ge(sem("vec_loaded"), 16 * NVEC_SP)
                pe.wait_ge(sem("vec_loaded_by_pool"), 16 * (NVEC - NVEC_SP))
                nc.tensor.transpose(PB[:, 0, 0:P], vec, ident[:, :]).then_inc(sem("setup_filled"), 1)

            def setup_l1():
                pe.wait_ge(sem("l1_loaded"), 16 * 6)
                nc.tensor.transpose(PB[:, 1, 0:NE * FC], eb1r, ident[0:64, 0:64])
                for k in range(2):
                    nc.tensor.transpose(PB[:, 1, P + k * A1:P + (k + 1) * A1], downW[:, ck(k)], ident[0:64, 0:64])
                    nc.tensor.transpose(PB[0:A1, 1, (2 + k) * P:(3 + k) * P], upW[:, k, :], ident[:, :])\
                        .then_inc(sem("setup_filled"), 1)
                for e in range(ND):
                    last = nc.tensor.transpose(PB[0:A1, 2 + e // 8, (e % 8) * A1:(e % 8 + 1) * A1], expW[:, e, :],
                                               ident[0:64, 0:64])
                last.then_inc(sem("setup_filled"), 1)
                pe.wait_ge(sem("onehot_ready"), 1)
                pe.wait_ge(sem("setup_read"), 1)
                mm(PB[0:A1, 0, P:P + B], expb, sce[0:ND, 0, 0:B], start=True, stop=False)
                mm(PB[0:A1, 0, P:P + B], demb, sce[0:ND, 1, 0:B], start=False, stop=True)\
                    .then_inc(sem("setup_filled"), 1)

            def setup_ada():
                pe.wait_ge(sem("tab_loaded"), 16 * 6)
                pe.wait_ge(sem("emb_ready"), 1)
                pe.wait_ge(sem("setup_read"), 4)
                for m in range(4):
                    for k in range(2):
                        last = mm(PB[:, 1, m * B:(m + 1) * B], wada[:, k, ck(m)], scr(2 + k), start=(k == 0), stop=(k == 1))
                last.then_inc(sem("setup_filled"), 1)

            def setup_sty(n):
                if n == 0:
                    mm(PB[0:SE, 2, 0:B], semb, sce[0:NSUB, 2, 0:B], start=True, stop=True)\
                        .then_inc(sem("setup_filled"), 1)
                    return
                pe.wait_ge(sem("sty_step"), n)
                if n == 1:
                    last = mm(PB[:, 2, 0:B], hw1, scr(4)[0:SE, :], start=True, stop=True)
                if n == 2:
                    last = mm(PB[:, 2, 0:B], hw2, scr(5), start=True, stop=True)
                if n == 3:
                    last = mm(PB[0:SE, 2, 0:B], sw1, scr(6), start=True, stop=True)
                if n == 4:
                    for m in range(4):
                        last = mm(PB[:, 3, m * B:(m + 1) * B], sw2[:, ck(m)], scr(7)[0:SE, :], start=True, stop=True)
                last.then_inc(sem("setup_filled"), 1)

            def setup_first():
                setup_cols()
                setup_l1()

            setup = {"A.hid0": setup_first, "A.sr2b": setup_ada, "A.out": lambda: setup_sty(0),
                     "A.r0": lambda: setup_sty(1), "A.x1": lambda: setup_sty(2), "A.ex": lambda: setup_sty(3),
                     "A.up": lambda: setup_sty(4)}
            for s in ORDER:
                if s[0] == "A" and s in steps:
                    steps[s](0)
                    if s in setup:
                        setup[s]()
            pe.wait_ge(sem("setup_read"), 7)
            pe.wait_ge(sem("l3_loaded"), 32)
            rounds(steps, 1, "AB")
            rounds(steps, 2)
            with pe.Fori(3, NG) as i:
                rounds(steps, i)
            rounds(steps, NG, "BC")
            rounds(steps, NG + 1, "C")

            bank8 = lambda k: (PA if k < 4 else PB)[:, k % 4, :]

            def lay(t_, k):
                pe.wait_ge(sem(f"xs_loaded{k}"), 8 * (t_ - k) + 16)
                for c in range(DC):
                    last = nc.tensor.transpose(bank8(k)[:, ck(c)], xs[:, k, ck(c)], ident[:, :])
                last.then_inc(sem("xsT_filled"), 1)

            def up(t_, k, first=False):
                pe.wait_ge(sem("xsT_copied"), t_ + 1)
                pe.wait_ge(sem(f"w1_loaded{k}"), 8 * (t_ - k) + 16)
                for h in range(2):
                    if not first:
                        pe.wait_ge(sem(f"hid_done{h}"), t_ - 1)
                    for f in range(4 * h, 4 * h + 4):
                        for c in range(DC):
                            last = mm(bank8(2 + 2 * k + h)[:, ck(f % 4)], w1slot[k][:, c, ck(f)], xsT[:, k, ck(c)],
                                      start=(c == 0), stop=(c == 1))
                    last.then_inc(sem("g1_filled"), 1)

            def down(t_, k, first=False):
                e = pe.value_load(meta[0:1, 0, part(t_, 1)], min_val=0, max_val=NE - 1)
                if not first:
                    pe.wait_ge(sem("y_copied"), t_ - 1)
                for f in range(FC):
                    if f % 4 == 0:
                        pe.wait_ge(sem("hid_parted"), 2 * t_ + (f // 4 + 1))
                    for n, (h, w) in enumerate(((hid_h, w2high), (hid_h, w2low), (hid_l, w2high))):
                        last = mm(bank8(6 + k)[:, 0:D], h[:, k, f, :],
                                  w[:, bass.ds(e * FC + f, 1), :].rearrange("p a n -> p (a n)"),
                                  start=(f + n == 0), stop=(f == FC - 1 and n == 2))
                last.then_inc(sem("y_filled"), 1)

            pe.wait_ge(*ub.read(NG, "b21"))
            pe.wait_ge(*ub.read(NG, "hr1"))
            pe.wait_ge(sem("plan_ready"), 1)
            lay(0, 0)
            lay(1, 1)
            up(0, 0, True)
            up(1, 1, True)
            pe.wait_ge(sem("w2_parted"), NE - 2)
            pe.wait_ge(sem("w2_parted_by_pool"), 2)
            for t_ in range(2):
                if t_:
                    up(t_ + 1, 1 - t_)
                lay(t_ + 2, t_)
                down(t_, t_, True)
            with pe.Fori(1, (MT - 3) // 2) as j:
                for k in range(2):
                    up(2 * j + (k + 1), 1 - k)
                    lay(2 * j + (k + 2), k)
                    down(2 * j + k, k)
            for t_ in range(MT - 3, MT):
                if t_ + 1 < MT:
                    up(t_ + 1, (t_ + 1) % 2)
                if t_ + 2 < MT:
                    lay(t_ + 2, t_ % 2)
                down(t_, t_ % 2)

        @block.scalar
        def _(act):
            def acts(out, src, func, **kw):
                return nc.scalar.activation(out, src, func, **kw)

            for n, dst, name in W_A:
                act.dma_start(dst, kview(name)).then_inc(sem(f"{n}_loaded"), 16)

            def gelu(u, i, name, out, bias_col, func=ACT.Gelu, rows=P):
                act.wait_ge(*u.filled(i, name))
                u.done(acts(out, u.bank(name)[0:rows, :], func, bias=bias_col), name)

            def affine(u, i, name, out, g, b):
                act.wait_ge(*u.filled(i, name))
                u.done(acts(out, u.bank(name), ACT.Identity, bias=b, scale=g), name)

            def a_hid0(i):
                if isinstance(i, int):
                    act.wait_ge(sem("setup_read"), 1)
                for n, h, b in (("nr", hn, "L0_cond_b1_nr"), ("ts", ht, "L0_cond_b1_tsr")):
                    for c in range(2):
                        gelu(ua, i, f"{n}{c}", h[:, c, :], col(b, c))

            def a_hid1(i, chunks):
                for c in chunks:
                    gelu(ua, i, f"sr{c}", hs[:, c, :], col("L0_cond_b1_sr", c))

            def a_sr2(i, c):
                gelu(ua, i, f"su{c}", hs2[:, c, :], col("L0_cond_b2_sr", c))

            def a_x1(i):
                for c in range(2):
                    affine(ua, i, f"x1{c}", x1T[:, c, :], col("L0_cond_gamma", c), col("L0_cond_beta", c))

            def a_dn(i):
                gelu(ua, i, "dn", hd[:, :], col("L1_cond_down_b", parts=A1), rows=A1)

            def a_q(i):
                if isinstance(i, int):
                    act.wait_ge(sem("bq4_ready"), 1)
                for c in range(2):
                    act.wait_ge(*ua.filled(i, f"q{c}"))
                    ua.done(acts(qT[:, c, :], ua.bank(f"q{c}"), ACT.Identity, bias=bq4[:, c:c + 1], scale=HD ** -0.5), f"q{c}")

            def b_e(i, duo):
                for pr in range(2):
                    act.wait_ge(sem("centered"), half(i, duo, pr))
                    acts(sc[:, pr, :, :], sc[:, pr, :, :], ACT.Exp).then_inc(sem("exped"), 1)

            def b_t(i, duo):
                for k in (1, 3):
                    act.wait_ge(*ub.filled(i, f"pt{duo}{k}"))
                    ub.done(acts(pT[:, k, :], ub.bank(f"pt{duo}{k}"), ACT.Copy), f"pt{duo}{k}")

            def b_p(i, duo):
                act.wait_ge(*ub.filled(i, f"cx{duo}"))
                ub.done(acts(ctxT[:, :, duo * D:(duo + 1) * D], ub.bank(f"cx{duo}").rearrange("p (c n) -> p c n", c=2),
                             ACT.Copy), f"cx{duo}")

            def b_h3(i):
                for c in range(2):
                    act.wait_ge(*ub.filled(i, f"h3{c}"))
                    for out in (h3T, thigh):
                        last = acts(out[:, c, :], ub.bank(f"h3{c}"), ACT.Identity, bias=col("L2_cond_beta2", c),
                                    scale=col("L2_cond_g2", c))
                    ub.done(last, f"h3{c}")

            def b_f1(i, chunks):
                for f in chunks:
                    gelu(ub, i, f"f{f}", fT[:, f, :], col("L2_cond_b1", f), ACT.Gelu_apprx_sigmoid)

            def c_h4(i):
                for c in range(2):
                    affine(ub, i + 1, f"h4{c}", h4T[:, c, :], col("L3_cond_ln_g", c), col("L3_cond_ln_b", c))

            def c_hr(i):
                if not (isinstance(i, int) and i == 0):
                    act.wait_ge(sem("scattered"), 16 * TT * TOPK * i)
                for n in range(2):
                    act.wait_ge(*ub.filled(i + 1, f"hr{n}"))
                    for k in range(TOPK):
                        last = acts(hrow[:, 2 * n:2 * n + 2, k, 0:D], ub.bank(f"hr{n}").rearrange("p (a d) -> p a d", a=2),
                                    ACT.Copy)
                    ub.done(last, f"hr{n}")

            def c_ge(i):
                act.wait_ge(sem("gate_diff"), i + 1)
                acts(ge[:, :], gd[:, :], ACT.Exp).then_inc(sem("gate_exp"), 1)

            steps = {"A.hid0": a_hid0, "A.hid1a": lambda i: a_hid1(i, (0, 1)),
                     "A.hid1b": lambda i: a_hid1(i, (2, 3)), "A.sr2a": lambda i: a_sr2(i, 0),
                     "A.sr2b": lambda i: a_sr2(i, 1), "A.x1": a_x1, "A.dn": a_dn, "A.q": a_q,
                     "B.e0": lambda i: b_e(i, 0), "B.e1": lambda i: b_e(i, 1), "B.p0": lambda i: b_p(i, 0),
                     "B.p1": lambda i: b_p(i, 1), "B.t0": lambda i: b_t(i, 0), "B.t1": lambda i: b_t(i, 1),
                     "B.h3": b_h3,
                     **{f"B.f1{n}": (lambda i, k=k: b_f1(i, (2 * k, 2 * k + 1))) for k, n in enumerate("abcd")}, "C.h4": c_h4, "C.hr": c_hr, "C.ge": c_ge}

            def setup_ada():
                act.wait_ge(sem("angle_ready"), 1)
                acts(scr(8, 2 * B), scr(0, 2 * B), ACT.Sin).then_inc(sem("sin_done"), 1)
                act.wait_ge(sem("sin_done"), 1)
                acts(scr(10, 2 * B), scr(8, 2 * B), ACT.Exp, scale=-1.0).then_inc(sem("silu_exp"), 1)

            def setup_sty():
                act.wait_ge(sem("abs_ready"), 1)
                acts(scr(12, 2 * B), scr(12, 2 * B), ACT.Exp, scale=-1.0).then_inc(sem("sp_exp"), 1)
                act.wait_ge(sem("sp_exp"), 1)
                acts(scr(14, 2 * B), scr(12, 2 * B), ACT.Ln, bias=1.0).then_inc(sem("sp_ln"), 1)

            def high(w, whole):
                acts(w[0], whole, ACT.Copy).then_inc(sem("w_high"), 1)

            def setup_w1():
                for n, w, whole in (("w1nr", w1nr, raw(0, D)), ("w1ts", w1ts, raw(2, D)), ("w1sr", w1sr, raw(4, 2 * D))):
                    act.wait_ge(sem(f"{n}_loaded"), 16)
                    high(w, whole)
                act.wait_ge(sem("w_split"), 3)
                act.dma_start(raw(0, FF), kview("L2_cond_W1")).then_inc(sem("wf1_loaded"), 16)

            def setup_l2():
                act.wait_ge(sem("l2_loaded"), 16 * len(W_L2))
                high(wq, raw_qk[0])
                high(wk, raw_qk[1])
                act.wait_ge(sem("wf1_loaded"), 16)
                high(wf1, raw(0, FF))

            setup = {"A.sr2b": setup_ada, "A.dn": setup_l2, "A.v1": setup_sty}
            setup_w1()
            for s in ORDER:
                if s in steps and s[0] == "A":
                    steps[s](0)
                if s in setup:
                    setup[s]()
            rounds(steps, 1, "AB")
            rounds(steps, 2)
            with act.Fori(3, NG) as i:
                rounds(steps, i)
            rounds(steps, NG, "BC")

            def high2():
                act.wait_ge(sem("w2_loaded"), 16 * NE)
                for e in range(NE):
                    acts(w2high[:, e * FC:(e + 1) * FC, :], w2all[:, e * FC:(e + 1) * FC, :], ACT.Copy)\
                        .then_inc(sem("w2_high"), 1)

            rounds(steps, NG + 1, "C", {"C.h4": high2})

            bank8 = lambda k: (PA if k < 4 else PB)[:, k % 4, :]

            def relu(t_, k, first=False):
                act.wait_ge(sem("b1_ready"), t_ + 1)
                if not first:
                    act.wait_ge(sem("hid_parted"), 2 * (t_ - 1))
                for h in range(2):
                    act.wait_ge(sem("g1_filled"), 2 * t_ + (h + 1))
                    for f in range(4 * h, 4 * h + 4):
                        last = acts(hid[:, k, f, :], bank8(2 + 2 * k + h)[:, (f % 4) * P:(f % 4 + 1) * P], ACT.Relu,
                                    bias=b1c[:, k, f:f + 1])
                    last.then_inc(sem(f"hid_done{h}"), 1)

            relu(0, 0, True)
            relu(1, 1, True)
            with act.Fori(1, (MT - 1) // 2) as j:
                for k in range(2):
                    relu(2 * j + k, k)
            relu(MT - 1, 0)
            for k in range(2):
                act.wait_ge(*added(k))
            copy_out(act, range(NG // 4, NG // 2))

        @block.vector
        def _(v):
            ts, tt, stt, cp = v.tensor_scalar, v.tensor_tensor, v.scalar_tensor_tensor, v.tensor_copy

            once = [0]

            def link(ins):
                once[0] += 1
                ins.then_inc(sem("dve_setup"), 1)
                v.wait_ge(sem("dve_setup"), once[0])

            def after(ins, name, value):
                ins.then_inc(sem(name), 1)
                wait_apart(v, sem(name), value)

            def stats(i, s, srcs, tag, eps, wait=None):
                for n in range(TT):
                    if wait:
                        wait(n)
                    last = v.bn_stats(st[s][:, n, :], srcs[n])
                after(last, f"{tag}_stats", i + 1)
                for n in range(TT):
                    last = v.bn_aggr(mv[s][:, n, :], st[s][:, n, :])
                after(last, f"{tag}_aggr", i + 1)
                ts(ve[s][:, :], mv[s][:, :, 1], eps, None, ALU.add).then_inc(sem(f"{tag}_var"), 1)

            def normalise(i, u, units, s, tag, out, eps, before=None):
                srcs = [u.bank(units[n // 2])[:, (n % 2) * D:(n % 2 + 1) * D] for n in range(TT)]

                def wait(n):
                    if n % 2 == 0:
                        v.wait_ge(*u.filled(i, units[n // 2]))
                stats(i, s, srcs, tag, eps, wait)
                if before:
                    before()
                v.wait_ge(sem(f"{tag}_rstd"), i + 1)
                for n in range(TT):
                    last = ts(out[:, n, :], srcs[n], mv[s][:, n, 0:1], rs[s][:, n:n + 1], ALU.subtract, ALU.mult)
                    if n % 2:
                        u.done(last, units[n // 2])

            def a_xT(i):
                for c in range(2):
                    v.wait_ge(*ua.filled(i, f"xT{c}"))
                    cp(thigh[:, c, :], ua.bank(f"xT{c}")).then_inc(sem("x_high"), 1)
                for c in range(2):
                    wait_apart(v, sem("x_high"), 2 * i + (c + 1))
                    ua.done(tt(tlow[:, c, :], ua.bank(f"xT{c}"), thigh[:, c, :].bitcast(F32), ALU.subtract), f"xT{c}")

            def a_out(i):
                v.wait_ge(sem("xb_ready"), i + 1)
                for c in range(2):
                    v.wait_ge(*ua.filled(i, f"y{c}"))
                    ua.done(tt(xT[:, c, :], ua.bank(f"y{c}"), xb[:, c, :], ALU.add), f"y{c}")

            def a_r0(i):
                normalise(i, ua, ["r00", "r01"], "A", "l0", nrow, EPS)

            def a_ex(i):
                v.wait_ge(*ua.filled(i, "ex"))
                ua.done(tt(by_seq(he[:, :]), by_seq(ua.bank("ex")[0:A1, :]), over_tokens(bsel1[:, part(i, GB)]), ALU.add), "ex")

            def a_up(i):
                for c in range(2):
                    v.wait_ge(*ua.filled(i, f"u{c}"))
                    ua.done(stt(x1T[:, c, :], ua.bank(f"u{c}"), col("L1_cond_up_b", c), x1T[:, c, :], ALU.add, ALU.add), f"u{c}")

            def a_r1(i):
                normalise(i, ua, ["r10", "r11"], "A", "l1", nrow, EPS)
                v.wait_ge(sem("x2_ready"), i + 1)
                stats(i, "A", [x2row[:, n, :] for n in range(TT)], "l2", EPS)
                v.wait_ge(sem("l2_rstd"), i + 1)
                for n in range(TT):
                    last = ts(nrow[:, n, :], x2row[:, n, :], mv["A"][:, n, 0:1], rs["A"][:, n:n + 1], ALU.subtract, ALU.mult)
                last.then_inc(sem("n2_ready"), 1)

            def a_x2(i):
                for c in range(2):
                    v.wait_ge(*ua.filled(i, f"x2{c}"))
                    ua.done(tt(by_seq(xmT[:, c, :]), by_seq(ua.bank(f"x2{c}")), over_tokens(ada[:, c, part(i, GB)]), ALU.mult), f"x2{c}")
                for c in range(2):
                    v.wait_ge(*ua.read(i, f"x2{c}"))
                    tt(by_seq(xmT[:, c, :]), by_seq(xmT[:, c, :]), over_tokens(ada[:, 2 + c, part(i, GB)]), ALU.add)\
                        .then_inc(sem("xm_whole"), 1)
                for c in range(2):
                    wait_apart(v, sem("xm_whole"), 2 * i + (c + 1))
                    cp(thigh[:, c, :], xmT[:, c, :]).then_inc(sem("xm_high"), 1)
                for c in range(2):
                    wait_apart(v, sem("xm_high"), 2 * i + (c + 1))
                    last = tt(tlow[:, c, :], xmT[:, c, :], thigh[:, c, :].bitcast(F32), ALU.subtract)
                last.then_inc(sem("xm_ready"), 1)

            def a_k(i):
                for c in range(2):
                    v.wait_ge(*ua.filled(i, f"k{c}"))
                    src = by_seq(ua.bank(f"k{c}"))
                    for j in range(2):
                        last = ts(kbd[:, c, :, j, :], src, col("L2_cond_bk", c), head_half[:, j:j + 1], ALU.add, ALU.mult)
                    ua.done(last, f"k{c}")

            def a_v(i, units):
                for n in units:
                    v.wait_ge(*ua.filled(i, f"v{n}"))
                    for j in range(2):
                        rows = slice(j * S, (j + 1) * S)
                        src = ua.bank(f"v{n}")[rows, :].rearrange("p (b a j d) -> p b a j d", b=2, j=2, d=HD)[:, :, :, j, :]
                        bv = bvrow[rows, :].rearrange("p (a j d) -> p a j d", j=2, d=HD)[:, :, j, :]
                        b0, b1 = (b + j for b in v_seqs(n))
                        if b1 < GB:
                            last = tt(vbd[rows, b0:b1 + 1:2, :, j * HD:(j + 1) * HD], src,
                                      bv.unsqueeze(1).broadcast_to([S, 2, H // 2, HD]), ALU.add)
                        else:
                            for h, b in enumerate((b0, 0)):
                                last = tt(vbd[rows, b, :, j * HD:(j + 1) * HD], src[:, h], bv, ALU.add)
                    ua.done(last, f"v{n}")

            def b_s(i, duo):
                v.wait_ge(sem("bias_masked"), 2 * i + (duo + 1))
                v.wait_ge(*ub.filled(i, f"sc{duo}"))
                nat = lambda a: a.rearrange("p (c r j) k -> p r c (j k)", c=2, r=4)
                for pr in range(2):
                    last = tt(nat(sc[:, pr, :, :]), PB[:, :, pr * D:(pr + 1) * D].rearrange("p r (c x) -> p r c x", c=2),
                              nat(bias[:, duo, pr, :, :]), ALU.add)
                    if pr == 0:
                        last.then_inc(sem("half_added"), 1)
                ub.done(last, f"sc{duo}")
                v.wait_ge(sem("half_added"), 2 * i + (duo + 1))
                v.reduce_max(smx[:, 0, :], sc[:, 0, :, :], axis=AX.X).then_inc(sem("scored"), 1)
                v.wait_ge(*ub.read(i, f"sc{duo}"))
                v.reduce_max(smx[:, 1, :], sc[:, 1, :, :], axis=AX.X).then_inc(sem("scored"), 1)

            def b_m(i, duo):
                for pr in range(2):
                    v.wait_ge(sem("exped"), half(i, duo, pr))
                    v.reduce_sum(ssum[:, pr, :], sc[:, pr, :, :], axis=AX.X).then_inc(sem("summed"), 1)
                    wait_apart(v, sem("summed"), half(i, duo, pr))
                    v.reciprocal(rsum[:, pr, :], ssum[:, pr, :]).then_inc(sem("rsum_ready"), 1)

            def b_t(i, duo):
                for k in (0, 2):
                    v.wait_ge(*ub.filled(i, f"pt{duo}{k}"))
                    ub.done(cp(pT[:, k, :], ub.bank(f"pt{duo}{k}")), f"pt{duo}{k}")

            def b_o(i):
                for c in range(2):
                    v.wait_ge(*ub.filled(i, f"o{c}"))
                    ub.done(stt(x3T[:, c, :], ub.bank(f"o{c}"), col("L2_cond_bo", c), xmT[:, c, :], ALU.add, ALU.add), f"o{c}")

            def b_r2(i):
                normalise(i, ub, ["r20", "r21"], "B", "l3", n3row, EPS)

            def b_h3(i):
                for c in range(2):
                    wait_apart(v, *ub.read(i, f"h3{c}"))
                    last = tt(tlow[:, c, :], h3T[:, c, :], thigh[:, c, :].bitcast(F32), ALU.subtract)
                last.then_inc(sem("h3_split"), 1)

            def b_f2(i, c):
                v.wait_ge(*ub.filled(i, f"g{c}"))
                ub.done(stt(x3T[:, c, :], ub.bank(f"g{c}"), col("L2_cond_b2", c), x3T[:, c, :], ALU.add, ALU.add), f"g{c}")

            def b_r3(i):
                def keep():
                    if not (isinstance(i, int) and i == 0):
                        wait_apart(v, sem("x_stored"), 16 * i)
                    for k in range(2):
                        last = cp(xres[:, 2 * k:2 * k + 2, :], ub.bank(f"r3{k}").rearrange("p (a d) -> p a d", a=2))
                    last.then_inc(sem("xres_ready"), 1)
                normalise(i, ub, ["r30", "r31"], "B", "l4", n4row, EPS, keep)

            def c_tok(i):
                for c in range(2):
                    v.wait_ge(*ub.read(i + 1, f"h4{c}"))
                    for b in range(GB):
                        last = v.bn_stats(st4[:, c, b, :], h4T[:, c, b * S:(b + 1) * S])
                after(last, "t_stats", i + 1)
                f = lambda k: st4[:, :, :, k]
                tt(tst["sum"][:, :, :], f(1), f(4), ALU.add)
                tt(tst["dif"][:, :, :], f(1), f(4), ALU.subtract)
                after(tt(tst["var"][:, :, :], f(2), f(5), ALU.add), "t_halves", i + 1)
                tt(tst["sq"][:, :, :], tst["dif"][:, :, :], tst["dif"][:, :, :], ALU.mult)
                after(ts(tst["var"][:, :, :], tst["var"][:, :, :], 1.0 / S, EPS_T, ALU.mult, ALU.add), "t_within", i + 1)
                stt(tst["var"][:, :, :], tst["sq"][:, :, :], 0.25, tst["var"][:, :, :], ALU.mult, ALU.add)\
                    .then_inc(sem("t_var"), 1)

            def c_hf(i):
                v.wait_ge(sem("t_rstd"), i + 1)
                after(tt(tst["mul"][:, :, :], tst["rstd"][:, :, :], sty[:, 0:2, part(i, GB)], ALU.mult), "t_mul", i + 1)
                after(stt(tst["mm"][:, :, :], tst["sum"][:, :, :], 0.5, tst["mul"][:, :, :], ALU.mult, ALU.mult), "t_mm", i + 1)
                tt(tst["add"][:, :, :], sty[:, 2:4, part(i, GB)], tst["mm"][:, :, :], ALU.subtract)
                for c in range(2):
                    last = tt(by_seq(hfT[:, c, :]), by_seq(h4T[:, c, :]), over_tokens(tst["mul"][:, c, :]), ALU.mult)
                after(last, "t_scaled", i + 1)
                for c in range(2):
                    last = tt(by_seq(hfT[:, c, :]), by_seq(hfT[:, c, :]), over_tokens(tst["add"][:, c, :]), ALU.add)
                last.then_inc(sem("hf_ready"), 1)

            def c_lg(i):
                v.wait_ge(*ub.filled(i + 1, "lg"))
                ub.done(cp(lgs[:, :, :], ub.bank("lg")[:, 0:TT * NE].rearrange("p (n e) -> p n e", e=NE)), "lg")
                wait_apart(v, *ub.read(i + 1, "lg"))
                for n in range(TT):
                    last = v.max(mx8[:, n, :], lgs[:, n, :])
                after(last, "top_values", i + 1)
                for n in range(TT):
                    last = v.max_index(mi8[:, n, :], mx8[:, n, :], lgs[:, n, :])
                tt(gd[:, :], mx8[:, :, 1], mx8[:, :, 0], ALU.subtract).then_inc(sem("gate_diff"), 1)
                v.wait_ge(sem("gate_diff"), i + 1)
                after(cp(mif[:, :, :], mi8[:, :, 0:TOPK]), "top_index", i + 1)
                for k in range(TOPK):
                    last = tt(oh[:, k, :, :], iot[:, 0:NE].unsqueeze(1).broadcast_to([P, TT, NE]),
                              mif[:, :, k:k + 1].broadcast_to([P, TT, NE]), ALU.is_equal)
                after(last, "onehots", i + 1)
                tt(picked[:, :, :], oh[:, 0, :, :], oh[:, 1, :, :], ALU.add).then_inc(sem("picked_ready"), 1)

            def c_ge(i):
                wait_apart(v, sem("gate_exp"), i + 1)
                after(ts(gp[:, :], ge[:, :], 1.0, None, ALU.add), "gate_sum", i + 1)
                after(v.reciprocal(gp[:, :], gp[:, :]), "gate_recip", i + 1)
                after(tt(gd[:, :], gp[:, :], ge[:, :], ALU.mult), "gate_second", i + 1)
                if not (isinstance(i, int) and i == 0):
                    wait_apart(v, sem("scattered"), 16 * TT * TOPK * i)
                for k, a in enumerate((gp, gd)):
                    cp(hrow[:, :, k, D:D + 1], tok[:, :].unsqueeze(2))
                    cp(hrow[:, :, k, D + 1:DX], a[:, :].unsqueeze(2))
                after(ts(tok[:, :], tok[:, :], float(GT), None, ALU.add), "tok_moved", i + 1)
                for k, a in enumerate((gp, gd)):
                    last = tt(cm[:, k, :, :], oh[:, k, :, :], a[:, :].unsqueeze(2).broadcast_to([P, TT, NE]), ALU.mult)
                after(last, "gates_placed", i + 1)
                tt(cmix[:, :, :], cm[:, 0, :, :], cm[:, 1, :, :], ALU.add).then_inc(sem("cmix_ready"), 1)

            def c_rk(i):
                v.wait_ge(*ub.filled(i + 1, "rk"))
                bank = ub.bank("rk")
                last = tt(pos[:, :, :], bank[:, 0:TT * NE].rearrange("p (n e) -> p n e", e=NE),
                          base[:, :].unsqueeze(1).broadcast_to([P, TT, NE]), ALU.add)
                after(last, "ranked", i + 1)
                ub.done(tt(base[:, :], bank[:, TT * NE:(TT + 1) * NE], base[:, :], ALU.add), "rk")
                for k in range(TOPK):
                    last = tt(posk[:, k, :, :], oh[:, k, :, :], pos[:, :, :], ALU.mult)
                after(last, "rank_picked", i + 1)
                for k in range(TOPK):
                    last = v.reduce_sum(slot[:, :, k], posk[:, k, :, :], axis=AX.X)
                after(last, "slots", i + 1)
                if not (isinstance(i, int) and i == 0):
                    wait_apart(v, sem("scattered"), 16 * TT * TOPK * i)
                cp(idx[:, :, :], slot[:, :, :]).then_inc(sem("idx_ready"), 1)

            def c_ct(i):
                v.wait_ge(*ub.filled(i + 1, "ct"))
                ub.done(cp(ctT, ub.bank("ct")[0:NE, :]), "ct")

            def c_b2(i):
                v.wait_ge(sem("xres_ready"), i + 1)
                for k in range(2):
                    v.wait_ge(*ub.filled(i + 1, f"b2{k}"))
                    x = xres[:, 2 * k:2 * k + 2, :]
                    ub.done(tt(x, ub.bank(f"b2{k}").rearrange("p (a d) -> p a d", a=2), x, ALU.add), f"b2{k}")

            steps = {"A.xT": a_xT, "A.out": a_out, "A.r0": a_r0, "A.ex": a_ex, "A.up": a_up, "A.r1": a_r1,
                     "A.x2": a_x2,
                     "A.k": a_k, "A.v0": lambda i: a_v(i, (0, 1)), "A.v1": lambda i: a_v(i, (2, 3)),
                     "B.s0": lambda i: b_s(i, 0), "B.s1": lambda i: b_s(i, 1), "B.m0": lambda i: b_m(i, 0),
                     "B.m1": lambda i: b_m(i, 1), "B.t0": lambda i: b_t(i, 0), "B.t1": lambda i: b_t(i, 1),
                     "B.o": b_o,
                     "B.r2": b_r2, "B.h3": b_h3, "B.f2a": lambda i: b_f2(i, 0),
                     "B.f2b": lambda i: b_f2(i, 1), "B.r3": b_r3,
                     "C.tok": c_tok, "C.hf": c_hf, "C.lg": c_lg, "C.ge": c_ge, "C.rk": c_rk, "C.ct": c_ct, "C.b2": c_b2}

            v.memset(vec, 0.0).then_inc(sem("vec_cleared"), 1)
            v.memset(mhalf[:, :], -0.5).then_inc(sem("mhalf_ready"), 1)
            v.memset(ones[:, :], 1.0)
            v.memset(vbd, 0.0)
            v.wait_ge(sem("iota_ready"), 1)
            cp(pidx[:, :], pidx_i[:, 0:1])
            link(ts(pidx_i[:, 1:2], pidx_i[:, 0:1], 4, 1, ALU.logical_shift_right, ALU.bitwise_and))
            link(cp(head_half[:, 1:2], pidx_i[:, 1:2]))
            link(ts(head_half[:, 0:1], head_half[:, 1:2], -1.0, 1.0, ALU.mult, ALU.add))

            def setup_cols():
                v.wait_ge(sem("ints_loaded"), 64)
                ts(eoff[:, :], iot[:, 0:NE], float(CAP), None, ALU.mult)
                ts(base[:, :], iot[:, 0:NE], float(CAP), None, ALU.mult)
                ts(tok[:, :], iot[:, 0:TT], float(P), pidx[:, 0:1], ALU.mult, ALU.add)
                link(cp(idf, ints))
                for k in range(3):
                    last = ts(mcond[:, k, :], idf[:, 0, :], float(k), None, ALU.is_equal)
                last.then_inc(sem("mcond_ready"), 1)
                v.wait_ge(sem("mcond_ready"), 1)
                v.wait_ge(sem("setup_filled"), 1)
                cp(colv[:, :], PB[:, 0, 0:NROWS]).then_inc(sem("setup_read"), 1)
                v.wait_ge(sem("setup_read"), 1)
                ts(bq4[:, :], colv[:, ROW["L2_cond_bq"]:ROW["L2_cond_bq"] + 2], HD ** -0.5, None, ALU.mult)\
                    .then_inc(sem("bq4_ready"), 1)
                for c in range(2):
                    last = ts(bsel0[:, c, :], mcond[:, 0, :], col("L0_cond_b2_nr", c), None, ALU.mult)
                link(last)
                for k, name in ((1, "L0_cond_b2_tsr"), (2, "L0_cond_b3_sr")):
                    for c in range(2):
                        last = stt(bsel0[:, c, :], mcond[:, k, :], col(name, c), bsel0[:, c, :], ALU.mult, ALU.add)
                    last.then_inc(sem("bsel0_ready"), 1)
                    v.wait_ge(sem("bsel0_ready"), k)

            def setup_l1():
                clip = scr(16)
                ts(clip, idf[:, 1, :], 0.0, float(ND - 1), ALU.max, ALU.min)
                link(ts(scr(17), idf[:, 3, :], 0.0, float(NSUB - 1), ALU.max, ALU.min))
                ts(sce[:, 0, 0:B], idf[:, 1, :], pidx[:, 0:1], None, ALU.is_equal)
                ts(sce[:, 1, 0:B], clip, pidx[:, 0:1], None, ALU.is_equal)
                ts(sce[:, 2, 0:B], scr(17), pidx[:, 0:1], None, ALU.is_equal).then_inc(sem("onehot_ready"), 1)
                link(tt(scr(18), clip, idf[:, 1, :], ALU.is_equal))
                link(ts(scr(19), clip, -float(ND), None, ALU.add))
                link(tt(scr(18), scr(18), scr(19), ALU.mult))
                link(ts(scr(18), scr(18), float(ND), None, ALU.add))
                cp(widx[:, :], scr(18)[0:1, :]).then_inc(sem("widx_ready"), 1)
                v.wait_ge(sem("setup_filled"), 3)
                cp(eb1[:, :], PB[:, 1, 0:NE * FC])
                cp(downT[:, :, :], PB[:, 1, P:2 * P].rearrange("p (k a) -> p k a", k=2))
                cp(upT[:, :], PB[0:A1, 1, 2 * P:4 * P]).then_inc(sem("setup_read"), 1)
                v.wait_ge(sem("setup_filled"), 4)
                cp(expT[:, 0:ND, :], PB[0:A1, 2:4, :].rearrange("p a (b c) -> p (a b) c", c=A1))
                cp(expT[:, ND, :], ident[0:A1, 0:A1]).then_inc(sem("setup_read"), 1)
                v.wait_ge(sem("setup_filled"), 5)
                cp(bsel1[:, :], PB[0:A1, 0, P:P + B]).then_inc(sem("setup_read"), 1)

            def setup_angles():
                link(ts(scr(20), idf[:, 2, :], 0.01, 4000.0, ALU.mult, ALU.mult))
                link(ts(scr(21), scr(20), col("freqs"), None, ALU.mult))
                ts(scr(22), scr(21), INV2PI, MAGIC, ALU.mult, ALU.add)
                link(ts(scr(23), scr(21), INV2PI, 0.25, ALU.mult, ALU.add))
                link(ts(scr(23), scr(23), MAGIC, None, ALU.add))
                link(ts(scr(22, 2 * B), scr(22, 2 * B), MAGIC, None, ALU.subtract))
                both = lambda k: scr(k, 2 * B).rearrange("p (a b) -> p a b", a=2)
                two = scr(21).unsqueeze(1).broadcast_to([P, 2, B])
                link(stt(both(0), both(22), -C1, two, ALU.mult, ALU.add))
                link(stt(both(0), both(22), -C2, both(0), ALU.mult, ALU.add))
                link(ts(scr(1), scr(1), PI / 2, None, ALU.add))
                link(stt(both(0), both(22), -C3, both(0), ALU.mult, ALU.add))
                ts(scr(0, 2 * B), scr(0, 2 * B), -3.1415925, 3.1415925, ALU.max, ALU.min)\
                    .then_inc(sem("angle_ready"), 1)
                v.wait_ge(sem("mask_loaded"), 32)
                ts(mneg[:, :, :], mask8[:, :, :], NEG, None, ALU.mult).then_inc(sem("mneg_ready"), 1)

            def setup_ada():
                v.wait_ge(sem("silu_exp"), 1)
                link(ts(scr(10, 2 * B), scr(10, 2 * B), 1.0, None, ALU.add))
                link(v.reciprocal(scr(10, 2 * B), scr(10, 2 * B)))
                tt(scr(2, 2 * B), scr(8, 2 * B), scr(10, 2 * B), ALU.mult).then_inc(sem("emb_ready"), 1)
                v.wait_ge(sem("setup_filled"), 6)
                for m in range(4):
                    last = ts(ada[:, m, :], PB[:, 1, m * B:(m + 1) * B], col("L2_cond_b_ada", m), 1.0 if m < 2 else 0.0,
                              ALU.add, ALU.add)
                last.then_inc(sem("setup_read"), 1)

            def setup_sty(n):
                v.wait_ge(sem("setup_filled"), 7 + n)
                if n == 0:
                    last = cp(scr(4)[0:SE, :], PB[0:SE, 2, 0:B])
                if n == 1:
                    last = ts(scr(5), PB[:, 2, 0:B], col("L3_cond_hyp_b1"), 0.0, ALU.add, ALU.max)
                if n == 2:
                    last = ts(scr(6), PB[:, 2, 0:B], col("L3_cond_hyp_b2"), None, ALU.add)
                if n == 3:
                    last = ts(scr(7)[0:SE, :], PB[0:SE, 2, 0:B], col("L3_cond_sty_b1", parts=SE), 0.0, ALU.add, ALU.max)
                if n < 4:
                    last.then_inc(sem("sty_step"), 1)
                    return
                for m in range(4):
                    last = ts(sty[:, m, :], PB[:, 3, m * B:(m + 1) * B], col("L3_cond_sty_b2", m), None, ALU.add)
                last.then_inc(sem("setup_read"), 1)
                v.wait_ge(sem("setup_read"), 6)
                g = sty[:, 0:2, :].rearrange("p a b -> p (a b)")
                link(ts(scr(12, 2 * B), g, -1.0, None, ALU.mult))
                tt(scr(12, 2 * B), scr(12, 2 * B), g, ALU.max).then_inc(sem("abs_ready"), 1)
                v.wait_ge(sem("sp_ln"), 1)
                link(stt(g, g, 0.0, scr(14, 2 * B), ALU.max, ALU.add))
                ts(g, g, 1e-8, None, ALU.add).then_inc(sem("setup_read"), 1)
                v.wait_ge(sem("setup_read"), 7)

            def low(w, whole, n):
                v.wait_ge(sem("w_high"), n)
                tt(w[1], whole, w[0].bitcast(F32), ALU.subtract).then_inc(sem("w_split"), 1)

            def setup_first():
                for n, (w, whole) in enumerate(((w1nr, raw(0, D)), (w1ts, raw(2, D)), (w1sr, raw(4, 2 * D)))):
                    low(w, whole, n + 1)
                setup_cols()
                setup_l1()

            def setup_l2():
                for n, (w, whole) in enumerate(((wq, raw_qk[0]), (wk, raw_qk[1]), (wf1, raw(0, FF)))):
                    low(w, whole, n + 4)

            setup = {"A.xT": setup_first, "A.up": setup_l2, "A.hid0": setup_angles, "A.sr2b": setup_ada,
                     "A.out": lambda: setup_sty(0),
                     "A.r0": lambda: setup_sty(1), "A.x1": lambda: setup_sty(2), "A.ex": lambda: setup_sty(3),
                     "A.v1": lambda: setup_sty(4)}
            v.wait_ge(sem("ident_ready"), 1)
            for s in ORDER:
                if s in steps and s[0] == "A":
                    if s == "A.ex" or s == "A.v0":
                        v.wait_ge(sem("rows_loaded"), 48)
                    steps[s](0)
                if s in setup:
                    setup[s]()
            rounds(steps, 1, "AB")
            rounds(steps, 2)
            with v.Fori(3, NG) as i:
                rounds(steps, i)
            rounds(steps, NG, "BC")

            def low2(e):
                part_e = slice(e * FC, (e + 1) * FC)
                v.wait_ge(sem("w2_high"), e + 1)
                tt(w2low[:, part_e, :], w2all[:, part_e, :], w2high[:, part_e, :].bitcast(F32), ALU.subtract)\
                    .then_inc(sem("w2_parted"), 1)

            rounds(steps, NG + 1, "C", {"C.tok": lambda: low2(0), "C.hf": lambda: low2(1), "C.lg": lambda: low2(2)})

            v.wait_ge(*ub.read(NG, "rk"))
            link(v.memset(zrow, 0.0))
            ts(zrow[:, D:D + 1], pidx[:, 0:1], float(B * S), None, ALU.add)
            cp(padi[:, :], base[:, :]).then_inc(sem("pads_ready"), 1)
            link(tt(cnt[:, :], base[:, :], eoff[:, :], ALU.subtract))
            n8, incl = pl8["n"][:, :], pl8["incl"][:, :]
            v.memset(pl8["one"][:, :], 1.0)
            link(ts(n8, cnt[:, :], float(P - 1), 1.0 / P, ALU.add, ALU.mult))
            link(ts(n8, n8, -255.0 / 512, MAGIC, ALU.add, ALU.add))
            link(ts(n8, n8, MAGIC, None, ALU.subtract))
            link(v.tensor_tensor_scan(incl, pl8["one"][:, :], n8, 0.0, ALU.mult, ALU.add))
            tile = iot[:, :]
            e, start, idle, src = (plan[k] for k in ("e", "start", "idle", "src"))
            seven = lambda a: a[:, 0:NE - 1].unsqueeze(1).broadcast_to([P, MTP, NE - 1])
            ge7 = pge[:, :, 0:NE - 1]
            link(tt(ge7, tile.unsqueeze(2).broadcast_to([P, MTP, NE - 1]), seven(pl8["incl"][:, :]), ALU.is_ge))
            link(v.reduce_sum(e, ge7, axis=AX.X))
            link(tt(ge7, ge7, seven(pl8["n"][:, :]), ALU.mult))
            link(v.reduce_sum(start, ge7, axis=AX.X))
            link(tt(start, tile, start, ALU.subtract))
            link(ts(src, e, float(CAP), None, ALU.mult))
            link(stt(src, start, float(P), src, ALU.mult, ALU.add))
            link(ts(idle, tile, pl8["incl"][:, NE - 1:NE], None, ALU.is_ge))
            link(stt(idle, src, base[:, NE - 1:NE], idle, ALU.subtract, ALU.mult))
            link(tt(src, src, idle, ALU.subtract))
            cp(meta[:, 0, :], e)
            cp(meta[:, 1, :], src).then_inc(sem("plan_ready"), 1)
            for e in range(3, NE - 2):
                low2(e)

            bank8 = lambda k: (PA if k < 4 else PB)[:, k % 4, :]

            def turn(t_, k, first=False):
                v.wait_ge(sem("xsT_filled"), t_ + 1)
                if not first:
                    v.wait_ge(sem("g1_filled"), 2 * (t_ - 1))
                cp(xsT[:, k, :], bank8(k)[:, 0:D]).then_inc(sem("xsT_copied"), 1)
                cp(info[:, part(t_, 1), :], xs[:, k:k + 1, D:DX]).then_inc(sem("info_kept"), 1)

            def part_hid(t_, k, first=False):
                if not first:
                    wait_apart(v, sem("y_filled"), t_ - 1)
                for h in range(2):
                    at = slice(4 * h, 4 * h + 4)
                    wait_apart(v, sem(f"hid_done{h}"), t_ + 1)
                    cp(hid_h[:, k, at, :], hid[:, k, at, :]).then_inc(sem("hid_high"), 1)
                for h in range(2):
                    at = slice(4 * h, 4 * h + 4)
                    wait_apart(v, sem("hid_high"), 2 * t_ + (h + 1))
                    tt(hid_l[:, k, at, :], hid[:, k, at, :], hid_h[:, k, at, :].bitcast(F32), ALU.subtract)\
                        .then_inc(sem("hid_parted"), 1)

            def take(t_, k, first=False):
                wait_apart(v, sem("y_filled"), t_ + 1)
                if not first:
                    v.wait_ge(sem(f"added{k}"), 8 * (t_ - k))
                v.wait_ge(sem("info_kept"), t_ + 1)
                ts(ys[:, k, :], bank8(6 + k)[:, 0:D], info[:, part(t_, 1), 1:2].rearrange("p a b -> p (a b)"), None, ALU.mult)\
                    .then_inc(sem("y_copied"), 1)

            turn(0, 0, True)
            turn(1, 1, True)
            part_hid(0, 0, True)
            for t_ in range(2):
                turn(t_ + 2, t_)
                part_hid(t_ + 1, 1 - t_, t_ == 0)
                take(t_, t_, True)
            with v.Fori(1, (MT - 3) // 2) as j:
                for k in range(2):
                    turn(2 * j + (k + 2), k)
                    part_hid(2 * j + (k + 1), 1 - k)
                    take(2 * j + k, k)
            for t_ in range(MT - 3, MT):
                if t_ + 2 < MT:
                    turn(t_ + 2, t_ % 2)
                if t_ + 1 < MT:
                    part_hid(t_ + 1, (t_ + 1) % 2)
                take(t_, t_ % 2)

        @block.gpsimd
        def _(g):
            g.memset(ident[:, :], 0.0).then_inc(sem("pool_setup"), 1)
            g.memset(upper[:, :], 1.0).then_inc(sem("pool_setup"), 1)
            g.wait_ge(sem("pool_setup"), 2)
            g.affine_select(out=ident[:, :], in_=ident[:, :], compare_op=ALU.not_equal, fill=1.0, base=0,
                            pattern=[[-1, P]], channel_multiplier=1).then_inc(sem("ident_ready"), 1)
            g.affine_select(out=upper[:, :], in_=upper[:, :], compare_op=ALU.is_gt, fill=0.0, base=0,
                            pattern=[[1, P]], channel_multiplier=-1).then_inc(sem("upper_ready"), 1)
            g.iota(pidx_i[:, 0:1], [[1, 1]], base=0, channel_multiplier=1)
            g.iota(iot[:, :], [[1, MTP]], base=0, channel_multiplier=0, allow_small_or_imprecise_dtypes=True)\
                .then_inc(sem("iota_ready"), 1)

            g.wait_ge(sem("vec_cleared"), 1)
            load_vecs(g, NVEC_SP, NVEC, "vec_loaded_by_pool")

            def rstd(s, i, tag):
                g.wait_ge(sem(f"{tag}_var"), i + 1)
                g.tensor_tensor(rs[s][:, :], ve[s][:, :], mhalf[:, 0:TT], ALU.pow).then_inc(sem(f"{tag}_rstd"), 1)

            def masked(i, ap, k):
                return g.tensor_tensor(by_seq(ap), by_seq(ap), over_tokens(mcond[:, k, part(i, GB)]), ALU.mult)

            def a_xb(i):
                if isinstance(i, int):
                    g.wait_ge(sem("bsel0_ready"), 2)
                wait_apart(g, *ua.read(i, "xT1"))
                for c in range(2):
                    g.tensor_tensor(xb[:, c, :], thigh[:, c, :].bitcast(F32), tlow[:, c, :].bitcast(F32), ALU.add)\
                        .then_inc(sem("x_whole"), 1)
                for c in range(2):
                    wait_apart(g, sem("x_whole"), 2 * i + (c + 1))
                    last = g.tensor_tensor(by_seq(xb[:, c, :]), by_seq(xb[:, c, :]), over_tokens(bsel0[:, c, part(i, GB)]), ALU.add)
                last.then_inc(sem("xb_ready"), 1)

            def a_mask0(i):
                for name, h, k in (("nr", hn, 0), ("ts", ht, 1)):
                    for c in range(2):
                        wait_apart(g, *ua.read(i, f"{name}{c}"))
                        last = masked(i, h[:, c, :], k)
                last.then_inc(sem("hidden_masked"), 1)

            def a_mask1(i):
                for c in range(2):
                    wait_apart(g, *ua.read(i, f"su{c}"))
                    last = masked(i, hs2[:, c, :], 2)
                last.then_inc(sem("hidden_masked"), 1)

            def a_wsel(i):
                if isinstance(i, int):
                    g.wait_ge(sem("widx_ready"), 1)
                    g.wait_ge(sem("setup_read"), 3)
                else:
                    g.wait_ge(*ua.filled(i - 1, "ex"))
                for b in range(GB):
                    e = g.value_load(widx[0:1, part(i, GB, b, 1)], min_val=0, max_val=ND)
                    last = g.tensor_copy(wsel[:, b:b + 1, :], expT[:, bass.ds(e, 1), :])
                last.then_inc(sem("wsel_ready"), 1)

            def a_r1(i):
                rstd("A", i, "l1")
                g.wait_ge(*ua.read(i, "r11"))
                wide = lambda r: r[:, :].unsqueeze(1).broadcast_to([P, TT, D])
                g.tensor_tensor(x2row, nrow, wide(g1row), ALU.mult).then_inc(sem("x2_scaled"), 1)
                g.wait_ge(sem("x2_scaled"), i + 1)
                g.tensor_tensor(x2row, x2row, wide(be1row), ALU.add).then_inc(sem("x2_ready"), 1)
                rstd("A", i, "l2")

            def bias_mask(i, duo):
                wait_apart(g, sem(f"bias_loaded{duo}"), 64 * i + 64)
                for pr in range(2):
                    m = mneg[:, part(i, TT, 2 * duo + pr, 1), :]
                    last = g.tensor_tensor(bias[:, duo, pr, :, :], bias[:, duo, pr, :, :], m.broadcast_to([P, H, S]), ALU.add)
                last.then_inc(sem("bias_masked"), 1)

            def b_s(i, duo):
                for pr in range(2):
                    g.wait_ge(sem("scored"), half(i, duo, pr))
                    wide = smx[:, pr, :].unsqueeze(2).broadcast_to([P, H, S])
                    g.tensor_tensor(sc[:, pr, :, :], sc[:, pr, :, :], wide, ALU.subtract)\
                        .then_inc(sem("centered"), 1)

            def b_m(i, duo):
                for pr in range(2):
                    g.wait_ge(sem("rsum_ready"), half(i, duo, pr))
                    wide = rsum[:, pr, :].unsqueeze(2).broadcast_to([P, H, S])
                    g.tensor_tensor(sc[:, pr, :, :], sc[:, pr, :, :], wide, ALU.mult)\
                        .then_inc(sem("probs_ready"), 1)

            def c_tok(i):
                g.wait_ge(sem("t_var"), i + 1)
                f = lambda k: tst[k][:, :, :].rearrange("p a b -> p (a b)")
                g.tensor_tensor(f("rstd"), f("var"), mhalf[:, :], ALU.pow).then_inc(sem("t_rstd"), 1)

            def c_scat(i):
                wait_apart(g, *ub.read(i + 1, "hr1"))
                g.wait_ge(sem("idx_ready"), i + 1)
                for n in range(TT):
                    for k in range(TOPK):
                        g.indirect_dma_start(out=rows_in, out_offset=bass.IndirectOffsetOnAxis(ap=idx[:, n, k:k + 1], axis=0),
                                             in_=hrow[:, n, k, :], in_offset=None).then_inc(sem("scattered"), 16)

            steps = {"A.xT": a_xb, "A.mask0": a_mask0, "A.mask1": a_mask1, "A.r0": lambda i: rstd("A", i, "l0"),
                     "A.x1": a_wsel, "A.r1": a_r1, "B.s0": lambda i: b_s(i, 0), "B.s1": lambda i: b_s(i, 1),
                     "B.m0": lambda i: b_m(i, 0), "B.m1": lambda i: b_m(i, 1),
                     "B.r2": lambda i: rstd("B", i, "l3"),
                     "B.r3": lambda i: rstd("B", i, "l4"), "C.tok": c_tok, "C.scat": c_scat,
                     "A.bias": lambda i: bias_mask(i, 0), "B.bias": lambda i: bias_mask(i, 1)}
            for s in ORDER:
                if s in steps and s[0] == "A":
                    if s == "A.r0":
                        g.wait_ge(sem("mhalf_ready"), 1)
                    if s == "A.r1":
                        g.wait_ge(sem("rows_loaded"), 48)
                    if s == "A.bias":
                        g.wait_ge(sem("mneg_ready"), 1)
                    steps[s](0)
            rounds(steps, 1, "AB")
            rounds(steps, 2)
            with g.Fori(3, NG) as i:
                rounds(steps, i)
            rounds(steps, NG, "BC")

            def low2():
                for e in range(NE - 2, NE):
                    part_e = slice(e * FC, (e + 1) * FC)
                    g.wait_ge(sem("w2_high"), e + 1)
                    g.tensor_tensor(w2low[:, part_e, :], w2all[:, part_e, :], w2high[:, part_e, :].bitcast(F32), ALU.subtract)\
                        .then_inc(sem("w2_parted_by_pool"), 1)

            rounds(steps, NG + 1, "C", {"C.tok": low2})
            g.wait_ge(sem("plan_ready"), 1)

            def bias_of(t_, k, first=False):
                e = g.value_load(meta[0:1, 0, part(t_, 1)], min_val=0, max_val=NE - 1)
                if not first:
                    g.wait_ge(sem("hid_done1"), t_ - 1)
                g.tensor_copy(b1c[:, k, :], eb1[:, bass.ds(e * FC, FC)]).then_inc(sem("b1_ready"), 1)

            def add(t_, k, first=False):
                g.wait_ge(sem("y_copied"), t_ + 1)
                if not first:
                    g.wait_ge(sem(f"added{1 - k}"), 8 * t_ + 8 * k)
                g.tensor_copy(idxc[:, k:k + 1], info[:, part(t_, 1), 0:1].rearrange("p a b -> p (a b)"))\
                    .then_inc(sem("idxc_ready"), 1)
                wait_apart(g, sem("idxc_ready"), t_ + 1)
                g.indirect_dma_start(out=sums, out_offset=bass.IndirectOffsetOnAxis(ap=idxc[:, k:k + 1], axis=0),
                                     in_=ys[:, k, :], in_offset=None, compute_op=ALU.add)\
                                         .then_inc(sem(f"added{k}"), 16)

            bias_of(0, 0, True)
            bias_of(1, 1, True)
            g.wait_ge(sem("x_stored"), 16 * NG)
            bias_of(2, 0)
            add(0, 0, True)
            bias_of(3, 1)
            add(1, 1)
            with g.Fori(1, (MT - 3) // 2) as j:
                for k in range(2):
                    bias_of(2 * j + (k + 2), k)
                    add(2 * j + k, k)
            bias_of(MT - 1, 0)
            for t_ in range(MT - 3, MT):
                add(t_, t_ % 2)


def kernel(**inputs):
    import numpy as np
    import concourse.bacc as bacc
    from concourse.bass_utils import run_bass_kernel_spmd

    nc = bacc.Bacc("TRN2", target_bir_lowering=False, num_devices=1)
    arrays, tensors = {}, {}
    for name in inputs:
        a = np.ascontiguousarray(inputs[name])
        arrays[name] = a
        tensors[name] = nc.dram_tensor(name, a.shape, mybir.dt.from_np(a.dtype), kind="ExternalInput").ap()
    half = D // 2
    arrays["freqs"] = np.exp(np.arange(half, dtype=np.float32) * np.float32(-np.log(10000.0) / (half - 1)))
    tensors["freqs"] = nc.dram_tensor("freqs", (half,), F32, kind="ExternalInput").ap()
    tensors["out"] = nc.dram_tensor("out", (B, S, D), F32, kind="ExternalOutput").ap()
    build(nc, tensors)
    r = run_bass_kernel_spmd(nc, [arrays], core_ids=[0])
    return r.results[0]["out"]
```
